# Optimizing a Trainium2 kernel written in Bass

```python
import numpy as np
import jax
import jax.numpy as jnp

def _softmax(x, axis=-1):
    return jax.nn.softmax(x, axis=axis)

def _gelu(x):
    return jax.nn.gelu(x, approximate=True)

def _silu(x):
    return jax.nn.silu(x)

def _sigmoid(x):
    return jax.nn.sigmoid(x)

def _layernorm(x, axis=-1, eps=1e-05):
    m = jnp.mean(x, axis=axis, keepdims=True)
    v = jnp.var(x, axis=axis, keepdims=True)
    return (x - m) / jnp.sqrt(v + eps)

def _scatter_add(tgt, idx, src, axis=0):
    return tgt.at[idx].add(src)

def _segment_sum(src, seg, n):
    return jax.ops.segment_sum(src, seg, n)
kernel_name = 'mk_gnn_preln_d4_gnn_r8_e872c0'

def setup_inputs(seed: int=0):
    np.random.seed(seed)
    _w = jnp.asarray

    def _rec_inputs():
        import jax
        import jax.numpy as jnp
        _gk = jax.random.key(seed)
        x = -0.000202 + 1 * jax.random.normal(jax.random.fold_in(_gk, 1), (12500, 64), jnp.float32)
        src = jax.random.randint(jax.random.fold_in(_gk, 2), (400000,), 0, 12500, jnp.int32)
        dst = jax.random.randint(jax.random.fold_in(_gk, 3), (400000,), 0, 12500, jnp.int32)
        _o = jnp.argsort(dst, stable=True)
        src = src[_o]
        dst = dst[_o]
        edge_attr_32 = 0.000196303 + 1.00016 * jax.random.normal(jax.random.fold_in(_gk, 12), (400000, 32), jnp.float32)
        return (x, src, dst, edge_attr_32)
    x, src, dst, edge_attr_32 = _rec_inputs()

    def _L0_gnn_setup():
        import jax, jax.numpy as jnp
        import numpy as np
        N_NODES = 12500
        N_EDGES = 200000
        IN_CH = 64
        OUT_CH = 64
        key = jax.random.key(seed)
        ks = jax.random.split(key, 6)
        x = jax.random.normal(ks[0], (N_NODES, IN_CH), dtype=jnp.float32)
        edge_index = jax.random.randint(ks[1], (2, N_EDGES), 0, N_NODES, dtype=jnp.int64)
        W1 = jax.random.normal(ks[2], (2 * IN_CH, OUT_CH), dtype=jnp.float32) * (1.0 / np.sqrt(2 * IN_CH))
        b1 = jnp.zeros((OUT_CH,), dtype=jnp.float32)
        W2 = jax.random.normal(ks[3], (OUT_CH, OUT_CH), dtype=jnp.float32) * (1.0 / np.sqrt(OUT_CH))
        b2 = jnp.zeros((OUT_CH,), dtype=jnp.float32)
        return {'x': x, 'edge_index': edge_index, 'W1': W1, 'b1': b1, 'W2': W2, 'b2': b2}
    _L0_gnn_all = _L0_gnn_setup()
    _L0_gnn_in = {k: v for k, v in _L0_gnn_all.items() if k in ('W1', 'b1', 'W2', 'b2')}
    del _L0_gnn_all

    def _L1_gnn_setup():
        import jax, jax.numpy as jnp
        import numpy as np
        N_NODES = 12500
        N_EDGES = 200000
        IN_C, HID_C, OUT_C = (64, 128, 64)

        def _sage_conv(x, src, dst, W_l, b, W_r, num_nodes):
            msg = x[src]
            agg = jax.ops.segment_sum(msg, dst, num_segments=num_nodes)
            deg = jax.ops.segment_sum(jnp.ones((src.shape[0],), dtype=x.dtype), dst, num_segments=num_nodes)
            mean = agg / jnp.maximum(deg, 1.0)[:, None]
            return mean @ W_l + b + x @ W_r
        key = jax.random.key(seed)
        ks = jax.random.split(key, 6)
        x = jax.random.normal(ks[0], (N_NODES, IN_C), dtype=jnp.float32)
        edge_index = jax.random.randint(ks[1], (2, N_EDGES), 0, N_NODES, dtype=jnp.int64)
        W1_l = jax.random.normal(ks[2], (IN_C, HID_C), dtype=jnp.float32) / np.sqrt(IN_C)
        b1 = jnp.zeros((HID_C,), dtype=jnp.float32)
        W1_r = jax.random.normal(ks[3], (IN_C, HID_C), dtype=jnp.float32) / np.sqrt(IN_C)
        W2_l = jax.random.normal(ks[4], (HID_C, OUT_C), dtype=jnp.float32) / np.sqrt(HID_C)
        b2 = jnp.zeros((OUT_C,), dtype=jnp.float32)
        W2_r = jax.random.normal(ks[5], (HID_C, OUT_C), dtype=jnp.float32) / np.sqrt(HID_C)
        return {'x': x, 'edge_index': edge_index, 'W1_l': W1_l, 'b1': b1, 'W1_r': W1_r, 'W2_l': W2_l, 'b2': b2, 'W2_r': W2_r}
    _L1_gnn_all = _L1_gnn_setup()
    _L1_gnn_in = {k: v for k, v in _L1_gnn_all.items() if k in ('W1_l', 'b1', 'W1_r', 'W2_l', 'b2', 'W2_r')}
    del _L1_gnn_all

    def _L2_gnn_setup():
        import jax, jax.numpy as jnp
        import numpy as np
        N_NODES = 6250
        N_EDGES = 100000
        F_X = 64
        F_E = 32
        H = 128
        F_OUT = 64

        def scatter_mean(vals, idx, num_segments):
            s = jax.ops.segment_sum(vals, idx, num_segments=num_segments)
            cnt = jax.ops.segment_sum(jnp.ones((vals.shape[0],), dtype=vals.dtype), idx, num_segments=num_segments)
            return s / jnp.maximum(cnt, 1.0)[:, None]
        key = jax.random.key(seed)
        ks = jax.random.split(key, 12)
        x = jax.random.normal(ks[0], (N_NODES, F_X), dtype=jnp.float32)
        edge_index = jax.random.randint(ks[1], (2, N_EDGES), 0, N_NODES)
        edge_attr = jax.random.normal(ks[2], (N_EDGES, F_E), dtype=jnp.float32)

        def lin(k, fan_in, fan_out):
            kw, kb = jax.random.split(k)
            bound = 1.0 / np.sqrt(fan_in)
            W = jax.random.uniform(kw, (fan_in, fan_out), minval=-bound, maxval=bound, dtype=jnp.float32)
            b = jax.random.uniform(kb, (fan_out,), minval=-bound, maxval=bound, dtype=jnp.float32)
            return (W, b)
        W1, b1 = lin(ks[3], F_X + F_E, H)
        W2, b2 = lin(ks[4], H, F_OUT)
        W3, b3 = lin(ks[5], F_X + F_OUT, H)
        W4, b4 = lin(ks[6], H, F_OUT)
        return {'x': x, 'edge_index': edge_index, 'edge_attr': edge_attr, 'W1': W1, 'b1': b1, 'W2': W2, 'b2': b2, 'W3': W3, 'b3': b3, 'W4': W4, 'b4': b4}
    _L2_gnn_all = _L2_gnn_setup()
    _L2_gnn_in = {k: v for k, v in _L2_gnn_all.items() if k in ('W1', 'b1', 'W2', 'b2', 'W3', 'b3', 'W4', 'b4')}
    del _L2_gnn_all

    def _L3_gnn_setup():
        import jax, jax.numpy as jnp
        import numpy as np
        key = jax.random.key(seed)
        k1, k2, k3 = jax.random.split(key, 3)
        N, E, D = (12500, 156250, 64)
        feat = jax.random.normal(k1, (N, D), dtype=jnp.float32)
        src = jax.random.randint(k2, (E,), 0, N, dtype=jnp.int32)
        dst = jax.random.randint(k3, (E,), 0, N, dtype=jnp.int32)
        return {'feat': feat, 'src': src, 'dst': dst, 'n_nodes': N}
    _L3_gnn_all = _L3_gnn_setup()
    _L3_gnn_in = {k: v for k, v in _L3_gnn_all.items() if k in ()}
    del _L3_gnn_all
    return {'x': x, 'src': src, 'dst': dst, 'edge_attr_32': edge_attr_32, 'L0_gnn_W1': _L0_gnn_in['W1'], 'L0_gnn_b1': _L0_gnn_in['b1'], 'L0_gnn_W2': _L0_gnn_in['W2'], 'L0_gnn_b2': _L0_gnn_in['b2'], 'L1_gnn_W1_l': _L1_gnn_in['W1_l'], 'L1_gnn_b1': _L1_gnn_in['b1'], 'L1_gnn_W1_r': _L1_gnn_in['W1_r'], 'L1_gnn_W2_l': _L1_gnn_in['W2_l'], 'L1_gnn_b2': _L1_gnn_in['b2'], 'L1_gnn_W2_r': _L1_gnn_in['W2_r'], 'L2_gnn_W1': _L2_gnn_in['W1'], 'L2_gnn_b1': _L2_gnn_in['b1'], 'L2_gnn_W2': _L2_gnn_in['W2'], 'L2_gnn_b2': _L2_gnn_in['b2'], 'L2_gnn_W3': _L2_gnn_in['W3'], 'L2_gnn_b3': _L2_gnn_in['b3'], 'L2_gnn_W4': _L2_gnn_in['W4'], 'L2_gnn_b4': _L2_gnn_in['b4']}

def reference(x, src, dst, edge_attr_32, L0_gnn_W1, L0_gnn_b1, L0_gnn_W2, L0_gnn_b2, L1_gnn_W1_l, L1_gnn_b1, L1_gnn_W1_r, L1_gnn_W2_l, L1_gnn_b2, L1_gnn_W2_r, L2_gnn_W1, L2_gnn_b1, L2_gnn_W2, L2_gnn_b2, L2_gnn_W3, L2_gnn_b3, L2_gnn_W4, L2_gnn_b4):
    import jax
    import jax.numpy as jnp

    def _L0_gnn_ref(x, edge_index, W1, b1, W2, b2):
        import jax, jax.numpy as jnp
        import numpy as np
        N_NODES = 12500
        N_EDGES = 200000
        IN_CH = 64
        OUT_CH = 64
        src = edge_index[0]
        dst = edge_index[1]
        x_i = x[dst]
        x_j = x[src]
        edge_features = jnp.concatenate([x_i, x_j - x_i], axis=-1)
        h = jax.nn.relu(edge_features @ W1 + b1)
        edge_messages = h @ W2 + b2
        out = jax.ops.segment_max(edge_messages, dst, num_segments=x.shape[0])
        return jnp.where(jnp.isfinite(out), out, jnp.zeros_like(out))

    def _L1_gnn_ref(x, edge_index, W1_l, b1, W1_r, W2_l, b2, W2_r):
        import jax, jax.numpy as jnp
        import numpy as np
        N_NODES = 12500
        N_EDGES = 200000
        IN_C, HID_C, OUT_C = (64, 128, 64)

        def _sage_conv(x, src, dst, W_l, b, W_r, num_nodes):
            msg = x[src]
            agg = jax.ops.segment_sum(msg, dst, num_segments=num_nodes)
            deg = jax.ops.segment_sum(jnp.ones((src.shape[0],), dtype=x.dtype), dst, num_segments=num_nodes)
            mean = agg / jnp.maximum(deg, 1.0)[:, None]
            return mean @ W_l + b + x @ W_r
        src, dst = (edge_index[0], edge_index[1])
        n = x.shape[0]
        h = _sage_conv(x, src, dst, W1_l, b1, W1_r, n)
        h = jax.nn.relu(h)
        out = _sage_conv(h, src, dst, W2_l, b2, W2_r, n)
        return out

    def _L2_gnn_ref(x, edge_index, edge_attr, W1, b1, W2, b2, W3, b3, W4, b4):
        import jax, jax.numpy as jnp
        import numpy as np
        N_NODES = 6250
        N_EDGES = 100000
        F_X = 64
        F_E = 32
        H = 128
        F_OUT = 64

        def scatter_mean(vals, idx, num_segments):
            s = jax.ops.segment_sum(vals, idx, num_segments=num_segments)
            cnt = jax.ops.segment_sum(jnp.ones((vals.shape[0],), dtype=vals.dtype), idx, num_segments=num_segments)
            return s / jnp.maximum(cnt, 1.0)[:, None]
        row, col = (edge_index[0], edge_index[1])
        h = jnp.concatenate([x[row], edge_attr], axis=1)
        h = jax.nn.relu(h @ W1 + b1)
        h = h @ W2 + b2
        agg = scatter_mean(h, col, x.shape[0])
        g = jnp.concatenate([x, agg], axis=1)
        g = jax.nn.relu(g @ W3 + b3)
        return g @ W4 + b4

    def _L3_gnn_ref(feat, src, dst, n_nodes):
        import jax, jax.numpy as jnp
        import numpy as np
        messages = feat[src]
        out = jax.ops.segment_sum(messages, dst, num_segments=n_nodes)
        return out
    edge_index = jnp.stack([src, dst])
    h = jnp.maximum(_layernorm(x, axis=-1), 0.0)
    x = x + _L0_gnn_ref(h, edge_index, L0_gnn_W1, L0_gnn_b1, L0_gnn_W2, L0_gnn_b2)
    h = jnp.maximum(_layernorm(x, axis=-1), 0.0)
    x = x + _L1_gnn_ref(h, edge_index, L1_gnn_W1_l, L1_gnn_b1, L1_gnn_W1_r, L1_gnn_W2_l, L1_gnn_b2, L1_gnn_W2_r)
    h = jnp.maximum(_layernorm(x, axis=-1), 0.0)
    x = x + _L2_gnn_ref(h, edge_index, edge_attr_32, L2_gnn_W1, L2_gnn_b1, L2_gnn_W2, L2_gnn_b2, L2_gnn_W3, L2_gnn_b3, L2_gnn_W4, L2_gnn_b4)
    h = jnp.maximum(_layernorm(x, axis=-1), 0.0)
    x = x + _L3_gnn_ref(h, src, dst, 12500)
    return x

_drawn_inputs = setup_inputs


def setup_inputs(seed=0):
    import zlib

    import numpy as np

    out = dict(_drawn_inputs(seed))
    spreads = {'L0_gnn_b1': (0.0, 0.375),
     'L0_gnn_b2': (0.0, 0.1),
     'L1_gnn_b1': (0.0, 0.373),
     'L1_gnn_b2': (0.0, 0.1)}
    factors = {'edge_attr_32': 8.0,
     'L2_gnn_W1': 7.033,
     'L2_gnn_b1': 8.0,
     'L2_gnn_W2': 4.106,
     'L2_gnn_b2': 31.134,
     'L2_gnn_b3': 4.435,
     'L2_gnn_b4': 3.139}
    for name, (base, spread) in spreads.items():
        noise = np.random.default_rng([zlib.crc32(name.encode()), seed]).standard_normal(out[name].shape)
        drawn = base * np.exp(spread * noise) if base else spread * noise
        out[name] = jnp.asarray(drawn.astype(out[name].dtype))
    for name, factor in factors.items():
        out[name] = (out[name] * factor).astype(out[name].dtype)
    return out
```

```python
import numpy as np
import concourse.bass as bass
from concourse import mybir
from contextlib import ExitStack

F32 = mybir.dt.float32
BF16 = mybir.dt.bfloat16
I32 = mybir.dt.int32
I16 = mybir.dt.int16
ALU = mybir.AluOpType
ACT = mybir.ActivationFunctionType
AX = mybir.AxisListType.X

PART = 128
NODES, D = 12500, 64
EDGES, DE = 400000, 32
HID = 128
TILES = EDGES // PART
BLOCKS = -(-NODES // PART)
NODES_PAD = BLOCKS * PART
LAST_ROWS = NODES - (BLOCKS - 1) * PART
SLOT = 4
SLOTS = 4
UNROLL = SLOT * SLOTS
ITERS = -(-(TILES + BLOCKS - 1) // UNROLL)
STEPS = ITERS * UNROLL
SLOT_E = SLOT * PART
MAPPED = -(-STEPS // PART) * PART
MAP_CHUNKS = MAPPED // PART
STEP_COLS = MAPPED + UNROLL
NAT_P = 125
NAT_T = TILES // NAT_P
NAT_E = NAT_T * PART
CH = 7
CHUNKS = BLOCKS // CH
CH_N = CH * PART
BIG = 1.5e38
EPS = 1e-5
MAP_COLS = 416
MAP_MMS = MAPPED // MAP_COLS


def gnn_kernel(nc, A, out):
    ctx = ExitStack()
    with ctx:
        def sb(name, shape, dt=F32, stack=ctx):
            return stack.enter_context(nc.sbuf_tensor(name, shape, dt))

        def dram(name, shape, dt=F32):
            return nc.dram_tensor(name, shape, dt).ap()

        ctx.enter_context(nc.allow_non_contiguous_dma(reason="a few single words for each partition"))
        sems = {}

        def S(name):
            if name not in sems:
                sems[name] = ctx.enter_context(nc.semaphore(name))
            return sems[name]

        tile_table = dram("tile_table", (TILES, 4 * PART))
        tile_ends = dram("tile_ends", (2, TILES))
        step_rows = dram("step_rows", (2, MAPPED), I32)
        step_rel = dram("step_rel", (MAPPED, PART), I16)
        step_mask = dram("step_mask", (MAPPED, PART), BF16)
        q_table = dram("q_table", (NODES_PAD, D))
        h1_table = dram("h1_table", (NODES_PAD, D))
        z_table = dram("z_table", (NODES_PAD, D))
        r_table = dram("r_table", (NODES_PAD, HID))
        h3_table = dram("h3_table", (NODES_PAD, D))
        blocked = "(g p) f -> p g f"

        x_sb = sb("x_sb", [PART, BLOCKS, D])
        h_sb = sb("h_sb", [PART, BLOCKS, D])
        P_WORDS = (BLOCKS + 1) * 3 * D // 2
        big = sb("big", [PART, (BLOCKS + 1) * D + P_WORDS])
        src_st = sb("src_st", [PART, STEP_COLS], I32)
        rel_st = sb("rel_st", [PART, STEP_COLS])
        end_st = sb("end_st", [PART, STEP_COLS])
        block_row = sb("block_row", [1, STEP_COLS], I32)
        tile_row = end_st[0:1, :].bitcast(I32)
        ident = sb("ident", [PART, PART])
        iota_f = sb("iota_f", [PART, PART])
        iota_p = sb("iota_p", [PART, 1])
        small = sb("small", [PART, 4, BLOCKS])
        deg_inv = sb("deg_inv", [PART, BLOCKS])
        has_edge = sb("has_edge", [PART, BLOCKS])
        eps_t = sb("eps_t", [PART, 1])
        idx = sb("idx", [PART, SLOTS, SLOT], I32)
        rows = sb("rows", [PART, SLOTS, SLOT, HID])
        w_pq = sb("w_pq", [D + 1, 2 * D])
        w_msg = sb("w_msg", [D + 1, D])
        w1_cat = sb("w1_cat", [2 * D, HID])
        w2_cat = sb("w2_cat", [HID, 2 * D])
        b1_col = sb("b1_col", [HID, 1])
        b2_row = sb("b2_row", [PART, D])
        w_r = sb("w_r", [D + 1, HID])
        w_e = sb("w_e", [DE, HID])
        w_agg = sb("w_agg", [HID, D])
        b_agg = sb("b_agg", [D + 1, D])
        w3_h = sb("w3_h", [D, HID])
        w3_a = sb("w3_a", [D, HID])
        b3_col = sb("b3_col", [HID, 1])
        w4 = sb("w4", [HID, D])
        b4_row = sb("b4_row", [PART, D])

        def acc(width):
            return big[:, 0:(BLOCKS + 1) * width].rearrange("p (g f) -> p g f", f=width)

        p_split = big[:, (BLOCKS + 1) * D:].bitcast(BF16).rearrange("p (g k f) -> p g k f", k=3, f=D)
        squares = big[:, 0:BLOCKS * D].rearrange("p (g f) -> p g f", f=D)

        ones_col = rows[:, 0, 0, D:D + 1]
        ps = ctx.enter_context(nc.psum_tensor("ps", [PART, 8, 512], F32))

        def stage(make):
            with ExitStack() as st:
                return make(lambda name, shape, dt=F32: sb(name, shape, dt, st))

        def map_bufs(a):
            return dict(raw=h_sb[:, :, :].rearrange("p g f -> p (g f)").bitcast(I32)[0:NAT_P, 0:NAT_E], cat=a("cat", [NAT_P, NAT_E + 2]),
                        ends=a("ends", [NAT_P, 2, NAT_T]), cols=a("cols", [PART, 8]), tri=a("tri", [PART, 2, PART]),
                        st_idx=a("st_idx", [PART, 2, MAP_CHUNKS], I32), cur=a("cur", [PART, 2, 1], I32),
                        got=a("got", [PART, 2, 4, PART]), rel=a("rel", [PART, 2, PART]), end=a("end", [PART, 2, PART]),
                        rel16=a("rel16", [PART, 2, PART], I16), mask16=a("mask16", [PART, 2, PART], BF16),
                        blk=a("blk", [PART, MAP_CHUNKS]))

        def l0_bufs(a):
            return dict(hc=a("hc0", [PART, CH, D]), hT=a("hT0", [D + 1, CH_N]), qst=a("qst", [PART, CH, D]),
                        pres=a("pres", [PART, CH, D]))

        def l0_loop_bufs(a):
            return dict(rel=a("rel_row", [PART, SLOTS, SLOT_E], I16), mask=a("mask_row", [D, SLOTS, SLOT_E], BF16),
                        ohT=a("ohT", [PART, SLOTS, SLOT_E], BF16), pre=a("pre", [D + 1, 2, SLOT_E]),
                        scan=a("scan", [D, 2, SLOT_E]), scanT=a("scanT", [PART, 2, SLOT, D]),
                        oh=a("oh0", [PART, 2, SLOT, PART]))

        def sum_bufs(a):
            return dict(oh=a("oh_sum", [PART, SLOTS, SLOT, PART]))

        def l1_bufs(a):
            return dict(cat=a("cat1", [PART, CH, 2 * D]), catT=a("catT", [PART, CH_N]), h1T=a("h1T", [PART, CH_N]),
                        zst=a("zst", [PART, CH, D]))

        def l2_pre_bufs(a):
            return dict(hc=a("hc2", [PART, CH, D]), hT=a("hT2", [D + 1, CH_N]), rst=a("rst", [PART, CH, HID]))

        def l2_loop_bufs(a):
            return dict(oh=a("oh2", [PART, SLOTS, SLOT, PART]), ea=a("ea", [DE, SLOTS, SLOT, PART]),
                        act=a("act2", [PART, 2, SLOT, HID]))

        def l2_post_bufs(a):
            return dict(m=a("m2", [PART, CH, HID]), hi=a("hi", [PART, CH, D + 1]), mT=a("mT", [PART, CH_N]),
                        hT=a("hTi", [D + 1, CH_N]), aT=a("aT", [D, CH_N]), gT=a("gT", [PART, CH_N]))

        MP, L0, L0E, SUM, L1, L2R, L2E, L2P = (stage(m) for m in (
            map_bufs, l0_bufs, l0_loop_bufs, sum_bufs, l1_bufs, l2_pre_bufs, l2_loop_bufs, l2_post_bufs))

        block = ctx.enter_context(nc.Block())
        SUM_LAYERS = {"l1a": (h1_table, D + 1), "l1b": (z_table, D), "l3": (h3_table, D)}

        def finish(sp):
            sp.wait_ge(S("result"), 1)
            sp.dma_start(out[0:(BLOCKS - 1) * PART, :].rearrange(blocked, p=PART), x_sb[:, 0:BLOCKS - 1, :]
                         ).then_inc(S("out_stored"), 16)
            sp.dma_start(out[(BLOCKS - 1) * PART:, :], x_sb[0:LAST_ROWS, BLOCKS - 1, :]).then_inc(S("out_stored"), 16)
            sp.wait_ge(S("out_stored"), 32)

        @block.sync
        def _(sp):
            sp.dma_start(x_sb[:, 0:BLOCKS - 1, :],
                         A["x"][0:(BLOCKS - 1) * PART, :].rearrange(blocked, p=PART)).then_inc(S("x_loaded"), 16)
            sp.wait_ge(S("x_zeroed"), 1)
            sp.dma_start(x_sb[0:LAST_ROWS, BLOCKS - 1, :], A["x"][(BLOCKS - 1) * PART:, :]).then_inc(S("x_loaded"), 16)

            sp.wait_ge(S("cat_ends"), 1)
            col = lambda e0, n: A["dst"][e0:e0 + (n - 1) * NAT_E + 1:NAT_E].rearrange("(p o) -> p o", o=1)
            sp.dma_start(MP["st_idx"][1:NAT_P, 0, 0:1], col(NAT_E - 1, NAT_P - 1)).then_inc(S("edge_ends"), 16)
            sp.dma_start(MP["st_idx"][0:NAT_P - 1, 1, 0:1], col(NAT_E, NAT_P - 1)).then_inc(S("edge_ends"), 16)
            for n, name in enumerate(("dst", "src")):
                view = A[name].rearrange("(p e) -> p e", p=NAT_P)
                if n:
                    sp.wait_ge(S("raw_used"), 1)
                sp.dma_start(MP["raw"], view).then_inc(S("raw_loaded"), 16)
            for name, dst_ap in (("L0_gnn_W2", w_msg[0:D, :]), ("L1_gnn_W1_l", w1_cat[0:D, :]),
                                 ("L1_gnn_W1_r", w1_cat[D:2 * D, :]), ("L1_gnn_W2_l", w2_cat[:, 0:D]),
                                 ("L1_gnn_W2_r", w2_cat[:, D:2 * D]), ("L2_gnn_W2", w_agg[:, :]), ("L2_gnn_W4", w4[:, :])):
                sp.dma_start(dst_ap, A[name]).then_inc(S("weights"), 16)
            row = lambda name: A[name].rearrange("(o f) -> o f", o=1)
            column = lambda name: A[name].rearrange("(f o) -> f o", o=1)
            W1 = A["L0_gnn_W1"]
            sp.dma_start(w_pq[0:D, 0:D], W1[0:D, :]).then_inc(S("weights"), 16)
            sp.dma_start(w_pq[0:D, D:2 * D], W1[D:2 * D, :]).then_inc(S("weights"), 16)
            sp.dma_start(w_msg[D:D + 1, :], row("L0_gnn_b2")).then_inc(S("weights"), 16)
            sp.dma_start(b1_col[:, :], column("L1_gnn_b1")).then_inc(S("weights"), 16)
            sp.dma_start(b3_col[:, :], column("L2_gnn_b3")).then_inc(S("weights"), 16)
            sp.dma_start(w_r[0:D, :], A["L2_gnn_W1"][0:D, :]).then_inc(S("weights"), 16)
            sp.dma_start(w_r[D:D + 1, :], row("L2_gnn_b1")).then_inc(S("weights"), 16)
            sp.dma_start(w_e[:, :], A["L2_gnn_W1"][D:D + DE, :]).then_inc(S("weights"), 16)
            sp.dma_start(w3_h[:, :], A["L2_gnn_W3"][0:D, :]).then_inc(S("weights"), 16)
            sp.dma_start(w3_a[:, :], A["L2_gnn_W3"][D:2 * D, :]).then_inc(S("weights"), 16)
            sp.dma_start(b2_row[:, :], row("L1_gnn_b2").to_broadcast([PART, D])).then_inc(S("weights"), 16)
            sp.dma_start(b4_row[:, :], row("L2_gnn_b4").to_broadcast([PART, D])).then_inc(S("weights"), 16)
            sp.wait_ge(S("w_zeroed"), 1)
            sp.dma_start(w_pq[D:D + 1, 0:D], row("L0_gnn_b1")).then_inc(S("weights"), 16)
            sp.dma_start(b_agg[D:D + 1, :], row("L2_gnn_b2")).then_inc(S("weights"), 16)

            sp.wait_ge(S("tiles_built"), 1)
            sp.dma_start(tile_table.rearrange("(p t) f -> p (t f)", p=NAT_P),
                         big[0:NAT_P, 0:NAT_T * 4 * PART]).then_inc(S("table_stored"), 16)
            sp.dma_start(tile_ends.rearrange("k (p t) -> p k t", p=NAT_P), MP["ends"][:, :, :]).then_inc(S("ends_stored"), 16)
            sp.wait_ge(S("ends_stored"), 16)
            sp.wait_ge(S("table_stored"), 16)
            sp.dma_start(big[:, 0:2 * TILES].rearrange("p (k t) -> p k t", k=2),
                         tile_ends.unsqueeze(0).to_broadcast([PART, 2, TILES])).then_inc(S("ends_spread"), 16)
            sp.wait_ge(S("steps_mapped"), 1)
            sp.dma_start(step_rows[0:1, :], tile_row[:, 0:MAPPED]).then_inc(S("steps_stored"), 16)
            sp.dma_start(step_rows[1:2, :], block_row[:, 0:MAPPED]).then_inc(S("steps_stored"), 16)
            sp.wait_ge(S("steps_stored"), 32)
            sp.dma_start(MP["st_idx"][:, :, :],
                         step_rows.rearrange("k (c p) -> p k c", p=PART)).then_inc(S("steps_turned"), 16)
            with sp.Fori(0, MAP_CHUNKS // 2) as i:
                for b in range(2):
                    sp.wait_ge(S("map_rows"), 2 * i + b + 1)
                    sp.dma_start(step_rel[bass.ds(i * (2 * PART) + b * PART, PART), :], MP["rel16"][:, b, :]
                                 ).then_inc(S(f"map_stored{b}"), 16)
                    sp.dma_start(step_mask[bass.ds(i * (2 * PART) + b * PART, PART), :], MP["mask16"][:, b, :]
                                 ).then_inc(S(f"map_stored{b}"), 16)

            with sp.Fori(0, CHUNKS) as c:
                sp.wait_ge(S("q_staged"), c + 1)
                sp.dma_start(q_table[bass.ds(c * CH_N, CH_N), :].rearrange(blocked, p=PART), L0["qst"][:, :, :]
                             ).then_inc(S("q_stored"), 16)
            for b in range(2):
                sp.wait_ge(S(f"map_stored{b}"), 16 * MAP_CHUNKS)
            def edge_rows(i, s, first):
                n = i * SLOTS + s
                if not first:
                    sp.wait_ge(S("l0_ohT"), n - SLOTS + 1)
                v0 = i * UNROLL + s * SLOT
                sp.dma_start(L0E["rel"][:, s, :], step_rel[bass.ds(v0, SLOT), :].rearrange("v e -> (v e)").unsqueeze(0)
                             .to_broadcast([PART, SLOT_E])).then_inc(S(f"l0_rel{s}"), 16)
                if not first:
                    sp.wait_ge(S("l0_scan"), n - SLOTS + 1)
                sp.dma_start(L0E["mask"][:, s, :], step_mask[bass.ds(v0, SLOT), :].rearrange("v e -> (v e)").unsqueeze(0)
                             .to_broadcast([D, SLOT_E])).then_inc(S(f"l0_mask{s}"), 16)
            sp.wait_ge(S("q_stored"), 16 * CHUNKS)
            sp.wait_ge(S("l0_piece"), 4 * CHUNKS)
            for s in range(SLOTS):
                edge_rows(0, s, True)
            with sp.Fori(1, ITERS) as i:
                for s in range(SLOTS):
                    edge_rows(i, s, False)
            edge_rows(ITERS, 0, False)

            sp.wait_ge(S("l1a_h"), 1)
            sp.dma_start(h1_table.rearrange(blocked, p=PART), h_sb[:, :, :]).then_inc(S("l1a_table"), 16)
            with sp.Fori(0, CHUNKS) as c:
                sp.wait_ge(S("z_staged"), c + 1)
                sp.dma_start(z_table[bass.ds(c * CH_N, CH_N), :].rearrange(blocked, p=PART), L1["zst"][:, :, :]
                             ).then_inc(S("z_stored"), 16)
            with sp.Fori(0, CHUNKS) as c:
                sp.wait_ge(S("r_staged"), c + 1)
                sp.dma_start(r_table[bass.ds(c * CH_N, CH_N), :].rearrange(blocked, p=PART), L2R["rst"][:, :, :]
                             ).then_inc(S("r_stored"), 16)
            sp.dma_start(tile_row[:, 0:MAPPED], step_rows[0:1, :]).then_inc(S("tiles_back"), 16)
            sp.wait_ge(S("tiles_back"), 16)
            def attributes(i, s, first):
                _, tiles = nc.values_load_multi_w_load_instructions(
                    tile_row[:, bass.ds(i * UNROLL + s * SLOT, SLOT)], engines=[sp.engine], min_val=0, max_val=TILES - 1)
                if not first:
                    sp.wait_ge(S("l2_pre"), (i - 1) * SLOTS + s + 1)
                for k in range(SLOT):
                    sp.dma_start(L2E["ea"][:, s, k, :], A["edge_attr_T"][bass.ds(tiles[k], 1), :, :]
                                 .rearrange("o f e -> (o f) e")).then_inc(S(f"l2_ea{s}"), 16)
            sp.wait_ge(S("r_stored"), 16 * CHUNKS)
            for s in range(SLOTS):
                attributes(0, s, True)
            with sp.Fori(1, ITERS) as i:
                for s in range(SLOTS):
                    attributes(i, s, False)
            sp.wait_ge(S("l3_h"), 1)
            sp.dma_start(h3_table.rearrange(blocked, p=PART), h_sb[:, :, :]).then_inc(S("l3_table"), 16)
            finish(sp)

        @block.gpsimd
        def _(pool):
            nc.gpsimd.memset(x_sb[:, BLOCKS - 1, :], 0.0).then_inc(S("x_zeroed"), 1)
            nc.gpsimd.iota(iota_f[:, :], [[1, PART]], base=0, channel_multiplier=0,
                           allow_small_or_imprecise_dtypes=True).then_inc(S("iotas"), 1)
            nc.gpsimd.iota(iota_p[:, :], [[0, 1]], base=0, channel_multiplier=1,
                           allow_small_or_imprecise_dtypes=True).then_inc(S("iotas"), 1)
            pool.wait_ge(S("table_stored"), 16)
            with pool.Fori(0, MAP_CHUNKS // 2) as i:
                for b in range(2):
                    pool.wait_ge(S("map_idx"), 2 * i + b + 1)
                    pool.sem_inc(S("map_begun"), 1)
                    nc.gpsimd.indirect_dma_start(
                        out=MP["got"][:, b, :, :].rearrange("p k e -> p (k e)"), out_offset=None, in_=tile_table,
                        in_offset=bass.IndirectOffsetOnAxis(MP["cur"][:, b, :], 0)).then_inc(S(f"map_got{b}"), 16)

            def gathers(layer, table, width):
                with pool.Fori(0, ITERS) as i:
                    for s in range(SLOTS):
                        pool.wait_ge(S(f"{layer}_idx"), i * SLOTS + s + 1)
                        pool.sem_inc(S(f"{layer}_begun"), 1)
                        for k in range(SLOT):
                            nc.gpsimd.indirect_dma_start(
                                out=rows[:, s, k, 0:width], out_offset=None, in_=table,
                                in_offset=bass.IndirectOffsetOnAxis(idx[:, s, k:k + 1], 0)).then_inc(S(f"{layer}_rows{s}"), 16)

            pool.wait_ge(S("q_stored"), 16 * CHUNKS)
            gathers("l0", q_table, D)
            pool.wait_ge(S("l1a_table"), 16)
            gathers("l1a", h1_table, D)
            pool.wait_ge(S("z_stored"), 16 * CHUNKS)
            gathers("l1b", z_table, D)
            pool.wait_ge(S("r_stored"), 16 * CHUNKS)
            gathers("l2", r_table, HID)
            pool.wait_ge(S("l3_table"), 16)
            gathers("l3", h3_table, D)

        @block.scalar
        def _(act):
            def indices(layer, i, s):
                nc.scalar.copy(idx[:, s, :], src_st[:, bass.ds(i * UNROLL + s * SLOT, SLOT)]).then_inc(S(f"{layer}_idx"), 1)

            def standard_deviation(layer):
                act.wait_ge(S(f"{layer}_var"), 1)
                nc.scalar.activation(small[:, 2, :], small[:, 1, :], ACT.Sqrt, bias=eps_t[:, :],
                                     scale=1.0 / D).then_inc(S(f"{layer}_std"), 1)

            act.wait_ge(S("w_zeroed"), 1)
            with act.Fori(0, MAP_CHUNKS // 2) as i:
                for b in range(2):
                    c = i * 2 + b
                    act.wait_ge(S("map_turned"), c + 1)
                    cols = bass.ds(i * (2 * PART) + b * PART, PART)
                    nc.scalar.copy(src_st[:, cols], ps[:, b, 0:PART])
                    nc.scalar.copy(rel_st[:, cols], ps[:, b, PART:2 * PART])
                    nc.scalar.copy(end_st[:, cols], ps[:, b, 2 * PART:3 * PART]).then_inc(S("map_done"), 1)

            standard_deviation("l0")
            with act.Fori(0, CHUNKS) as c:
                act.wait_ge(S("l0_hT"), c + 1)
                nc.scalar.copy(L0["hT"][0:D, :], ps[0:D, 0:2, :].rearrange("p b f -> p (b f)")[:, 0:CH_N]).then_inc(S("l0_hT_out"), 1)
                act.wait_ge(S("l0_pq"), c + 1)
                nc.scalar.copy(L0["qst"][:, :, :], ps[:, 2:4, :].rearrange("p b (g f) -> p (b g) f", f=2 * D)[:, 0:CH, D:2 * D]
                               ).then_inc(S("q_staged"), 1)
                act.wait_ge(S("q_stored"), c * 16 + 16)

            def relu0(n, s, i):
                act.wait_ge(S("l0_pre"), n + 1)
                if not isinstance(n, int) or n >= 2:
                    act.wait_ge(S("l0_msg"), n - 1)
                nc.scalar.activation(L0E["pre"][0:D, s % 2, :], ps[0:D, s % 2, :], ACT.Relu).then_inc(S("l0_relu"), 1)
                indices("l0", i + 1, s)

            def turned0(m, s):
                act.wait_ge(S("l0_turn"), m + 1)
                if not isinstance(m, int) or m >= 2:
                    act.wait_ge(S("l0_ends"), m - 1)
                nc.scalar.copy(L0E["scanT"][:, s % 2, :, :],
                               ps[:, 4 + s % 2, 0:SLOT * D].rearrange("p (k f) -> p k f", f=D)
                               ).then_inc(S("l0_turned"), 1)

            for s in range(SLOTS):
                indices("l0", 0, s)
            for s in range(SLOTS):
                relu0(s, s, 0)
                if s >= 2:
                    turned0(s - 2, s)
            with act.Fori(1, ITERS) as i:
                for s in range(SLOTS):
                    relu0(i * SLOTS + s, s, i)
                    turned0(i * SLOTS + (s - 2), s)
            for m in range(ITERS * SLOTS - 2, ITERS * SLOTS):
                turned0(m, m % SLOTS)

            def sums(layer):
                for s in range(SLOTS):
                    indices(layer, 0, s)
                with act.Fori(0, ITERS) as i:
                    for s in range(SLOTS):
                        act.wait_ge(S(f"{layer}_sum"), i * SLOTS + s + 1)
                        indices(layer, i + 1, s)

            standard_deviation("l1a")
            sums("l1a")
            with act.Fori(0, CHUNKS) as c:
                act.wait_ge(S("l1_cat"), c + 1)
                nc.scalar.copy(L1["catT"][:, :], ps[:, 0:2, :].rearrange("p b f -> p (b f)")[:, 0:CH_N]).then_inc(S("l1_catT"), 1)
                act.wait_ge(S("l1_hid"), c + 1)
                for b in range(2):
                    ins = nc.scalar.activation(L1["h1T"][:, b * CH_N // 2:(b + 1) * CH_N // 2], ps[:, 2 + b, 0:CH_N // 2],
                                               ACT.Relu, bias=b1_col[:, :])
                ins.then_inc(S("l1_h1T"), 1)
                act.wait_ge(S("l1_zy"), c + 1)
                nc.scalar.copy(L1["zst"][:, :, :], ps[:, 4:6, :].rearrange("p b (g f) -> p (b g) f", f=2 * D)[:, 0:CH, 0:D]
                               ).then_inc(S("z_staged"), 1)
                act.wait_ge(S("z_stored"), c * 16 + 16)
            sums("l1b")

            standard_deviation("l2")
            with act.Fori(0, CHUNKS) as c:
                act.wait_ge(S("l2_hT"), c + 1)
                nc.scalar.copy(L2R["hT"][0:D, :], ps[0:D, 0:2, :].rearrange("p b f -> p (b f)")[:, 0:CH_N]).then_inc(S("l2_hT_out"), 1)
                act.wait_ge(S("l2_r"), c + 1)
                nc.scalar.copy(L2R["rst"][:, :, :], ps[:, 2:4, :].rearrange("p b (g f) -> p (b g) f", f=HID)[:, 0:CH, :]
                               ).then_inc(S("r_staged"), 1)
                act.wait_ge(S("r_stored"), c * 16 + 16)

            def relu2(n, s, i):
                act.wait_ge(S("l2_pre"), n + 1)
                if not isinstance(n, int) or n >= 2:
                    act.wait_ge(S("l2_sum"), n - 1)
                nc.scalar.activation(L2E["act"][:, s % 2, :, :].rearrange("p k f -> p (k f)"), ps[:, s % 2, :], ACT.Relu
                                     ).then_inc(S("l2_relu"), 1)
                indices("l2", i + 1, s)

            for s in range(SLOTS):
                indices("l2", 0, s)
            for s in range(SLOTS):
                relu2(s, s, 0)
            with act.Fori(1, ITERS) as i:
                for s in range(SLOTS):
                    relu2(i * SLOTS + s, s, i)
            with act.Fori(0, CHUNKS) as c:
                act.wait_ge(S("l2_mT"), c + 1)
                nc.scalar.copy(L2P["mT"][:, :], ps[:, 0:2, :].rearrange("p b f -> p (b f)")[:, 0:CH_N])
                nc.scalar.copy(L2P["hT"][:, :], ps[0:D + 1, 2:4, :].rearrange("p b f -> p (b f)")[:, 0:CH_N]).then_inc(S("l2_mT_out"), 1)
                act.wait_ge(S("l2_agg"), c + 1)
                nc.scalar.copy(L2P["aT"][:, :].rearrange("p (b f) -> p b f", b=2), ps[0:D, 4:6, 0:CH_N // 2]).then_inc(S("l2_aT"), 1)
                act.wait_ge(S("l2_g"), c + 1)
                nc.scalar.activation(L2P["gT"][:, :].rearrange("p (b f) -> p b f", b=2), ps[:, 6:8, 0:CH_N // 2], ACT.Relu,
                                     bias=b3_col[:, :]).then_inc(S("l2_gT"), 1)
            standard_deviation("l3")
            sums("l3")

        @block.vector
        def _(dve):
            chain = [0]

            def link(ins):
                chain[0] += 1
                ins.then_inc(S("dve_chain"), 1)
                dve.wait_ge(S("dve_chain"), chain[0])

            def broadcast(ap, shape):
                return ap.unsqueeze(len(shape) - 1).to_broadcast(shape)

            vec = nc.vector
            vec.memset(src_st[:, MAPPED:], 0)
            vec.memset(rel_st[:, MAPPED:], -1.0)
            vec.memset(end_st[:, MAPPED:], -1.0)
            vec.memset(eps_t[:, :], EPS)
            vec.memset(w_pq[D:D + 1, D:2 * D], 0.0)
            vec.memset(rows[:, :, :, D:D + 1], 1.0)
            vec.memset(b_agg[:, :], 0.0)
            vec.memset(block_row[:, MAPPED:], 0).then_inc(S("w_zeroed"), 1)
            dve.wait_ge(S("iotas"), 2)
            vec.tensor_scalar(ident[:, :], iota_f[:, :], iota_p[:, :], None, ALU.is_equal)
            vec.tensor_scalar(MP["tri"][:, 0, :], iota_f[:, :], iota_p[:, :], None, ALU.is_gt)
            link(vec.tensor_scalar(MP["tri"][:, 1, :], iota_f[:, :], 1.0, iota_p[:, :], ALU.subtract, ALU.is_equal))
            vec.tensor_tensor(MP["tri"][:, 1, :], ident[:, :], MP["tri"][:, 1, :], ALU.subtract).then_inc(S("consts"), 1)
            vec.tensor_scalar(MP["cols"][:, 0:1], iota_p[:, :], float(PART), None, ALU.mult)
            vec.tensor_scalar(MP["cols"][:, 1:2], iota_p[:, :], 1.0, float(PART), ALU.add, ALU.mult)
            vec.memset(MP["st_idx"][:, :, 0:1], -1).then_inc(S("cat_ends"), 1)
            table = big[0:NAT_P, 0:NAT_T * 4 * PART].rearrange("p (t k e) -> p t k e", k=4, e=PART)
            tiled = lambda ap: ap.rearrange("p (t e) -> p t e", e=PART)
            cat = MP["cat"]
            dve.wait_ge(S("edge_ends"), 32)
            vec.tensor_copy(cat[:, 0:1], MP["st_idx"][0:NAT_P, 0, 0:1])
            vec.tensor_copy(cat[:, NAT_E + 1:], MP["st_idx"][0:NAT_P, 1, 0:1])
            dve.wait_ge(S("raw_loaded"), 16)
            link(vec.tensor_copy(cat[:, 1:NAT_E + 1], MP["raw"]))
            dve.sem_inc(S("raw_used"), 1)
            here = cat[:, 1:NAT_E + 1]
            vec.tensor_copy(table[:, :, 1, :], tiled(here))
            vec.tensor_copy(MP["ends"][:, 0, :], tiled(here)[:, :, 0])
            vec.tensor_copy(MP["ends"][:, 1, :], tiled(here)[:, :, PART - 1])
            link(vec.tensor_tensor(table[:, :, 2, :], tiled(cat[:, 0:NAT_E]), tiled(here), ALU.not_equal))
            vec.tensor_tensor(table[:, :, 3, :], tiled(here), tiled(cat[:, 2:]), ALU.not_equal)
            vec.tensor_scalar(table[:, :, 2, :], table[:, :, 2, :], -2.0 * BIG, BIG, ALU.mult, ALU.add)
            dve.wait_ge(S("raw_loaded"), 32)
            vec.tensor_copy(table[:, :, 0, :], tiled(MP["raw"])).then_inc(S("tiles_built"), 1)
            dve.wait_ge(S("ends_spread"), 16)
            junk = h_sb[:, :, :].rearrange("p g f -> p (g f)")
            link(vec.tensor_scalar(junk[:, 0:TILES], big[:, 0:TILES], MP["cols"][:, 1:2], 0.0, ALU.is_lt, ALU.add,
                                   accum_out=MP["cols"][:, 2:3]))
            link(vec.tensor_scalar(junk[:, TILES:2 * TILES], big[:, TILES:2 * TILES], MP["cols"][:, 0:1], 0.0, ALU.is_lt, ALU.add,
                                   accum_out=MP["cols"][:, 3:4]))
            link(vec.tensor_tensor(MP["cols"][:, 4:5], MP["cols"][:, 2:3], MP["cols"][:, 3:4], ALU.subtract))
            vec.tensor_scalar(MP["cols"][:, 4:5], MP["cols"][:, 4:5], 0.0, None, ALU.max).then_inc(S("block_steps"), 1)
            dve.wait_ge(S("block_begin"), 1)
            link(vec.tensor_copy(MP["cols"][:, 5:6], ps[:, 0, 0:1]))
            vec.tensor_tensor(MP["cols"][:, 6:7], MP["cols"][:, 3:4], MP["cols"][:, 5:6], ALU.subtract).then_inc(S("block_shift"), 1)
            dve.wait_ge(S("block_delta"), 1)
            link(vec.tensor_copy(MP["cols"][:, 7:8], ps[:, 0, 1:2]))
            iota_v = big[:, 2 * TILES:2 * TILES + MAPPED]
            begun = big[:, 2 * TILES + MAPPED:2 * TILES + 2 * MAPPED]
            link(vec.tensor_scalar(iota_v[:, 0:PART], iota_f[:, :], 0.0, None, ALU.add))
            for c in range(1, MAP_CHUNKS):
                ins = vec.tensor_scalar(iota_v[:, c * PART:(c + 1) * PART], iota_f[:, :], float(c * PART), None, ALU.add)
            link(ins)
            vec.tensor_scalar(begun, iota_v, MP["cols"][:, 5:6], None, ALU.is_ge).then_inc(S("block_begun"), 1)
            for m in range(MAP_MMS):
                cols = slice(m * MAP_COLS, (m + 1) * MAP_COLS)
                dve.wait_ge(S("steps_summed"), m + 1)
                link(vec.tensor_tensor(junk[0:1, 0:MAP_COLS], ps[0:1, 2 * (m % 2), 0:MAP_COLS], iota_v[0:1, cols], ALU.add))
                vec.tensor_scalar(tile_row[:, cols], junk[0:1, 0:MAP_COLS], float(TILES - 1), None, ALU.min)
                link(vec.tensor_scalar(block_row[:, cols], ps[0:1, 2 * (m % 2) + 1, 0:MAP_COLS], 1.0, float(BLOCKS),
                                       ALU.subtract, ALU.min))
                dve.sem_inc(S("steps_read"), 1)
            dve.sem_inc(S("steps_mapped"), 1)
            dve.wait_ge(S("steps_turned"), 16)
            link(vec.tensor_scalar(MP["blk"][:, :], MP["st_idx"][:, 1, :], float(PART), None, ALU.mult))
            for b in range(2):
                vec.tensor_copy(MP["cur"][:, b, :], MP["st_idx"][:, 0, b:b + 1]).then_inc(S("map_idx"), 1)

            def map_chunk(i, b, first, last):
                got, rel, end = MP["got"][:, b, :, :], MP["rel"][:, b, :], MP["end"][:, b, :]
                dve.wait_ge(S(f"map_got{b}"), i * 16 + 16)
                if not first:
                    dve.wait_ge(S(f"map_stored{b}"), i * 32)
                vec.tensor_scalar(rel, got[:, 1, :], MP["blk"][:, bass.ds(i * 2 + b, 1)], None, ALU.subtract).then_inc(S("map_rel"), 1)
                dve.wait_ge(S("map_rel"), i * 2 + b + 1)
                vec.scalar_tensor_tensor(end, rel, 1.0, got[:, 3, :], ALU.add, ALU.mult).then_inc(S("map_end"), 1)
                vec.tensor_copy(MP["mask16"][:, b, :], got[:, 2, :])
                vec.tensor_copy(MP["rel16"][:, b, :], rel)
                dve.wait_ge(S("map_end"), i * 2 + b + 1)
                vec.tensor_scalar(end, end, 1.0, None, ALU.subtract).then_inc(S("map_rows"), 1)
                dve.wait_ge(S("map_turned"), i * 2 + b + 1)
                if not last:
                    vec.tensor_copy(MP["cur"][:, b, :], MP["st_idx"][:, 0, bass.ds(i * 2 + b + 2, 1)]).then_inc(S("map_idx"), 1)
            for b in range(2):
                map_chunk(0, b, True, False)
            with dve.Fori(1, MAP_CHUNKS // 2 - 1) as i:
                for b in range(2):
                    map_chunk(i, b, False, False)
            for b in range(2):
                map_chunk(MAP_CHUNKS // 2 - 1, b, False, True)

            def centred(layer):
                link(vec.tensor_reduce(small[:, 0, :], x_sb[:, :, :], AX, ALU.add))
                link(vec.tensor_scalar(small[:, 0, :], small[:, 0, :], 1.0 / D, None, ALU.mult))
                link(vec.tensor_tensor(h_sb[:, :, :], x_sb[:, :, :], broadcast(small[:, 0, :], [PART, BLOCKS, D]), ALU.subtract))
                link(vec.tensor_tensor(squares, h_sb[:, :, :], h_sb[:, :, :], ALU.mult))
                vec.tensor_reduce(small[:, 1, :], squares, AX, ALU.add).then_inc(S(f"{layer}_var"), 1)
                dve.wait_ge(S(f"{layer}_std"), 1)
                link(vec.reciprocal(small[:, 3, :], small[:, 2, :]))

            def normed(out_ap, g0, n):
                return vec.scalar_tensor_tensor(out_ap, h_sb[:, bass.ds(g0, n), :], 0.0,
                                                broadcast(small[:, 3, bass.ds(g0, n)], [PART, n, D]), ALU.max, ALU.mult)

            def clear(width):
                link(vec.memset(big[:, 0:(BLOCKS + 1) * width], 0.0))

            def blocks_of(i, s):
                _, got = nc.values_load_multi_w_load_instructions(
                    block_row[:, bass.ds(i * UNROLL + s * SLOT, SLOT)], engines=[dve.engine], min_val=0, max_val=BLOCKS)
                return got

            def one_hot(out_ap, source, i, s):
                v0 = i * UNROLL + s * SLOT
                return vec.tensor_tensor(out_ap, iota_f[:, :].unsqueeze(1).to_broadcast([PART, SLOT, PART]),
                                         source[:, bass.ds(v0, SLOT)].unsqueeze(2).to_broadcast([PART, SLOT, PART]), ALU.is_equal)

            def add_up(layer, width, i, s, bank, m):
                got = blocks_of(i, s)
                for k in range(SLOT):
                    target = acc(width)[:, bass.ds(got[k], 1), :].rearrange("p o f -> p (o f)")
                    vec.tensor_tensor(target, target, bank[:, k * width:(k + 1) * width], ALU.add).then_inc(S(f"{layer}_added"), 1)
                    dve.wait_ge(S(f"{layer}_added"), m * SLOT + k + 1)

            dve.wait_ge(S("x_loaded"), 32)
            dve.wait_ge(S("weights"), 16 * 21)
            link(vec.tensor_tensor(w_pq[0:D, 0:D], w_pq[0:D, 0:D], w_pq[0:D, D:2 * D], ALU.subtract))
            for b in range(2):
                dve.wait_ge(S(f"map_stored{b}"), 16 * MAP_CHUNKS)
            vec.memset(L0["hT"][D:D + 1, :], 1.0)
            centred("l0")
            vec.memset(p_split[:, BLOCKS, :, :], 0.0)
            with dve.Fori(0, CHUNKS) as c:
                normed(L0["hc"][:, :, :], c * CH, CH).then_inc(S("l0_h"), 1)
                dve.wait_ge(S("q_staged"), c + 1)
                p = ps[:, 2:4, :].rearrange("p b (g f) -> p (b g) f", f=2 * D)[:, 0:CH, 0:D]
                pieces = [p_split[:, bass.ds(c * CH, CH), k, :] for k in range(3)]
                steps = [lambda: vec.tensor_copy(pieces[0], p),
                         lambda: vec.tensor_tensor(L0["pres"][:, :, :], p, pieces[0], ALU.subtract),
                         lambda: vec.tensor_copy(pieces[1], L0["pres"][:, :, :]),
                         lambda: vec.tensor_tensor(pieces[2], L0["pres"][:, :, :], pieces[1], ALU.subtract)]
                for k, step in enumerate(steps):
                    step().then_inc(S("l0_piece"), 1)
                    dve.wait_ge(S("l0_piece"), c * len(steps) + k + 1)
            clear(D)
            dve.wait_ge(S("q_stored"), 16 * CHUNKS)
            vec.memset(L0E["pre"][D:D + 1, :, :], 1.0)
            link(vec.memset(L0E["scan"][:, :, :], -BIG))

            def ohT0(n, s, i):
                dve.wait_ge(S(f"l0_rel{s}"), i * 16 + 16)
                if not isinstance(n, int) or n >= SLOTS:
                    dve.wait_ge(S("l0_pre"), n - SLOTS + 1)
                vec.tensor_scalar(L0E["ohT"][:, s, :], L0E["rel"][:, s, :], iota_p[:, :], None, ALU.is_equal).then_inc(S("l0_ohT"), 1)

            def scan0(m, s, i):
                dve.wait_ge(S("l0_msg"), m + 1)
                dve.wait_ge(S(f"l0_mask{s}"), i * 16 + 16)
                if not isinstance(m, int) or m >= 2:
                    dve.wait_ge(S("l0_turn"), m - 1)
                if not isinstance(m, int) or m >= 1:
                    dve.wait_ge(S("l0_scan"), m)
                vec.tensor_tensor_scan(L0E["scan"][:, s % 2, :], L0E["mask"][:, s, :], ps[0:D, 2 + s % 2, :],
                                       L0E["scan"][:, (s + 1) % 2, SLOT_E - 1:SLOT_E], ALU.min, ALU.max).then_inc(S("l0_scan"), 1)

            def ends0(m, s, i):
                if not isinstance(m, int) or m >= 2:
                    dve.wait_ge(S("l0_ends"), m - 1)
                one_hot(L0E["oh"][:, s % 2, :, :], end_st, i, s).then_inc(S("l0_oh"), 1)

            def add0(m, s, i):
                dve.wait_ge(S("l0_ends"), m + 1)
                add_up("l0", D, i, s, ps[:, 6 + s % 2, :], m)

            def slot0(i, s, only=None):
                for lag, work in ((-1, ohT0), (1, scan0), (2, ends0), (3, add0)):
                    sl, it = (s - lag) % SLOTS, i + (s - lag) // SLOTS
                    m = i * SLOTS + (s - lag)
                    if isinstance(m, int) and not 0 <= m < ITERS * SLOTS:
                        continue
                    work(m, sl, it)
            ohT0(0, 0, 0)
            for s in range(SLOTS):
                slot0(0, s)
            with dve.Fori(1, ITERS) as i:
                for s in range(SLOTS):
                    slot0(i, s)
            for s in range(3):
                slot0(ITERS, s)
            dve.wait_ge(S("l0_mask0"), 16 * (ITERS + 1))
            link(vec.tensor_tensor(x_sb[:, :, :], x_sb[:, :, :], acc(D)[:, 0:BLOCKS, :], ALU.add))

            def sums(layer, width):
                clear(width)
                for s in range(SLOTS):
                    one_hot(SUM["oh"][:, s, :, :], rel_st, 0, s).then_inc(S(f"{layer}_oh"), 1)
                with dve.Fori(0, ITERS) as i:
                    for s in range(SLOTS):
                        dve.wait_ge(S(f"{layer}_sum"), i * SLOTS + s + 1)
                        add_up(layer, width, i, s, ps[:, s, :], i * SLOTS + s)
                        one_hot(SUM["oh"][:, s, :, :], rel_st, i + 1, s).then_inc(S(f"{layer}_oh"), 1)

            centred("l1a")
            link(normed(h_sb[:, :, :], 0, BLOCKS))
            dve.sem_inc(S("l1a_h"), 1)
            sums("l1a", D + 1)
            sums1 = acc(D + 1)
            degrees = sums1[:, 0:BLOCKS, D:D + 1].rearrange("p g o -> p (g o)")
            link(vec.tensor_scalar(deg_inv[:, :], degrees, 1.0, None, ALU.max))
            vec.tensor_scalar(has_edge[:, :], degrees, 1.0, None, ALU.min)
            link(vec.reciprocal(deg_inv[:, :], deg_inv[:, :]))
            with dve.Fori(0, CHUNKS) as c:
                vec.tensor_tensor(L1["cat"][:, :, 0:D], sums1[:, bass.ds(c * CH, CH), 0:D],
                                  broadcast(deg_inv[:, bass.ds(c * CH, CH)], [PART, CH, D]), ALU.mult)
                vec.tensor_copy(L1["cat"][:, :, D:2 * D], h_sb[:, bass.ds(c * CH, CH), :]).then_inc(S("l1_nodes"), 1)
                dve.wait_ge(S("z_staged"), c + 1)
                vec.tensor_tensor(h_sb[:, bass.ds(c * CH, CH), :],
                                  ps[:, 4:6, :].rearrange("p b (g f) -> p (b g) f", f=2 * D)[:, 0:CH, D:2 * D],
                                  b2_row[:, :].unsqueeze(1).to_broadcast([PART, CH, D]), ALU.add).then_inc(S("l1_y"), 1)
                dve.wait_ge(S("l1_y"), c + 1)
            dve.wait_ge(S("z_stored"), 16 * CHUNKS)
            sums("l1b", D)
            link(vec.tensor_tensor(h_sb[:, :, :], h_sb[:, :, :], x_sb[:, :, :], ALU.add))
            link(vec.tensor_tensor(x_sb[:, :, :], acc(D)[:, 0:BLOCKS, :], broadcast(deg_inv[:, :], [PART, BLOCKS, D]), ALU.mult))
            link(vec.tensor_tensor(x_sb[:, :, :], x_sb[:, :, :], h_sb[:, :, :], ALU.add))

            centred("l2")
            link(normed(h_sb[:, :, :], 0, BLOCKS))
            vec.memset(L2R["hT"][D:D + 1, :], 1.0)
            with dve.Fori(0, CHUNKS) as c:
                vec.tensor_copy(L2R["hc"][:, :, :], h_sb[:, bass.ds(c * CH, CH), :]).then_inc(S("l2_h"), 1)
                dve.wait_ge(S("l2_hT"), c + 1)
            clear(HID)
            dve.wait_ge(S("r_staged"), CHUNKS)
            dve.wait_ge(S("r_stored"), 16 * CHUNKS)
            for s in range(SLOTS):
                one_hot(L2E["oh"][:, s, :, :], rel_st, 0, s).then_inc(S("l2_oh"), 1)
            with dve.Fori(0, ITERS) as i:
                for s in range(SLOTS):
                    dve.wait_ge(S("l2_sum"), i * SLOTS + s + 1)
                    add_up("l2", HID, i, s, ps[:, 2 + s % 2, :], i * SLOTS + s)
                    one_hot(L2E["oh"][:, s, :, :], rel_st, i + 1, s).then_inc(S("l2_oh"), 1)
            with dve.Fori(0, CHUNKS) as c:
                g = bass.ds(c * CH, CH)
                vec.tensor_tensor(L2P["m"][:, :, :], acc(HID)[:, g, :], broadcast(deg_inv[:, g], [PART, CH, HID]), ALU.mult)
                vec.tensor_copy(L2P["hi"][:, :, 0:D], h_sb[:, g, :])
                vec.tensor_copy(L2P["hi"][:, :, D:D + 1], has_edge[:, g].unsqueeze(2)).then_inc(S("l2_nodes"), 1)
                dve.wait_ge(S("l2_out"), c + 1)
                y = ps[:, 0, 0:CH * D].rearrange("p (g f) -> p g f", f=D)
                vec.tensor_tensor(x_sb[:, g, :], x_sb[:, g, :], y, ALU.add).then_inc(S("l2_x"), 1)
                dve.wait_ge(S("l2_x"), c + 1)
            link(vec.tensor_tensor(x_sb[:, :, :], x_sb[:, :, :], b4_row[:, :].unsqueeze(1).to_broadcast([PART, BLOCKS, D]), ALU.add))

            centred("l3")
            link(normed(h_sb[:, :, :], 0, BLOCKS))
            dve.sem_inc(S("l3_h"), 1)
            sums("l3", D)
            link(vec.tensor_tensor(x_sb[:, :, :], x_sb[:, :, :], acc(D)[:, 0:BLOCKS, :], ALU.add))
            dve.sem_inc(S("result"), 1)

        @block.tensor
        def _(pe):
            mm = nc.tensor.matmul
            pe.wait_ge(S("w_zeroed"), 1)
            pe.wait_ge(S("consts"), 1)
            pe.wait_ge(S("block_steps"), 1)
            mm(ps[:, 0, 0:1], MP["tri"][:, 0, :], MP["cols"][:, 4:5], start=True, stop=True).then_inc(S("block_begin"), 1)
            pe.wait_ge(S("block_shift"), 1)
            mm(ps[:, 0, 1:2], MP["tri"][:, 1, :], MP["cols"][:, 6:7], start=True, stop=True).then_inc(S("block_delta"), 1)
            pe.wait_ge(S("block_begun"), 1)
            begun = big[:, 2 * TILES + MAPPED:2 * TILES + 2 * MAPPED]
            for m in range(MAP_MMS):
                cols = slice(m * MAP_COLS, (m + 1) * MAP_COLS)
                if m >= 2:
                    pe.wait_ge(S("steps_read"), m - 1)
                mm(ps[0:1, 2 * (m % 2), 0:MAP_COLS], MP["cols"][:, 7:8], begun[:, cols], start=True, stop=True)
                mm(ps[0:1, 2 * (m % 2) + 1, 0:MAP_COLS], ones_col, begun[:, cols], start=True, stop=True).then_inc(S("steps_summed"), 1)
            pe.wait_ge(S("steps_read"), MAP_MMS)

            def map_chunk(i, b, first):
                pe.wait_ge(S("map_rows"), i * 2 + b + 1)
                if not first:
                    pe.wait_ge(S("map_done"), i * 2 + b - 1)
                for k, edges in enumerate((MP["got"][:, b, 0, :], MP["rel"][:, b, :], MP["end"][:, b, :])):
                    ins = nc.tensor.transpose(ps[:, b, k * PART:(k + 1) * PART], edges, ident[:, :])
                ins.then_inc(S("map_turned"), 1)
            for b in range(2):
                map_chunk(0, b, True)
            with pe.Fori(1, MAP_CHUNKS // 2) as i:
                for b in range(2):
                    map_chunk(i, b, False)
            pe.wait_ge(S("map_done"), MAP_CHUNKS)

            turned = lambda rows_, b0, k: ps[0:rows_, b0 + k // 4, (k % 4) * PART:(k % 4 + 1) * PART]

            with pe.Fori(0, CHUNKS) as c:
                pe.wait_ge(S("l0_h"), c + 1)
                pe.sem_inc(S("pe_begun"), 1)
                for k in range(CH):
                    ins = nc.tensor.transpose(turned(D, 0, k), L0["hc"][:, k, :], ident[:, :])
                ins.then_inc(S("l0_hT"), 1)
                pe.wait_ge(S("l0_hT_out"), c + 1)
                for k in range(CH):
                    ins = mm(turned(PART, 2, k), L0["hT"][:, k * PART:(k + 1) * PART], w_pq[:, :], start=True, stop=True)
                ins.then_inc(S("l0_pq"), 1)
            pe.wait_ge(S("l0_piece"), 4 * CHUNKS)
            pe.wait_ge(S("q_staged"), CHUNKS)

            def pre0(n, s, i):
                _, got = nc.values_load_multi_w_load_instructions(
                    block_row[:, bass.ds(i * UNROLL + s * SLOT, SLOT)], engines=[pe.engine], min_val=0, max_val=BLOCKS)
                pe.wait_ge(S(f"l0_rows{s}"), i * (16 * SLOT) + 16 * SLOT)
                pe.wait_ge(S("l0_ohT"), n + 1)
                if not isinstance(n, int) or n >= 2:
                    pe.wait_ge(S("l0_relu"), n - 1)
                for k in range(SLOT):
                    target = ps[0:D, s % 2, k * PART:(k + 1) * PART]
                    ins = mm(target, rows[:, s, k, 0:D], ident[:, :], start=True, stop=False)
                    for piece in range(3):
                        ins = mm(target, p_split[:, bass.ds(got[k], 1), piece, :].rearrange("p o f -> p (o f)"),
                                 L0E["ohT"][:, s, k * PART:(k + 1) * PART], start=False, stop=piece == 2)
                ins.then_inc(S("l0_pre"), 1)

            def msg0(m, s, i):
                pe.wait_ge(S("l0_relu"), m + 1)
                if not isinstance(m, int) or m >= 2:
                    pe.wait_ge(S("l0_scan"), m - 1)
                mm(ps[0:D, 2 + s % 2, :], w_msg[:, :], L0E["pre"][:, s % 2, :], start=True, stop=True).then_inc(S("l0_msg"), 1)

            def turn0(m, s, i):
                pe.wait_ge(S("l0_scan"), m + 1)
                if not isinstance(m, int) or m >= 2:
                    pe.wait_ge(S("l0_turned"), m - 1)
                pe.sem_inc(S("pe_begun"), 1)
                for k in range(SLOT):
                    ins = nc.tensor.transpose(ps[:, 4 + s % 2, k * D:(k + 1) * D],
                                              L0E["scan"][:, s % 2, k * PART:(k + 1) * PART], ident[0:D, 0:D])
                ins.then_inc(S("l0_turn"), 1)

            def ends0(m, s, i):
                pe.wait_ge(S("l0_turned"), m + 1)
                pe.wait_ge(S("l0_oh"), m + 1)
                if not isinstance(m, int) or m >= 2:
                    pe.wait_ge(S("l0_added"), (m - 1) * SLOT)
                for k in range(SLOT):
                    ins = mm(ps[:, 6 + s % 2, k * D:(k + 1) * D], L0E["oh"][:, s % 2, k, :], L0E["scanT"][:, s % 2, k, :],
                             start=True, stop=True)
                ins.then_inc(S("l0_ends"), 1)

            def slot0(i, s):
                for lag, work in ((0, pre0), (1, msg0), (2, turn0), (3, ends0)):
                    sl, it = (s - lag) % SLOTS, i + (-1 if s < lag else 0)
                    m = i * SLOTS + (s - lag)
                    if isinstance(m, int) and not 0 <= m < ITERS * SLOTS:
                        continue
                    work(m, sl, it)
            for s in range(SLOTS):
                slot0(0, s)
            with pe.Fori(1, ITERS) as i:
                for s in range(SLOTS):
                    slot0(i, s)
            for s in range(3):
                slot0(ITERS, s)

            def sums(layer, width):
                with pe.Fori(0, ITERS) as i:
                    for s in range(SLOTS):
                        pe.wait_ge(S(f"{layer}_rows{s}"), i * (16 * SLOT) + 16 * SLOT)
                        pe.wait_ge(S(f"{layer}_oh"), i * SLOTS + s + 1)
                        for k in range(SLOT):
                            ins = mm(ps[:, s, k * width:(k + 1) * width], SUM["oh"][:, s, k, :], rows[:, s, k, 0:width],
                                     start=True, stop=True)
                        ins.then_inc(S(f"{layer}_sum"), 1)

            sums("l1a", D + 1)
            pe.wait_ge(S("l1a_added"), STEPS)
            with pe.Fori(0, CHUNKS) as c:
                pe.wait_ge(S("l1_nodes"), c + 1)
                for k in range(CH):
                    ins = nc.tensor.transpose(turned(PART, 0, k), L1["cat"][:, k, :], ident[:, :])
                ins.then_inc(S("l1_cat"), 1)
                pe.wait_ge(S("l1_catT"), c + 1)
                for b in range(2):
                    ins = mm(ps[:, 2 + b, 0:CH_N // 2], w1_cat[:, :], L1["catT"][:, b * CH_N // 2:(b + 1) * CH_N // 2],
                             start=True, stop=True)
                ins.then_inc(S("l1_hid"), 1)
                pe.wait_ge(S("l1_h1T"), c + 1)
                for k in range(CH):
                    ins = mm(turned(PART, 4, k), L1["h1T"][:, k * PART:(k + 1) * PART], w2_cat[:, :], start=True, stop=True)
                ins.then_inc(S("l1_zy"), 1)
            pe.wait_ge(S("z_staged"), CHUNKS)
            sums("l1b", D)
            pe.wait_ge(S("l1b_added"), STEPS)

            with pe.Fori(0, CHUNKS) as c:
                pe.wait_ge(S("l2_h"), c + 1)
                pe.sem_inc(S("pe_begun"), 1)
                for k in range(CH):
                    ins = nc.tensor.transpose(turned(D, 0, k), L2R["hc"][:, k, :], ident[:, :])
                ins.then_inc(S("l2_hT"), 1)
                pe.wait_ge(S("l2_hT_out"), c + 1)
                for k in range(CH):
                    ins = mm(turned(PART, 2, k), L2R["hT"][:, k * PART:(k + 1) * PART], w_r[:, :], start=True, stop=True)
                ins.then_inc(S("l2_r"), 1)
            pe.wait_ge(S("r_staged"), CHUNKS)

            def pre2(n, s, i):
                pe.wait_ge(S(f"l2_ea{s}"), i * (16 * SLOT) + 16 * SLOT)
                pe.wait_ge(S(f"l2_rows{s}"), i * (16 * SLOT) + 16 * SLOT)
                if not isinstance(n, int) or n >= 2:
                    pe.wait_ge(S("l2_relu"), n - 1)
                for k in range(SLOT):
                    ins = mm(ps[:, s % 2, k * HID:(k + 1) * HID], L2E["ea"][:, s, k, :], w_e[:, :], start=True, stop=False)
                    ins = mm(ps[:, s % 2, k * HID:(k + 1) * HID], ident[:, :], rows[:, s, k, :], start=False, stop=True)
                ins.then_inc(S("l2_pre"), 1)

            def sum2(m, s, i):
                pe.wait_ge(S("l2_relu"), m + 1)
                pe.wait_ge(S("l2_oh"), m + 1)
                if not isinstance(m, int) or m >= 2:
                    pe.wait_ge(S("l2_added"), (m - 1) * SLOT)
                for k in range(SLOT):
                    ins = mm(ps[:, 2 + s % 2, k * HID:(k + 1) * HID], L2E["oh"][:, s, k, :], L2E["act"][:, s % 2, k, :],
                             start=True, stop=True)
                ins.then_inc(S("l2_sum"), 1)

            def slot2(i, s):
                for lag, work in ((0, pre2), (1, sum2)):
                    sl, it = (s - lag) % SLOTS, i + (-1 if s < lag else 0)
                    m = i * SLOTS + (s - lag)
                    if isinstance(m, int) and not 0 <= m < ITERS * SLOTS:
                        continue
                    work(m, sl, it)
            for s in range(SLOTS):
                slot2(0, s)
            with pe.Fori(1, ITERS) as i:
                for s in range(SLOTS):
                    slot2(i, s)
            slot2(ITERS, 0)
            pe.wait_ge(S("l2_added"), STEPS)
            with pe.Fori(0, CHUNKS) as c:
                pe.wait_ge(S("l2_nodes"), c + 1)
                for k in range(CH):
                    nc.tensor.transpose(turned(PART, 0, k), L2P["m"][:, k, :], ident[:, :])
                for k in range(CH):
                    ins = nc.tensor.transpose(turned(D + 1, 2, k), L2P["hi"][:, k, :], ident[:, :])
                ins.then_inc(S("l2_mT"), 1)
                pe.wait_ge(S("l2_mT_out"), c + 1)
                for b in range(2):
                    half = slice(b * CH_N // 2, (b + 1) * CH_N // 2)
                    mm(ps[0:D, 4 + b, 0:CH_N // 2], w_agg[:, :], L2P["mT"][:, half], start=True, stop=False)
                    ins = mm(ps[0:D, 4 + b, 0:CH_N // 2], b_agg[:, :], L2P["hT"][:, half], start=False, stop=True)
                ins.then_inc(S("l2_agg"), 1)
                pe.wait_ge(S("l2_aT"), c + 1)
                for b in range(2):
                    half = slice(b * CH_N // 2, (b + 1) * CH_N // 2)
                    mm(ps[:, 6 + b, 0:CH_N // 2], w3_h[:, :], L2P["hT"][0:D, half], start=True, stop=False)
                    ins = mm(ps[:, 6 + b, 0:CH_N // 2], w3_a[:, :], L2P["aT"][:, half], start=False, stop=True)
                ins.then_inc(S("l2_g"), 1)
                pe.wait_ge(S("l2_gT"), c + 1)
                for k in range(CH):
                    ins = mm(ps[:, 0, k * D:(k + 1) * D], L2P["gT"][:, k * PART:(k + 1) * PART], w4[:, :], start=True, stop=True)
                ins.then_inc(S("l2_out"), 1)
            pe.wait_ge(S("l2_x"), CHUNKS)
            sums("l3", D)


_INS = ["x", "src", "dst", "L0_gnn_W1", "L0_gnn_b1", "L0_gnn_W2", "L0_gnn_b2", "L1_gnn_W1_l", "L1_gnn_b1", "L1_gnn_W1_r",
        "L1_gnn_W2_l", "L1_gnn_b2", "L1_gnn_W2_r", "L2_gnn_W1", "L2_gnn_b1", "L2_gnn_W2", "L2_gnn_b2", "L2_gnn_W3", "L2_gnn_b3",
        "L2_gnn_W4", "L2_gnn_b4"]


def kernel(**inputs):
    import concourse.bacc as bacc
    from concourse.bass_utils import run_bass_kernel_spmd

    nc = bacc.Bacc("TRN2", target_bir_lowering=False, num_devices=1)
    arrays = {name: np.ascontiguousarray(inputs[name]) for name in _INS}
    arrays["edge_attr_T"] = np.ascontiguousarray(
        np.asarray(inputs["edge_attr_32"]).reshape(TILES, PART, DE).transpose(0, 2, 1))
    aps = {name: nc.dram_tensor(name, a.shape, mybir.dt.from_np(a.dtype), kind="ExternalInput").ap()
           for name, a in arrays.items()}
    out = nc.dram_tensor("out", (NODES, D), F32, kind="ExternalOutput").ap()
    gnn_kernel(nc, aps, out)
    result = run_bass_kernel_spmd(nc, [arrays], core_ids=[0])
    return result.results[0]["out"]
```

```python
import numpy as np
import concourse.bass as bass
from concourse import mybir
from contextlib import ExitStack

F32 = mybir.dt.float32
BF16 = mybir.dt.bfloat16
I32 = mybir.dt.int32
I16 = mybir.dt.int16
U8 = mybir.dt.uint8
F16 = mybir.dt.float16
ALU = mybir.AluOpType
ACT = mybir.ActivationFunctionType
AX = mybir.AxisListType.X

PART = 128
NODES, D = 12500, 64
EDGES, DE = 400000, 32
HID = 128
TILES = EDGES // PART
BLOCKS = -(-NODES // PART)
NODES_PAD = BLOCKS * PART
LAST_ROWS = NODES - (BLOCKS - 1) * PART
SLOT = 4
SLOTS = 4
UNROLL = SLOT * SLOTS
ITERS = -(-(TILES + BLOCKS - 1) // UNROLL)
STEPS = ITERS * UNROLL
SLOT_E = SLOT * PART
MAPPED = -(-STEPS // PART) * PART
MAP_CHUNKS = MAPPED // PART
STEP_COLS = MAPPED + UNROLL
NAT_P = 125
NAT_T = TILES // NAT_P
NAT_E = NAT_T * PART
CH = 7
CHUNKS = BLOCKS // CH
CH_N = CH * PART
BIG = 1.5e38
EPS = 1e-5
GROUP = 4
GROUPS = (ITERS * SLOTS + SLOTS) * 4
GROUP_CHUNKS = -(-GROUPS // PART)
HOT = GROUP * BLOCKS
WIN_STEP = 32
WINDOW = 2 * PART
WINDOWS = -(-(EDGES // WIN_STEP + 1) // 16) * 16
EDGES_PAD = (WINDOWS - 1) * WIN_STEP + WINDOW
NOWHERE = 1 << 14
ADJ_BLOCKS = ITERS * SLOTS * 4 * GROUP // PART
HALF_B = BLOCKS // 2
MAP_COLS = 416
MAP_MMS = MAPPED // MAP_COLS


def gnn_kernel(nc, A, out):
    ctx = ExitStack()
    with ctx:
        def sb(name, shape, dt=F32, stack=ctx):
            return stack.enter_context(nc.sbuf_tensor(name, shape, dt))

        def dram(name, shape, dt=F32):
            return nc.dram_tensor(name, shape, dt).ap()

        ctx.enter_context(nc.allow_non_contiguous_dma(reason="a few single words for each partition"))
        sems = {}

        def S(name):
            if name not in sems:
                sems[name] = ctx.enter_context(nc.semaphore(name))
            return sems[name]

        tile_table = dram("tile_table", (TILES, 4 * PART))
        tile_ends = dram("tile_ends", (2, TILES))
        pad_dst = dram("pad_dst", (EDGES_PAD,), I32)
        pad_src = dram("pad_src", (EDGES_PAD,), I32)
        windows = dram("windows", (WINDOWS, 2 * WINDOW), I32)
        adjacency = [dram(f"adjacency{k}", (ADJ_BLOCKS, PART, HALF_B * PART), BF16) for k in range(2)]
        step_rows = dram("step_rows", (2, MAPPED), I16)
        step_rel = dram("step_rel", (MAPPED, PART), I16)
        step_mask = dram("step_mask", (MAPPED, PART), BF16)
        q_table = dram("q_table", (NODES_PAD, D))
        h1_table = dram("h1_table", (NODES_PAD, D))
        z_table = dram("z_table", (NODES_PAD, D))
        r_table = dram("r_table", (NODES_PAD, HID))
        h3_table = dram("h3_table", (NODES_PAD, D))
        blocked = "(g p) f -> p g f"

        xh = sb("xh", [PART, 2, BLOCKS, D])
        x_sb = xh[:, 0, :, :]
        h_sb = xh[:, 1, :, :]
        adj_out = xh[:, :, :, :].rearrange("p k g f -> p (k g f)").bitcast(BF16).rearrange("p (k h j) -> p k h j", k=2, j=PART)
        ACC_WORDS = (BLOCKS + 1) * (D + 1)
        P_WORDS = max((BLOCKS + 1) * 3 * D, BLOCKS * 3 * (D + 1)) // 2
        big = sb("big", [PART, ACC_WORDS + P_WORDS])
        src_st = sb("src_st", [PART, STEP_COLS], I16)
        rel_st = sb("rel_st", [PART, STEP_COLS], I16)
        end_st = sb("end_st", [PART, STEP_COLS], I16)
        block_row = sb("block_row", [1, STEP_COLS], I16)
        tile_row = end_st[0:1, :]
        iota_hot = sb("iota_hot", [PART, HOT], F16)
        bad_row = sb("bad_row", [1, 4], I32)
        ident = sb("ident", [PART, PART])
        iota_f = sb("iota_f", [PART, PART])
        iota_p = sb("iota_p", [PART, 1])
        small = sb("small", [PART, 4, BLOCKS])
        deg_inv = sb("deg_inv", [PART, BLOCKS])
        has_edge = sb("has_edge", [PART, BLOCKS])
        eps_t = sb("eps_t", [PART, 1])
        idx = sb("idx", [PART, SLOTS, SLOT], I32)
        rows = sb("rows", [PART, SLOTS, SLOT, HID])
        w_pq = sb("w_pq", [D + 1, 2 * D])
        w_msg = sb("w_msg", [D + 1, D])
        w1_cat = sb("w1_cat", [2 * D, HID])
        w2_cat = sb("w2_cat", [HID, 2 * D])
        b1_col = sb("b1_col", [HID, 1])
        b2_row = sb("b2_row", [PART, D])
        w_r = sb("w_r", [D + 1, HID])
        w_e = sb("w_e", [DE, HID])
        w_agg = sb("w_agg", [HID, D])
        b_agg = sb("b_agg", [D + 1, D])
        w3_h = sb("w3_h", [D, HID])
        w3_a = sb("w3_a", [D, HID])
        b3_col = sb("b3_col", [HID, 1])
        w4 = sb("w4", [HID, D])
        b4_row = sb("b4_row", [PART, D])

        def acc(width):
            return big[:, 0:(BLOCKS + 1) * width].rearrange("p (g f) -> p g f", f=width)

        def split(width, n):
            words = n * 3 * width // 2
            return big[:, ACC_WORDS:ACC_WORDS + words].bitcast(BF16).rearrange("p (g k f) -> p g k f", k=3, f=width)

        p_split = split(D, BLOCKS + 1)
        squares = big[:, 0:BLOCKS * D].rearrange("p (g f) -> p g f", f=D)

        ones_col = rows[:, 0, 0, D:D + 1]
        ps = ctx.enter_context(nc.psum_tensor("ps", [PART, 8, 512], F32))

        def stage(make):
            with ExitStack() as st:
                return make(lambda name, shape, dt=F32: sb(name, shape, dt, st))

        def map_bufs(a):
            return dict(raw=h_sb[:, :, :].rearrange("p g f -> p (g f)").bitcast(I32)[0:NAT_P, 0:NAT_E], cat=a("cat", [NAT_P, NAT_E + 2]),
                        st_idx=a("st_idx", [PART, 2, MAP_CHUNKS], I16), near=a("near", [PART, 2, 1], I32), ends=a("ends", [NAT_P, 2, NAT_T]), cols=a("cols", [PART, 8]), tri=a("tri", [PART, 2, PART]),
                        cur=a("cur", [PART, 2, 1], I32),
                        got=a("got", [PART, 2, 4, PART]), rel=a("rel", [PART, 2, PART]), end=a("end", [PART, 2, PART]),
                        rel16=a("rel16", [PART, 2, PART], I16), mask16=a("mask16", [PART, 2, PART], BF16),
                        blk=a("blk", [PART, MAP_CHUNKS]))

        def adj_bufs(a):
            return dict(hot=a("hot_st", [PART, GROUP_CHUNKS * WINDOW], I16),
                        low=a("low_st", [PART, GROUP_CHUNKS * WINDOW], U8),
                        oh_hot=a("oh_hot", [PART, 4, 2, HOT], BF16), oh_low=a("oh_low", [PART, 4, 2, PART], BF16))

        def group_bufs(a):
            return dict(node0=a("node0", [PART, GROUP_CHUNKS]), node4=a("node4", [PART, GROUP_CHUNKS]),
                        tile=a("tile", [PART, GROUP_CHUNKS]), inside=a("inside", [PART, GROUP_CHUNKS]),
                        bad=a("bad", [PART, GROUP_CHUNKS]), tile_i=a("tile_i", [PART, GROUP_CHUNKS], I32),
                        win_i=a("win_i", [PART, GROUP_CHUNKS], I32), cur=a("gcur", [PART, 2, 1], I32),
                        dst=a("gdst", [PART, 2, PART], I32), win=a("gwin", [PART, 2, 2, WINDOW], I32),
                        below=a("below", [PART, PART]), node=a("gnode", [PART, WINDOW]), ok=a("gok", [PART, WINDOW]),
                        sblk=a("gsblk", [PART, WINDOW], I32), slow=a("gslow", [PART, WINDOW], I32),
                        hot=a("ghot", [PART, 2, WINDOW]), low=a("glow", [PART, 2, WINDOW]), sum=a("gsum", [PART, 1]))

        def ring_bufs(a):
            return dict(adj=a("ring", [PART, 4, HALF_B, PART], BF16))

        def l0_bufs(a):
            return dict(hc=a("hc0", [PART, CH, D]), hT=a("hT0", [D + 1, CH_N]), qst=a("qst", [PART, CH, D]),
                        pres=a("pres", [PART, CH, D]))

        def l0_loop_bufs(a):
            return dict(rel=a("rel_row", [PART, SLOTS, SLOT_E], I16), mask=a("mask_row", [D, SLOTS, SLOT_E], BF16),
                        ohT=a("ohT", [PART, 2, SLOT_E], BF16), pre=a("pre", [D + 1, 2, SLOT_E]),
                        scan=a("scan", [D, 2, SLOT_E]), scanT=a("scanT", [PART, 2, SLOT, D]),
                        oh=a("oh0", [PART, 2, SLOT, PART]))

        def sum_bufs(a):
            return dict(oh=a("oh_sum", [PART, SLOTS, SLOT, PART]))

        def l1_bufs(a):
            return dict(cat=a("cat1", [PART, CH, 2 * D]), catT=a("catT", [PART, CH_N]), h1T=a("h1T", [PART, CH_N]),
                        zst=a("zst", [PART, CH, D]), spare=a("zspare", [PART, CH, D]))

        def l2_pre_bufs(a):
            return dict(hc=a("hc2", [PART, CH, D]), hT=a("hT2", [D + 1, CH_N]), rst=a("rst", [PART, CH, HID]))

        def l2_loop_bufs(a):
            return dict(oh=a("oh2", [PART, SLOTS, SLOT, PART]), ea=a("ea", [DE, SLOTS, SLOT, PART]),
                        act=a("act2", [PART, 2, SLOT, HID]))

        def l2_post_bufs(a):
            return dict(m=a("m2", [PART, CH, HID]), hi=a("hi", [PART, CH, D + 1]), mT=a("mT", [PART, CH_N]),
                        hT=a("hTi", [D + 1, CH_N]), aT=a("aT", [D, CH_N]), gT=a("gT", [PART, CH_N]))

        with ExitStack() as l0_stack:
            ADJ = adj_bufs(lambda name, shape, dt=F32: sb(name, shape, dt, l0_stack))
            MP, GRP, L0, L0E = (stage(m) for m in (map_bufs, group_bufs, l0_bufs, l0_loop_bufs))
        SUM, L1, L2R, L2E, L2P, RING = (stage(m) for m in (sum_bufs, l1_bufs, l2_pre_bufs, l2_loop_bufs, l2_post_bufs, ring_bufs))

        def bad_groups(eng):
            eng.wait_ge(S("bad_known"), 1)
            _, (bad,) = nc.values_load_multi_w_load_instructions(bad_row[0:1, 0:1], engines=[eng.engine], min_val=0,
                                                                 max_val=GROUPS)
            return bad

        block = ctx.enter_context(nc.Block())
        NORMS = ("l0", "l1a", "l2", "l3")
        DENSE = {"l1a": 0, "l1b": 1, "l3": 2}

        def finish(sp):
            sp.wait_ge(S("result"), 1)
            sp.dma_start(out[0:(BLOCKS - 1) * PART, :].rearrange(blocked, p=PART), x_sb[:, 0:BLOCKS - 1, :]
                         ).then_inc(S("out_stored"), 16)
            sp.dma_start(out[(BLOCKS - 1) * PART:, :], x_sb[0:LAST_ROWS, BLOCKS - 1, :]).then_inc(S("out_stored"), 16)
            sp.wait_ge(S("out_stored"), 32)

        @block.sync
        def _(sp):
            sp.dma_start(x_sb[:, 0:BLOCKS - 1, :],
                         A["x"][0:(BLOCKS - 1) * PART, :].rearrange(blocked, p=PART)).then_inc(S("x_loaded"), 16)
            sp.wait_ge(S("x_zeroed"), 1)
            sp.dma_start(x_sb[0:LAST_ROWS, BLOCKS - 1, :], A["x"][(BLOCKS - 1) * PART:, :]).then_inc(S("x_loaded"), 16)

            sp.wait_ge(S("cat_ends"), 1)
            col = lambda e0, n: A["dst"][e0:e0 + (n - 1) * NAT_E + 1:NAT_E].rearrange("(p o) -> p o", o=1)
            sp.dma_start(MP["near"][1:NAT_P, 0, :], col(NAT_E - 1, NAT_P - 1)).then_inc(S("edge_ends"), 16)
            sp.dma_start(MP["near"][0:NAT_P - 1, 1, :], col(NAT_E, NAT_P - 1)).then_inc(S("edge_ends"), 16)
            for name, padded, fill in (("dst", pad_dst, 0), ("src", pad_src, 1)):
                sp.dma_start(padded[0:EDGES].rearrange("(p e) -> p e", p=PART),
                             A[name].rearrange("(p e) -> p e", p=PART)).then_inc(S("padded"), 16)
                sp.dma_start(padded[EDGES:].rearrange("(p e) -> p e", p=WIN_STEP),
                             MP["got"][0:WIN_STEP, fill, 0, 0:(EDGES_PAD - EDGES) // WIN_STEP].bitcast(I32)
                             ).then_inc(S("padded"), 16)
            for n, name in enumerate(("dst", "src")):
                view = A[name].rearrange("(p e) -> p e", p=NAT_P)
                if n:
                    sp.wait_ge(S("raw_used"), 1)
                sp.dma_start(MP["raw"], view).then_inc(S("raw_loaded"), 16)
            for name, dst_ap in (("L0_gnn_W2", w_msg[0:D, :]), ("L1_gnn_W1_l", w1_cat[0:D, :]),
                                 ("L1_gnn_W1_r", w1_cat[D:2 * D, :]), ("L1_gnn_W2_l", w2_cat[:, 0:D]),
                                 ("L1_gnn_W2_r", w2_cat[:, D:2 * D]), ("L2_gnn_W2", w_agg[:, :]), ("L2_gnn_W4", w4[:, :])):
                sp.dma_start(dst_ap, A[name]).then_inc(S("weights"), 16)
            row = lambda name: A[name].rearrange("(o f) -> o f", o=1)
            column = lambda name: A[name].rearrange("(f o) -> f o", o=1)
            W1 = A["L0_gnn_W1"]
            sp.dma_start(w_pq[0:D, 0:D], W1[0:D, :]).then_inc(S("weights"), 16)
            sp.dma_start(w_pq[0:D, D:2 * D], W1[D:2 * D, :]).then_inc(S("weights"), 16)
            sp.dma_start(w_msg[D:D + 1, :], row("L0_gnn_b2")).then_inc(S("weights"), 16)
            sp.dma_start(b1_col[:, :], column("L1_gnn_b1")).then_inc(S("weights"), 16)
            sp.dma_start(b3_col[:, :], column("L2_gnn_b3")).then_inc(S("weights"), 16)
            sp.dma_start(w_r[0:D, :], A["L2_gnn_W1"][0:D, :]).then_inc(S("weights"), 16)
            sp.dma_start(w_r[D:D + 1, :], row("L2_gnn_b1")).then_inc(S("weights"), 16)
            sp.dma_start(w_e[:, :], A["L2_gnn_W1"][D:D + DE, :]).then_inc(S("weights"), 16)
            sp.dma_start(w3_h[:, :], A["L2_gnn_W3"][0:D, :]).then_inc(S("weights"), 16)
            sp.dma_start(w3_a[:, :], A["L2_gnn_W3"][D:2 * D, :]).then_inc(S("weights"), 16)
            sp.dma_start(b2_row[:, :], row("L1_gnn_b2").to_broadcast([PART, D])).then_inc(S("weights"), 16)
            sp.dma_start(b4_row[:, :], row("L2_gnn_b4").to_broadcast([PART, D])).then_inc(S("weights"), 16)
            sp.wait_ge(S("w_zeroed"), 1)
            sp.dma_start(w_pq[D:D + 1, 0:D], row("L0_gnn_b1")).then_inc(S("weights"), 16)
            sp.dma_start(b_agg[D:D + 1, :], row("L2_gnn_b2")).then_inc(S("weights"), 16)

            sp.wait_ge(S("padded"), 64)
            for n, padded in enumerate((pad_dst, pad_src)):
                overlapping = bass.AP(tensor=padded.tensor, offset=0, ap=[[WIN_STEP, WINDOWS], [1, WINDOW]])
                sp.dma_start(windows[:, n * WINDOW:(n + 1) * WINDOW], overlapping).then_inc(S("windowed"), 16)
            sp.wait_ge(S("tiles_built"), 1)
            sp.dma_start(tile_table.rearrange("(p t) f -> p (t f)", p=NAT_P),
                         big[0:NAT_P, 0:NAT_T * 4 * PART]).then_inc(S("table_stored"), 16)
            sp.dma_start(tile_ends.rearrange("k (p t) -> p k t", p=NAT_P), MP["ends"][:, :, :]).then_inc(S("ends_stored"), 16)
            sp.wait_ge(S("ends_stored"), 16)
            sp.wait_ge(S("table_stored"), 16)
            sp.dma_start(big[:, 0:2 * TILES].rearrange("p (k t) -> p k t", k=2),
                         tile_ends.unsqueeze(0).to_broadcast([PART, 2, TILES])).then_inc(S("ends_spread"), 16)
            sp.wait_ge(S("steps_mapped"), 1)
            sp.dma_start(step_rows[0:1, :], tile_row[:, 0:MAPPED]).then_inc(S("steps_stored"), 16)
            sp.dma_start(step_rows[1:2, :], block_row[:, 0:MAPPED]).then_inc(S("steps_stored"), 16)
            sp.wait_ge(S("steps_stored"), 32)
            sp.dma_start(MP["st_idx"][:, :, :],
                         step_rows.rearrange("k (c p) -> p k c", p=PART)).then_inc(S("steps_turned"), 16)
            with sp.Fori(0, MAP_CHUNKS // 2) as i:
                for b in range(2):
                    sp.wait_ge(S("map_rows"), 2 * i + b + 1)
                    sp.dma_start(step_rel[bass.ds(i * (2 * PART) + b * PART, PART), :], MP["rel16"][:, b, :]
                                 ).then_inc(S(f"map_stored{b}"), 16)
                    sp.dma_start(step_mask[bass.ds(i * (2 * PART) + b * PART, PART), :], MP["mask16"][:, b, :]
                                 ).then_inc(S(f"map_stored{b}"), 16)

            with sp.Fori(0, CHUNKS) as c:
                sp.wait_ge(S("q_staged"), c + 1)
                sp.dma_start(q_table[bass.ds(c * CH_N, CH_N), :].rearrange(blocked, p=PART), L0["qst"][:, :, :]
                             ).then_inc(S("q_stored"), 16)
            for b in range(2):
                sp.wait_ge(S(f"map_stored{b}"), 16 * MAP_CHUNKS)
            def edge_rows(i, s, first):
                n = i * SLOTS + s
                if not first:
                    sp.wait_ge(S("l0_ohT"), n - SLOTS + 1)
                v0 = i * UNROLL + s * SLOT
                sp.dma_start(L0E["rel"][:, s, :], step_rel[bass.ds(v0, SLOT), :].rearrange("v e -> (v e)").unsqueeze(0)
                             .to_broadcast([PART, SLOT_E])).then_inc(S(f"l0_rel{s}"), 16)
                if not first:
                    sp.wait_ge(S("l0_scan"), n - SLOTS + 1)
                sp.dma_start(L0E["mask"][:, s, :], step_mask[bass.ds(v0, SLOT), :].rearrange("v e -> (v e)").unsqueeze(0)
                             .to_broadcast([D, SLOT_E])).then_inc(S(f"l0_mask{s}"), 16)
            sp.wait_ge(S("q_stored"), 16 * CHUNKS)
            sp.wait_ge(S("l0_piece"), 4 * CHUNKS)
            for s in range(SLOTS):
                edge_rows(0, s, True)
            def store_block(b):
                sp.wait_ge(S("l0_evac"), b * 16 + 16)
                for half in range(2):
                    sp.dma_start(adjacency[half][bass.ds(b, 1), :, :].rearrange("o p f -> (o p) f"),
                                 adj_out[:, bass.ds(b % 2, 1), half * HALF_B:(half + 1) * HALF_B, :].rearrange("p o h j -> p (o h j)")
                                 ).then_inc(S("adj_stored"), 16)

            with sp.Fori(0, ADJ_BLOCKS - 1) as b:
                for s in range(2 * SLOTS):
                    edge_rows(b * 2 + 1 + s // SLOTS, s % SLOTS, False)
                store_block(b)
            for s in range(SLOTS + 1):
                edge_rows(ITERS - 1 + s // SLOTS, s % SLOTS, False)
            store_block(ADJ_BLOCKS - 1)
            sp.wait_ge(S("adj_stored"), 2 * 16 * ADJ_BLOCKS)
            sp.dma_start(x_sb[:, 0:BLOCKS - 1, :],
                         A["x"][0:(BLOCKS - 1) * PART, :].rearrange(blocked, p=PART)).then_inc(S("x_back"), 16)
            sp.wait_ge(S("x_cleared"), 1)
            sp.dma_start(x_sb[0:LAST_ROWS, BLOCKS - 1, :], A["x"][(BLOCKS - 1) * PART:, :]).then_inc(S("x_back"), 16)

            def adjacency_blocks(layer):
                used = DENSE[layer] * 2 * BLOCKS

                def half(b, k, first):
                    if not first:
                        sp.wait_ge(S("adj_used"), b * 2 + (used + k - 3))
                    sp.dma_start(RING["adj"][:, k, :, :].rearrange("p h j -> p (h j)"),
                                 adjacency[k % 2][bass.ds(b + k // 2, 1), :, :].rearrange("o p f -> (o p) f")
                                 ).then_inc(S(f"adj_half{k}"), 16)
                for k in range(4):
                    half(0, k, True)
                with sp.Fori(1, HALF_B) as i:
                    for k in range(4):
                        half(i * 2, k, False)

            bad = bad_groups(sp)
            sp.wait_ge(S("l1a_h"), 1)
            with sp.If(bad == 0):
                adjacency_blocks("l1a")
            with sp.Else():
                sp.dma_start(h1_table.rearrange(blocked, p=PART), h_sb[:, :, :]).then_inc(S("l1a_table"), 16)
            with sp.Fori(0, CHUNKS) as c:
                sp.wait_ge(S("z_staged"), c + 1)
                sp.dma_start(z_table[bass.ds(c * CH_N, CH_N), :].rearrange(blocked, p=PART), L1["zst"][:, :, :]
                             ).then_inc(S("z_stored"), 16)
            sp.wait_ge(S("z_stored"), 16 * CHUNKS)
            sp.wait_ge(S("l1b_nodes"), 1)
            with sp.If(bad == 0):
                adjacency_blocks("l1b")
            with sp.Fori(0, CHUNKS) as c:
                sp.wait_ge(S("r_staged"), c + 1)
                sp.dma_start(r_table[bass.ds(c * CH_N, CH_N), :].rearrange(blocked, p=PART), L2R["rst"][:, :, :]
                             ).then_inc(S("r_stored"), 16)
            sp.dma_start(tile_row[:, 0:MAPPED], step_rows[0:1, :]).then_inc(S("tiles_back"), 16)
            sp.wait_ge(S("tiles_back"), 16)
            def attributes(i, s, first):
                _, tiles = nc.values_load_multi_w_load_instructions(
                    tile_row[:, bass.ds(i * UNROLL + s * SLOT, SLOT)], engines=[sp.engine], min_val=0, max_val=TILES - 1)
                if not first:
                    sp.wait_ge(S("l2_pre"), (i - 1) * SLOTS + s + 1)
                for k in range(SLOT):
                    sp.dma_start(L2E["ea"][:, s, k, :], A["edge_attr_T"][bass.ds(tiles[k], 1), :, :]
                                 .rearrange("o f e -> (o f) e")).then_inc(S(f"l2_ea{s}"), 16)
            sp.wait_ge(S("r_stored"), 16 * CHUNKS)
            for s in range(SLOTS):
                attributes(0, s, True)
            with sp.Fori(1, ITERS) as i:
                for s in range(SLOTS):
                    attributes(i, s, False)
            sp.wait_ge(S("l3_h"), 1)
            with sp.If(bad == 0):
                adjacency_blocks("l3")
            with sp.Else():
                sp.dma_start(h3_table.rearrange(blocked, p=PART), h_sb[:, :, :]).then_inc(S("l3_table"), 16)
            finish(sp)

        @block.gpsimd
        def _(pool):
            nc.gpsimd.memset(x_sb[:, BLOCKS - 1, :], 0.0).then_inc(S("x_zeroed"), 1)
            nc.gpsimd.iota(iota_f[:, :], [[1, PART]], base=0, channel_multiplier=0,
                           allow_small_or_imprecise_dtypes=True).then_inc(S("iotas"), 1)
            nc.gpsimd.iota(iota_p[:, :], [[0, 1]], base=0, channel_multiplier=1,
                           allow_small_or_imprecise_dtypes=True).then_inc(S("iotas"), 1)
            nc.gpsimd.iota(iota_hot[:, :], [[1, HOT]], base=1, channel_multiplier=0,
                           allow_small_or_imprecise_dtypes=True).then_inc(S("iotas"), 1)
            pool.wait_ge(S("table_stored"), 16)
            with pool.Fori(0, MAP_CHUNKS // 2) as i:
                for b in range(2):
                    pool.wait_ge(S("map_idx"), 2 * i + b + 1)
                    pool.sem_inc(S("pool_begun"), 1)
                    nc.gpsimd.indirect_dma_start(
                        out=MP["got"][:, b, :, :].rearrange("p k e -> p (k e)"), out_offset=None, in_=tile_table,
                        in_offset=bass.IndirectOffsetOnAxis(MP["cur"][:, b, :], 0)).then_inc(S(f"map_got{b}"), 16)

            def gathers(layer, table, width, turn=0):
                ready = turn * (ITERS + 1) * SLOTS
                with pool.Fori(0, ITERS) as i:
                    for s in range(SLOTS):
                        pool.wait_ge(S(f"{layer}_idx"), i * SLOTS + (ready + s + 1))
                        pool.sem_inc(S("pool_begun"), 1)
                        for k in range(SLOT):
                            nc.gpsimd.indirect_dma_start(
                                out=rows[:, s, k, 0:width], out_offset=None, in_=table,
                                in_offset=bass.IndirectOffsetOnAxis(idx[:, s, k:k + 1], 0)).then_inc(S(f"{layer}_rows{s}"), 16)

            def group_gathers(name, table, out_of):
                with pool.Fori(0, GROUP_CHUNKS // 2) as i:
                    for b in range(2):
                        pool.wait_ge(S(f"{name}_idx"), i * 2 + b + 1)
                        pool.sem_inc(S("pool_begun"), 1)
                        nc.gpsimd.indirect_dma_start(out=out_of(b), out_offset=None, in_=table,
                                                     in_offset=bass.IndirectOffsetOnAxis(GRP["cur"][:, b, :], 0)
                                                     ).then_inc(S(f"{name}_got{b}"), 16)
            group_gathers("gtile", A["dst"].rearrange("(t e) -> t e", e=PART), lambda b: GRP["dst"][:, b, :])
            pool.wait_ge(S("windowed"), 32)
            group_gathers("gwin", windows, lambda b: GRP["win"][:, b, :, :].rearrange("p k e -> p (k e)"))

            pool.wait_ge(S("q_stored"), 16 * CHUNKS)
            gathers("l0", q_table, D)
            bad = bad_groups(pool)
            with pool.If(bad > 0):
                pool.wait_ge(S("l1a_table"), 16)
                gathers("sum", h1_table, D, DENSE["l1a"])
                pool.wait_ge(S("z_stored"), 16 * CHUNKS)
                gathers("sum", z_table, D, DENSE["l1b"])
            pool.wait_ge(S("r_stored"), 16 * CHUNKS)
            gathers("l2", r_table, HID)
            with pool.If(bad > 0):
                pool.wait_ge(S("l3_table"), 16)
                gathers("sum", h3_table, D, DENSE["l3"])

        @block.scalar
        def _(act):
            def indices(layer, i, s):
                nc.scalar.copy(idx[:, s, :], src_st[:, bass.ds(i * UNROLL + s * SLOT, SLOT)]).then_inc(S(f"{layer}_idx"), 1)

            def standard_deviation(layer):
                act.wait_ge(S("variance"), NORMS.index(layer) + 1)
                nc.scalar.activation(small[:, 2, :], small[:, 1, :], ACT.Sqrt, bias=eps_t[:, :],
                                     scale=1.0 / D).then_inc(S("deviation"), 1)

            act.wait_ge(S("w_zeroed"), 1)
            with act.Fori(0, MAP_CHUNKS // 2) as i:
                for b in range(2):
                    c = i * 2 + b
                    act.wait_ge(S("map_turned"), c + 1)
                    cols = bass.ds(i * (2 * PART) + b * PART, PART)
                    nc.scalar.copy(src_st[:, cols], ps[:, b, 0:PART])
                    nc.scalar.copy(rel_st[:, cols], ps[:, b, PART:2 * PART])
                    nc.scalar.copy(end_st[:, cols], ps[:, b, 2 * PART:3 * PART]).then_inc(S("map_done"), 1)

            with act.Fori(0, GROUP_CHUNKS // 2) as i:
                for b in range(2):
                    act.wait_ge(S("gturned"), i * 2 + b + 1)
                    cols = bass.ds(i * (2 * WINDOW) + b * WINDOW, WINDOW)
                    for n, store in enumerate((ADJ["hot"], ADJ["low"])):
                        ins = nc.scalar.copy(store[:, cols].rearrange("p (g h) -> p h g", h=2),
                                             ps[:, b, n * WINDOW:(n + 1) * WINDOW].rearrange("p (h g) -> p h g", h=2))
                    ins.then_inc(S("group_done"), 1)

            standard_deviation("l0")
            with act.Fori(0, CHUNKS) as c:
                act.wait_ge(S("l0_hT"), c + 1)
                nc.scalar.copy(L0["hT"][0:D, :], ps[0:D, 0:2, :].rearrange("p b f -> p (b f)")[:, 0:CH_N]).then_inc(S("l0_hT_out"), 1)
                act.wait_ge(S("l0_pq"), c + 1)
                nc.scalar.copy(L0["qst"][:, :, :], ps[:, 2:4, :].rearrange("p b (g f) -> p (b g) f", f=2 * D)[:, 0:CH, D:2 * D]
                               ).then_inc(S("q_staged"), 1)
                act.wait_ge(S("q_stored"), c * 16 + 16)

            def evac0(n, b, s, pair):
                act.wait_ge(S("l0_built"), n * 2 + pair + 1)
                at = s * (4 * GROUP) + pair * (2 * GROUP)
                nc.scalar.copy(adj_out[:, bass.ds(b % 2, 1), :, at:at + 2 * GROUP].rearrange("p o h (g j) -> p g (o h) j", g=2),
                               ps[:, 4 + 2 * pair:6 + 2 * pair, 0:HOT].rearrange("p g (h j) -> p g h j", j=GROUP)
                               ).then_inc(S("l0_evac"), 1)

            def relu0(n, s, i):
                act.wait_ge(S("l0_pre"), n + 1)
                if not isinstance(n, int) or n >= 2:
                    act.wait_ge(S("l0_msg"), n - 1)
                nc.scalar.activation(L0E["pre"][0:D, s % 2, :], ps[0:D, 0, :], ACT.Relu).then_inc(S("l0_relu"), 1)
                indices("l0", i + 1, s)

            def turned0(m, s):
                act.wait_ge(S("l0_turn"), m + 1)
                if not isinstance(m, int) or m >= 2:
                    act.wait_ge(S("l0_ends"), m - 1)
                nc.scalar.copy(L0E["scanT"][:, s % 2, :, :], ps[:, 2, 0:SLOT * D].rearrange("p (k f) -> p k f", f=D)
                               ).then_inc(S("l0_turned"), 1)

            def slot0(b, s):
                n = b * (2 * SLOTS) + s
                evac0(n, b, s, 0)
                relu0(n, s % SLOTS, b * 2 + s // SLOTS)
                evac0(n, b, s, 1)
                if not isinstance(n, int) or n >= 2:
                    turned0(b * (2 * SLOTS) + (s - 2), s)

            for s in range(SLOTS):
                indices("l0", 0, s)
            for b in range(2):
                for s in range(2 * SLOTS):
                    slot0(b, s)
            with act.Fori(2, ADJ_BLOCKS) as b:
                act.wait_ge(S("adj_stored"), b * 32 - 32)
                for s in range(2 * SLOTS):
                    slot0(b, s)
            for m in range(ITERS * SLOTS - 2, ITERS * SLOTS):
                turned0(m, m % SLOTS)

            def sums(layer):
                used = DENSE[layer] * ITERS * SLOTS
                for s in range(SLOTS):
                    indices("sum", 0, s)
                with act.Fori(0, ITERS) as i:
                    for s in range(SLOTS):
                        act.wait_ge(S("sum_sum"), i * SLOTS + (used + s + 1))
                        indices("sum", i + 1, s)

            bad = bad_groups(act)
            standard_deviation("l1a")
            with act.If(bad > 0):
                sums("l1a")
            with act.Fori(0, CHUNKS) as c:
                act.wait_ge(S("l1_cat"), c + 1)
                nc.scalar.copy(L1["catT"][:, :], ps[:, 0:2, :].rearrange("p b f -> p (b f)")[:, 0:CH_N]).then_inc(S("l1_catT"), 1)
                act.wait_ge(S("l1_hid"), c + 1)
                for b in range(2):
                    ins = nc.scalar.activation(L1["h1T"][:, b * CH_N // 2:(b + 1) * CH_N // 2], ps[:, 2 + b, 0:CH_N // 2],
                                               ACT.Relu, bias=b1_col[:, :])
                ins.then_inc(S("l1_h1T"), 1)
                act.wait_ge(S("l1_zy"), c + 1)
                nc.scalar.copy(L1["zst"][:, :, :], ps[:, 4:6, :].rearrange("p b (g f) -> p (b g) f", f=2 * D)[:, 0:CH, 0:D]
                               ).then_inc(S("z_staged"), 1)
                act.wait_ge(S("z_stored"), c * 16 + 16)
            with act.If(bad > 0):
                sums("l1b")

            standard_deviation("l2")
            with act.Fori(0, CHUNKS) as c:
                act.wait_ge(S("l2_hT"), c + 1)
                nc.scalar.copy(L2R["hT"][0:D, :], ps[0:D, 0:2, :].rearrange("p b f -> p (b f)")[:, 0:CH_N]).then_inc(S("l2_hT_out"), 1)
                act.wait_ge(S("l2_r"), c + 1)
                nc.scalar.copy(L2R["rst"][:, :, :], ps[:, 2:4, :].rearrange("p b (g f) -> p (b g) f", f=HID)[:, 0:CH, :]
                               ).then_inc(S("r_staged"), 1)
                act.wait_ge(S("r_stored"), c * 16 + 16)

            def relu2(n, s, i):
                act.wait_ge(S("l2_pre"), n + 1)
                if not isinstance(n, int) or n >= 2:
                    act.wait_ge(S("l2_sum"), n - 1)
                nc.scalar.activation(L2E["act"][:, s % 2, :, :].rearrange("p k f -> p (k f)"), ps[:, s % 2, :], ACT.Relu
                                     ).then_inc(S("l2_relu"), 1)
                indices("l2", i + 1, s)

            for s in range(SLOTS):
                indices("l2", 0, s)
            for s in range(SLOTS):
                relu2(s, s, 0)
            with act.Fori(1, ITERS) as i:
                for s in range(SLOTS):
                    relu2(i * SLOTS + s, s, i)
            with act.Fori(0, CHUNKS) as c:
                act.wait_ge(S("l2_mT"), c + 1)
                nc.scalar.copy(L2P["mT"][:, :], ps[:, 0:2, :].rearrange("p b f -> p (b f)")[:, 0:CH_N])
                nc.scalar.copy(L2P["hT"][:, :], ps[0:D + 1, 2:4, :].rearrange("p b f -> p (b f)")[:, 0:CH_N]).then_inc(S("l2_mT_out"), 1)
                act.wait_ge(S("l2_agg"), c + 1)
                nc.scalar.copy(L2P["aT"][:, :].rearrange("p (b f) -> p b f", b=2), ps[0:D, 4:6, 0:CH_N // 2]).then_inc(S("l2_aT"), 1)
                act.wait_ge(S("l2_g"), c + 1)
                nc.scalar.activation(L2P["gT"][:, :].rearrange("p (b f) -> p b f", b=2), ps[:, 6:8, 0:CH_N // 2], ACT.Relu,
                                     bias=b3_col[:, :]).then_inc(S("l2_gT"), 1)
            standard_deviation("l3")
            with act.If(bad > 0):
                sums("l3")

        @block.vector
        def _(dve):
            chain = [0]

            def link(ins):
                chain[0] += 1
                ins.then_inc(S("dve_chain"), 1)
                dve.wait_ge(S("dve_chain"), chain[0])

            def broadcast(ap, shape):
                return ap.unsqueeze(len(shape) - 1).to_broadcast(shape)

            vec = nc.vector
            vec.memset(src_st[:, MAPPED:], 0)
            vec.memset(rel_st[:, MAPPED:], -1.0)
            vec.memset(end_st[:, MAPPED:], -1.0)
            vec.memset(eps_t[:, :], EPS)
            vec.memset(w_pq[D:D + 1, D:2 * D], 0.0)
            vec.memset(rows[:, :, :, D:D + 1], 1.0)
            vec.memset(b_agg[:, :], 0.0)
            vec.memset(block_row[:, MAPPED:], 0).then_inc(S("w_zeroed"), 1)
            dve.wait_ge(S("iotas"), 3)
            vec.tensor_scalar(ident[:, :], iota_f[:, :], iota_p[:, :], None, ALU.is_equal)
            vec.tensor_scalar(MP["tri"][:, 0, :], iota_f[:, :], iota_p[:, :], None, ALU.is_gt)
            link(vec.tensor_scalar(MP["tri"][:, 1, :], iota_f[:, :], 1.0, iota_p[:, :], ALU.subtract, ALU.is_equal))
            vec.tensor_tensor(MP["tri"][:, 1, :], ident[:, :], MP["tri"][:, 1, :], ALU.subtract).then_inc(S("consts"), 1)
            vec.tensor_scalar(MP["cols"][:, 0:1], iota_p[:, :], float(PART), None, ALU.mult)
            vec.tensor_scalar(MP["cols"][:, 1:2], iota_p[:, :], 1.0, float(PART), ALU.add, ALU.mult)
            vec.memset(MP["got"][:, 0, 0, :].bitcast(I32), NOWHERE)
            vec.memset(MP["got"][:, 1, 0, :].bitcast(I32), 0)
            vec.memset(MP["near"][:, :, :], -1).then_inc(S("cat_ends"), 1)
            table = big[0:NAT_P, 0:NAT_T * 4 * PART].rearrange("p (t k e) -> p t k e", k=4, e=PART)
            tiled = lambda ap: ap.rearrange("p (t e) -> p t e", e=PART)
            cat = MP["cat"]
            dve.wait_ge(S("edge_ends"), 32)
            vec.tensor_copy(cat[:, 0:1], MP["near"][0:NAT_P, 0, :])
            vec.tensor_copy(cat[:, NAT_E + 1:], MP["near"][0:NAT_P, 1, :])
            dve.wait_ge(S("raw_loaded"), 16)
            link(vec.tensor_copy(cat[:, 1:NAT_E + 1], MP["raw"]))
            dve.sem_inc(S("raw_used"), 1)
            here = cat[:, 1:NAT_E + 1]
            vec.tensor_copy(table[:, :, 1, :], tiled(here))
            vec.tensor_copy(MP["ends"][:, 0, :], tiled(here)[:, :, 0])
            vec.tensor_copy(MP["ends"][:, 1, :], tiled(here)[:, :, PART - 1])
            link(vec.tensor_tensor(table[:, :, 2, :], tiled(cat[:, 0:NAT_E]), tiled(here), ALU.not_equal))
            vec.tensor_tensor(table[:, :, 3, :], tiled(here), tiled(cat[:, 2:]), ALU.not_equal)
            vec.tensor_scalar(table[:, :, 2, :], table[:, :, 2, :], -2.0 * BIG, BIG, ALU.mult, ALU.add)
            dve.wait_ge(S("raw_loaded"), 32)
            vec.tensor_copy(table[:, :, 0, :], tiled(MP["raw"])).then_inc(S("tiles_built"), 1)
            dve.wait_ge(S("ends_spread"), 16)
            junk = h_sb[:, :, :].rearrange("p g f -> p (g f)")
            link(vec.tensor_scalar(junk[:, 0:TILES], big[:, 0:TILES], MP["cols"][:, 1:2], 0.0, ALU.is_lt, ALU.add,
                                   accum_out=MP["cols"][:, 2:3]))
            link(vec.tensor_scalar(junk[:, TILES:2 * TILES], big[:, TILES:2 * TILES], MP["cols"][:, 0:1], 0.0, ALU.is_lt, ALU.add,
                                   accum_out=MP["cols"][:, 3:4]))
            link(vec.tensor_tensor(MP["cols"][:, 4:5], MP["cols"][:, 2:3], MP["cols"][:, 3:4], ALU.subtract))
            vec.tensor_scalar(MP["cols"][:, 4:5], MP["cols"][:, 4:5], 0.0, None, ALU.max).then_inc(S("block_steps"), 1)
            dve.wait_ge(S("block_begin"), 1)
            link(vec.tensor_copy(MP["cols"][:, 5:6], ps[:, 0, 0:1]))
            vec.tensor_tensor(MP["cols"][:, 6:7], MP["cols"][:, 3:4], MP["cols"][:, 5:6], ALU.subtract).then_inc(S("block_shift"), 1)
            dve.wait_ge(S("block_delta"), 1)
            link(vec.tensor_copy(MP["cols"][:, 7:8], ps[:, 0, 1:2]))
            iota_v = big[:, 2 * TILES:2 * TILES + MAPPED]
            begun = big[:, 2 * TILES + MAPPED:2 * TILES + 2 * MAPPED]
            link(vec.tensor_scalar(iota_v[:, 0:PART], iota_f[:, :], 0.0, None, ALU.add))
            for c in range(1, MAP_CHUNKS):
                ins = vec.tensor_scalar(iota_v[:, c * PART:(c + 1) * PART], iota_f[:, :], float(c * PART), None, ALU.add)
            link(ins)
            vec.tensor_scalar(begun, iota_v, MP["cols"][:, 5:6], None, ALU.is_ge).then_inc(S("block_begun"), 1)
            for m in range(MAP_MMS):
                cols = slice(m * MAP_COLS, (m + 1) * MAP_COLS)
                dve.wait_ge(S("steps_summed"), m + 1)
                link(vec.tensor_tensor(junk[0:1, 0:MAP_COLS], ps[0:1, 2 * (m % 2), 0:MAP_COLS], iota_v[0:1, cols], ALU.add))
                vec.tensor_scalar(tile_row[:, cols], junk[0:1, 0:MAP_COLS], float(TILES - 1), None, ALU.min)
                link(vec.tensor_scalar(block_row[:, cols], ps[0:1, 2 * (m % 2) + 1, 0:MAP_COLS], 1.0, float(BLOCKS),
                                       ALU.subtract, ALU.min))
                dve.sem_inc(S("steps_read"), 1)
            dve.sem_inc(S("steps_mapped"), 1)
            dve.wait_ge(S("steps_turned"), 16)
            link(vec.tensor_scalar(MP["blk"][:, :], MP["st_idx"][:, 1, :], float(PART), None, ALU.mult))
            for b in range(2):
                vec.tensor_copy(MP["cur"][:, b, :], MP["st_idx"][:, 0, b:b + 1]).then_inc(S("map_idx"), 1)

            def map_chunk(i, b, first, last):
                got, rel, end = MP["got"][:, b, :, :], MP["rel"][:, b, :], MP["end"][:, b, :]
                dve.wait_ge(S(f"map_got{b}"), i * 16 + 16)
                if not first:
                    dve.wait_ge(S(f"map_stored{b}"), i * 32)
                vec.tensor_scalar(rel, got[:, 1, :], MP["blk"][:, bass.ds(i * 2 + b, 1)], None, ALU.subtract).then_inc(S("map_rel"), 1)
                dve.wait_ge(S("map_rel"), i * 2 + b + 1)
                vec.scalar_tensor_tensor(end, rel, 1.0, got[:, 3, :], ALU.add, ALU.mult).then_inc(S("map_end"), 1)
                vec.tensor_copy(MP["mask16"][:, b, :], got[:, 2, :])
                vec.tensor_copy(MP["rel16"][:, b, :], rel)
                dve.wait_ge(S("map_end"), i * 2 + b + 1)
                vec.tensor_scalar(end, end, 1.0, None, ALU.subtract).then_inc(S("map_rows"), 1)
                dve.wait_ge(S("map_turned"), i * 2 + b + 1)
                if not last:
                    vec.tensor_copy(MP["cur"][:, b, :], MP["st_idx"][:, 0, bass.ds(i * 2 + b + 2, 1)]).then_inc(S("map_idx"), 1)
            for b in range(2):
                map_chunk(0, b, True, False)
            with dve.Fori(1, MAP_CHUNKS // 2 - 1) as i:
                for b in range(2):
                    map_chunk(i, b, False, False)
            for b in range(2):
                map_chunk(MAP_CHUNKS // 2 - 1, b, False, True)

            for b in range(2):
                dve.wait_ge(S(f"map_stored{b}"), 16 * MAP_CHUNKS)
            for c in range(GROUP_CHUNKS):
                ins = vec.tensor_scalar(GRP["node0"][:, c:c + 1], iota_p[:, :], float(GROUP), float(c * PART * GROUP), ALU.mult, ALU.add)
            link(ins)
            link(vec.tensor_scalar(GRP["node4"][:, :], GRP["node0"][:, :], float(GROUP), None, ALU.add))
            with dve.Fori(0, GROUP_CHUNKS) as c:
                vec.tensor_scalar(junk[:, 0:TILES], big[:, 0:TILES], GRP["node0"][:, bass.ds(c, 1)], 0.0, ALU.is_lt, ALU.add,
                                  accum_out=GRP["tile"][:, bass.ds(c, 1)]).then_inc(S("group_tile"), 1)
                dve.wait_ge(S("group_tile"), c + 1)
            link(vec.tensor_scalar(GRP["tile"][:, :], GRP["tile"][:, :], 1.0, 0.0, ALU.subtract, ALU.max))
            link(vec.tensor_copy(GRP["tile_i"][:, :], GRP["tile"][:, :]))

            def next_index(name, store, col, b):
                vec.tensor_copy(GRP["cur"][:, b, :], store[:, col]).then_inc(S(f"{name}_idx"), 1)

            def tile_chunk(i, b, last):
                c = i * 2 + b
                dve.wait_ge(S(f"gtile_got{b}"), i * 16 + 16)
                vec.tensor_scalar(GRP["below"][:, :], GRP["dst"][:, b, :], GRP["node0"][:, bass.ds(c, 1)], 0.0, ALU.is_lt, ALU.add,
                                  accum_out=GRP["inside"][:, bass.ds(c, 1)]).then_inc(S("group_inside"), 1)
                dve.wait_ge(S("group_inside"), c + 1)
                if not last:
                    next_index("gtile", GRP["tile_i"], bass.ds(c + 2, 1), b)

            def two_ahead(chunk, *args):
                with dve.Fori(0, GROUP_CHUNKS // 2 - 1) as i:
                    for b in range(2):
                        chunk(i, b, False)
                for b in range(2):
                    chunk(GROUP_CHUNKS // 2 - 1, b, True)

            for b in range(2):
                next_index("gtile", GRP["tile_i"], slice(b, b + 1), b)
            two_ahead(tile_chunk)
            link(vec.scalar_tensor_tensor(GRP["tile"][:, :], GRP["tile"][:, :], float(PART), GRP["inside"][:, :], ALU.mult, ALU.add))
            link(vec.tensor_copy(GRP["tile_i"][:, :], GRP["tile"][:, :]))
            link(vec.tensor_scalar(GRP["win_i"][:, :], GRP["tile_i"][:, :], WIN_STEP.bit_length() - 1, None, ALU.logical_shift_right))

            def window_chunk(i, b, last):
                c = i * 2 + b
                dve.wait_ge(S(f"gwin_got{b}"), i * 16 + 16)
                dst, src = GRP["win"][:, b, 0, :], GRP["win"][:, b, 1, :]
                col = bass.ds(c, 1)
                steps = [
                    lambda: vec.tensor_scalar(GRP["node"][:, :], dst, GRP["node0"][:, col], None, ALU.subtract),
                    lambda: vec.tensor_scalar(GRP["ok"][:, :], GRP["node"][:, :], 0.0, None, ALU.is_ge),
                    lambda: vec.scalar_tensor_tensor(GRP["ok"][:, :], GRP["node"][:, :], float(GROUP), GRP["ok"][:, :], ALU.is_lt, ALU.mult),
                    lambda: vec.tensor_scalar(GRP["sblk"][:, :], src, PART.bit_length() - 1, None, ALU.logical_shift_right),
                    lambda: vec.tensor_scalar(GRP["slow"][:, :], src, PART - 1, None, ALU.bitwise_and),
                    lambda: vec.scalar_tensor_tensor(GRP["node"][:, :], GRP["sblk"][:, :], float(GROUP), GRP["node"][:, :], ALU.mult, ALU.add),
                    lambda: vec.scalar_tensor_tensor(GRP["hot"][:, b, :], GRP["node"][:, :], 1.0, GRP["ok"][:, :], ALU.add, ALU.mult),
                    lambda: vec.tensor_scalar(GRP["bad"][:, col], dst[:, WINDOW - 1:WINDOW], GRP["node4"][:, col], None, ALU.is_lt),
                    lambda: vec.tensor_scalar(GRP["low"][:, b, :], GRP["slow"][:, :], 1.0, None, ALU.add)]
                for k, step in enumerate(steps):
                    step().then_inc(S("group_step"), 1)
                    dve.wait_ge(S("group_step"), c * len(steps) + k + 1)
                dve.sem_inc(S("group_rows"), 1)
                dve.wait_ge(S("gturned"), c + 1)
                if not last:
                    next_index("gwin", GRP["win_i"], bass.ds(c + 2, 1), b)

            for b in range(2):
                next_index("gwin", GRP["win_i"], slice(b, b + 1), b)
            two_ahead(window_chunk)
            vec.tensor_reduce(GRP["sum"][:, :], GRP["bad"][:, :], AX, ALU.add).then_inc(S("bad_sum"), 1)
            dve.wait_ge(S("bad_total"), 1)
            link(vec.tensor_copy(bad_row[0:1, 0:1], ps[0:1, 0, 0:1]))
            dve.sem_inc(S("bad_known"), 1)

            def centred(layer):
                link(vec.tensor_reduce(small[:, 0, :], x_sb[:, :, :], AX, ALU.add))
                link(vec.tensor_scalar(small[:, 0, :], small[:, 0, :], 1.0 / D, None, ALU.mult))
                link(vec.tensor_tensor(h_sb[:, :, :], x_sb[:, :, :], broadcast(small[:, 0, :], [PART, BLOCKS, D]), ALU.subtract))
                link(vec.tensor_tensor(squares, h_sb[:, :, :], h_sb[:, :, :], ALU.mult))
                vec.tensor_reduce(small[:, 1, :], squares, AX, ALU.add).then_inc(S("variance"), 1)
                dve.wait_ge(S("deviation"), NORMS.index(layer) + 1)
                link(vec.reciprocal(small[:, 3, :], small[:, 2, :]))

            def normed(out_ap, g0, n):
                return vec.scalar_tensor_tensor(out_ap, h_sb[:, bass.ds(g0, n), :], 0.0,
                                                broadcast(small[:, 3, bass.ds(g0, n)], [PART, n, D]), ALU.max, ALU.mult)

            def clear(layer, width, turn=0):
                vec.memset(big[:, 0:(BLOCKS + 1) * width], 0.0).then_inc(S(f"{layer}_cleared"), 1)
                dve.wait_ge(S(f"{layer}_cleared"), turn + 1)

            def blocks_of(i, s):
                _, got = nc.values_load_multi_w_load_instructions(
                    block_row[:, bass.ds(i * UNROLL + s * SLOT, SLOT)], engines=[dve.engine], min_val=0, max_val=BLOCKS)
                return got

            def one_hot(out_ap, source, i, s):
                for k in range(SLOT):
                    ins = vec.tensor_scalar(out_ap[:, k, :], iota_f[:, :], source[:, bass.ds(i * UNROLL + s * SLOT + k, 1)],
                                            None, ALU.is_equal)
                return ins

            def add_up(layer, width, i, s, bank, m):
                got = blocks_of(i, s)
                for k in range(SLOT):
                    target = acc(width)[:, bass.ds(got[k], 1), :].rearrange("p o f -> p (o f)")
                    vec.tensor_tensor(target, target, bank[:, k * width:(k + 1) * width], ALU.add).then_inc(S(f"{layer}_added"), 1)
                    dve.wait_ge(S(f"{layer}_added"), m * SLOT + k + 1)

            dve.wait_ge(S("x_loaded"), 32)
            dve.wait_ge(S("weights"), 16 * 21)
            link(vec.tensor_tensor(w_pq[0:D, 0:D], w_pq[0:D, 0:D], w_pq[0:D, D:2 * D], ALU.subtract))
            dve.wait_ge(S("group_done"), GROUP_CHUNKS)
            vec.memset(L0["hT"][D:D + 1, :], 1.0)
            centred("l0")
            vec.memset(p_split[:, BLOCKS, :, :], 0.0)
            with dve.Fori(0, CHUNKS) as c:
                normed(L0["hc"][:, :, :], c * CH, CH).then_inc(S("l0_h"), 1)
                dve.wait_ge(S("q_staged"), c + 1)
                p = ps[:, 2:4, :].rearrange("p b (g f) -> p (b g) f", f=2 * D)[:, 0:CH, 0:D]
                pieces = [p_split[:, bass.ds(c * CH, CH), k, :] for k in range(3)]
                steps = [lambda: vec.tensor_copy(pieces[0], p),
                         lambda: vec.tensor_tensor(L0["pres"][:, :, :], p, pieces[0], ALU.subtract),
                         lambda: vec.tensor_copy(pieces[1], L0["pres"][:, :, :]),
                         lambda: vec.tensor_tensor(pieces[2], L0["pres"][:, :, :], pieces[1], ALU.subtract)]
                for k, step in enumerate(steps):
                    step().then_inc(S("l0_piece"), 1)
                    dve.wait_ge(S("l0_piece"), c * len(steps) + k + 1)
            clear("l0", D)
            dve.wait_ge(S("q_stored"), 16 * CHUNKS)
            vec.memset(L0E["pre"][D:D + 1, :, :], 1.0)
            link(vec.memset(L0E["scan"][:, :, :], -BIG))

            def ohT0(n, s, i):
                dve.wait_ge(S(f"l0_rel{s}"), i * 16 + 16)
                if not isinstance(n, int) or n >= 2:
                    dve.wait_ge(S("l0_pre"), n - 1)
                vec.tensor_scalar(L0E["ohT"][:, s % 2, :], L0E["rel"][:, s, :], iota_p[:, :], None, ALU.is_equal).then_inc(S("l0_ohT"), 1)

            def scan0(m, s, i):
                dve.wait_ge(S("l0_msg"), m + 1)
                dve.wait_ge(S(f"l0_mask{s}"), i * 16 + 16)
                if not isinstance(m, int) or m >= 2:
                    dve.wait_ge(S("l0_turn"), m - 1)
                if not isinstance(m, int) or m >= 1:
                    dve.wait_ge(S("l0_scan"), m)
                vec.tensor_tensor_scan(L0E["scan"][:, s % 2, :], L0E["mask"][:, s, :], ps[0:D, 1, :],
                                       L0E["scan"][:, (s + 1) % 2, SLOT_E - 1:SLOT_E], ALU.min, ALU.max).then_inc(S("l0_scan"), 1)

            def ends0(m, s, i):
                if not isinstance(m, int) or m >= 2:
                    dve.wait_ge(S("l0_ends"), m - 1)
                one_hot(L0E["oh"][:, s % 2, :, :], end_st, i, s).then_inc(S("l0_oh"), 1)

            def add0(m, s, i):
                dve.wait_ge(S("l0_ends"), m + 1)
                add_up("l0", D, i, s, ps[:, 3, :], m)

            def hot0(i, s, pair):
                n1 = i * SLOTS + s + 1
                if not isinstance(n1, int) or n1 >= 1:
                    dve.wait_ge(S("l0_built"), n1 * 2 - 1 + pair)
                for g in (2 * pair, 2 * pair + 1):
                    for h in range(2):
                        col = bass.ds((i * SLOTS + s + 1) * 8 + 2 * g + h, 1)
                        vec.tensor_scalar(ADJ["oh_low"][:, g, h, :], iota_hot[:, 0:PART], ADJ["low"][:, col], None, ALU.is_equal)
                        ins = vec.tensor_scalar(ADJ["oh_hot"][:, g, h, :], iota_hot[:, :], ADJ["hot"][:, col], None, ALU.is_equal)
                ins.then_inc(S("l0_hot"), 1)

            def staged(work, i, s, lag):
                m = i * SLOTS + (s - lag)
                if not isinstance(m, int) or 0 <= m < ITERS * SLOTS:
                    work(m, (s - lag) % SLOTS, i + (s - lag) // SLOTS)

            def slot0(i, s):
                staged(ohT0, i, s, -1)
                staged(add0, i, s, 4)
                staged(ends0, i, s, 2)
                hot0(i, s, 0)
                staged(scan0, i, s, 1)
                hot0(i, s, 1)

            ohT0(0, 0, 0)
            hot0(0, -1, 0)
            hot0(0, -1, 1)
            for s in range(SLOTS):
                slot0(0, s)
            with dve.Fori(1, ITERS) as i:
                for s in range(SLOTS):
                    slot0(i, s)
            for s in range(4):
                staged(add0, ITERS, s, 4)
                staged(ends0, ITERS, s, 2)
                staged(scan0, ITERS, s, 1)
            dve.wait_ge(S("adj_stored"), 2 * 16 * ADJ_BLOCKS)
            vec.memset(x_sb[:, BLOCKS - 1, :], 0.0).then_inc(S("x_cleared"), 1)
            dve.wait_ge(S("x_back"), 32)
            dve.wait_ge(S("l0_mask0"), 16 * (ITERS + 1))
            link(vec.tensor_tensor(x_sb[:, :, :], x_sb[:, :, :], acc(D)[:, 0:BLOCKS, :], ALU.add))

            def sums(layer, width):
                done = DENSE[layer] * ITERS * SLOTS
                clear("sum", width, DENSE[layer])
                for s in range(SLOTS):
                    one_hot(SUM["oh"][:, s, :, :], rel_st, 0, s).then_inc(S("sum_oh"), 1)
                with dve.Fori(0, ITERS) as i:
                    for s in range(SLOTS):
                        dve.wait_ge(S("sum_sum"), i * SLOTS + (done + s + 1))
                        add_up("sum", width, i, s, ps[:, s, :], i * SLOTS + (done + s))
                        one_hot(SUM["oh"][:, s, :, :], rel_st, i + 1, s).then_inc(S("sum_oh"), 1)

            def pieces_of(width, g, value, spare, count):
                t = split(width, BLOCKS)
                piece = [t[:, g, k, 0:D] for k in range(3)]
                for k, step in enumerate((
                        lambda: vec.tensor_copy(piece[0], value),
                        lambda: vec.tensor_tensor(spare, value, piece[0], ALU.subtract),
                        lambda: vec.tensor_copy(piece[1], spare),
                        lambda: vec.tensor_tensor(piece[2], spare, piece[1], ALU.subtract))):
                    step().then_inc(S("piece"), 1)
                    dve.wait_ge(S("piece"), count * 4 + k + 1)

            def block_sums(layer, width):
                with dve.Fori(0, HALF_B) as i:
                    for b in range(2):
                        dve.wait_ge(S("adj_used"), i * 4 + (DENSE[layer] * 2 * BLOCKS + 2 * b + 2))
                        vec.tensor_reduce(acc(width)[:, bass.ds(i * 2 + b, 1), :].rearrange("p o f -> p (o f)"),
                                          ps[:, b, 0:3 * width].rearrange("p (k f) -> p f k", k=3), AX, ALU.add
                                          ).then_inc(S("adj_summed"), 1)
                dve.wait_ge(S("adj_summed"), (DENSE[layer] + 1) * BLOCKS)

            bad = bad_groups(dve)
            centred("l1a")
            link(normed(h_sb[:, :, :], 0, BLOCKS))
            ones = split(D + 1, BLOCKS)
            vec.memset(ones[:, :, 0, D:D + 1], 1.0)
            vec.memset(ones[:, :, 1:3, D:D + 1], 0.0)
            pieces_of(D + 1, slice(0, BLOCKS), h_sb[:, :, :], squares, 0)
            dve.sem_inc(S("l1a_h"), 1)
            with dve.If(bad == 0):
                block_sums("l1a", D + 1)
            with dve.Else():
                sums("l1a", D + 1)
            sums1 = acc(D + 1)
            degrees = sums1[:, 0:BLOCKS, D:D + 1].rearrange("p g o -> p (g o)")
            link(vec.tensor_scalar(deg_inv[:, :], degrees, 1.0, None, ALU.max))
            vec.tensor_scalar(has_edge[:, :], degrees, 1.0, None, ALU.min)
            link(vec.reciprocal(deg_inv[:, :], deg_inv[:, :]))
            with dve.Fori(0, CHUNKS) as c:
                vec.tensor_tensor(L1["cat"][:, :, 0:D], sums1[:, bass.ds(c * CH, CH), 0:D],
                                  broadcast(deg_inv[:, bass.ds(c * CH, CH)], [PART, CH, D]), ALU.mult)
                vec.tensor_copy(L1["cat"][:, :, D:2 * D], h_sb[:, bass.ds(c * CH, CH), :]).then_inc(S("l1_nodes"), 1)
                dve.wait_ge(S("z_staged"), c + 1)
                zy = ps[:, 4:6, :].rearrange("p b (g f) -> p (b g) f", f=2 * D)
                pieces_of(D, bass.ds(c * CH, CH), zy[:, 0:CH, 0:D], L1["spare"][:, :, :], c + 1)
                vec.tensor_tensor(h_sb[:, bass.ds(c * CH, CH), :],
                                  ps[:, 4:6, :].rearrange("p b (g f) -> p (b g) f", f=2 * D)[:, 0:CH, D:2 * D],
                                  b2_row[:, :].unsqueeze(1).to_broadcast([PART, CH, D]), ALU.add).then_inc(S("l1_y"), 1)
                dve.wait_ge(S("l1_y"), c + 1)
            dve.wait_ge(S("z_stored"), 16 * CHUNKS)
            dve.sem_inc(S("l1b_nodes"), 1)
            with dve.If(bad == 0):
                block_sums("l1b", D)
            with dve.Else():
                sums("l1b", D)
            link(vec.tensor_tensor(h_sb[:, :, :], h_sb[:, :, :], x_sb[:, :, :], ALU.add))
            link(vec.tensor_tensor(x_sb[:, :, :], acc(D)[:, 0:BLOCKS, :], broadcast(deg_inv[:, :], [PART, BLOCKS, D]), ALU.mult))
            link(vec.tensor_tensor(x_sb[:, :, :], x_sb[:, :, :], h_sb[:, :, :], ALU.add))

            centred("l2")
            link(normed(h_sb[:, :, :], 0, BLOCKS))
            vec.memset(L2R["hT"][D:D + 1, :], 1.0)
            with dve.Fori(0, CHUNKS) as c:
                vec.tensor_copy(L2R["hc"][:, :, :], h_sb[:, bass.ds(c * CH, CH), :]).then_inc(S("l2_h"), 1)
                dve.wait_ge(S("l2_hT"), c + 1)
            clear("l2", HID)
            dve.wait_ge(S("r_staged"), CHUNKS)
            dve.wait_ge(S("r_stored"), 16 * CHUNKS)
            for s in range(SLOTS):
                one_hot(L2E["oh"][:, s, :, :], rel_st, 0, s).then_inc(S("l2_oh"), 1)
            with dve.Fori(0, ITERS) as i:
                for s in range(SLOTS):
                    dve.wait_ge(S("l2_sum"), i * SLOTS + s + 1)
                    add_up("l2", HID, i, s, ps[:, 2 + s % 2, :], i * SLOTS + s)
                    one_hot(L2E["oh"][:, s, :, :], rel_st, i + 1, s).then_inc(S("l2_oh"), 1)
            with dve.Fori(0, CHUNKS) as c:
                g = bass.ds(c * CH, CH)
                vec.tensor_tensor(L2P["m"][:, :, :], acc(HID)[:, g, :], broadcast(deg_inv[:, g], [PART, CH, HID]), ALU.mult)
                vec.tensor_copy(L2P["hi"][:, :, 0:D], h_sb[:, g, :])
                vec.tensor_copy(L2P["hi"][:, :, D:D + 1], has_edge[:, g].unsqueeze(2)).then_inc(S("l2_nodes"), 1)
                dve.wait_ge(S("l2_out"), c + 1)
                y = ps[:, 0, 0:CH * D].rearrange("p (g f) -> p g f", f=D)
                vec.tensor_tensor(x_sb[:, g, :], x_sb[:, g, :], y, ALU.add).then_inc(S("l2_x"), 1)
                dve.wait_ge(S("l2_x"), c + 1)
            link(vec.tensor_tensor(x_sb[:, :, :], x_sb[:, :, :], b4_row[:, :].unsqueeze(1).to_broadcast([PART, BLOCKS, D]), ALU.add))

            centred("l3")
            link(normed(h_sb[:, :, :], 0, BLOCKS))
            pieces_of(D, slice(0, BLOCKS), h_sb[:, :, :], squares, 1 + CHUNKS)
            dve.sem_inc(S("l3_h"), 1)
            with dve.If(bad == 0):
                block_sums("l3", D)
            with dve.Else():
                sums("l3", D)
            link(vec.tensor_tensor(x_sb[:, :, :], x_sb[:, :, :], acc(D)[:, 0:BLOCKS, :], ALU.add))
            dve.sem_inc(S("result"), 1)

        @block.tensor
        def _(pe):
            mm = nc.tensor.matmul
            pe.wait_ge(S("w_zeroed"), 1)
            pe.wait_ge(S("consts"), 1)
            pe.wait_ge(S("block_steps"), 1)
            mm(ps[:, 0, 0:1], MP["tri"][:, 0, :], MP["cols"][:, 4:5], start=True, stop=True).then_inc(S("block_begin"), 1)
            pe.wait_ge(S("block_shift"), 1)
            mm(ps[:, 0, 1:2], MP["tri"][:, 1, :], MP["cols"][:, 6:7], start=True, stop=True).then_inc(S("block_delta"), 1)
            pe.wait_ge(S("block_begun"), 1)
            begun = big[:, 2 * TILES + MAPPED:2 * TILES + 2 * MAPPED]
            for m in range(MAP_MMS):
                cols = slice(m * MAP_COLS, (m + 1) * MAP_COLS)
                if m >= 2:
                    pe.wait_ge(S("steps_read"), m - 1)
                mm(ps[0:1, 2 * (m % 2), 0:MAP_COLS], MP["cols"][:, 7:8], begun[:, cols], start=True, stop=True)
                mm(ps[0:1, 2 * (m % 2) + 1, 0:MAP_COLS], ones_col, begun[:, cols], start=True, stop=True).then_inc(S("steps_summed"), 1)
            pe.wait_ge(S("steps_read"), MAP_MMS)

            def map_chunk(i, b, first):
                pe.wait_ge(S("map_rows"), i * 2 + b + 1)
                if not first:
                    pe.wait_ge(S("map_done"), i * 2 + b - 1)
                for k, edges in enumerate((MP["got"][:, b, 0, :], MP["rel"][:, b, :], MP["end"][:, b, :])):
                    ins = nc.tensor.transpose(ps[:, b, k * PART:(k + 1) * PART], edges, ident[:, :])
                ins.then_inc(S("map_turned"), 1)
            for b in range(2):
                map_chunk(0, b, True)
            with pe.Fori(1, MAP_CHUNKS // 2) as i:
                for b in range(2):
                    map_chunk(i, b, False)
            pe.wait_ge(S("map_done"), MAP_CHUNKS)

            def group_chunk(i, b, first):
                pe.wait_ge(S("group_rows"), i * 2 + b + 1)
                if not first:
                    pe.wait_ge(S("group_done"), i * 2 + b - 1)
                for k, edges in enumerate((GRP["hot"][:, b, :], GRP["low"][:, b, :])):
                    for h in range(2):
                        ins = nc.tensor.transpose(ps[:, b, (2 * k + h) * PART:(2 * k + h + 1) * PART],
                                                  edges[:, h * PART:(h + 1) * PART], ident[:, :])
                ins.then_inc(S("gturned"), 1)
            for b in range(2):
                group_chunk(0, b, True)
            with pe.Fori(1, GROUP_CHUNKS // 2) as i:
                for b in range(2):
                    group_chunk(i, b, False)
            pe.wait_ge(S("group_done"), GROUP_CHUNKS)
            pe.wait_ge(S("bad_sum"), 1)
            mm(ps[0:1, 0, 0:1], GRP["sum"][:, :], ones_col, start=True, stop=True).then_inc(S("bad_total"), 1)
            pe.wait_ge(S("bad_known"), 1)

            turned = lambda rows_, b0, k: ps[0:rows_, b0 + k // 4, (k % 4) * PART:(k % 4 + 1) * PART]

            with pe.Fori(0, CHUNKS) as c:
                pe.wait_ge(S("l0_h"), c + 1)
                pe.sem_inc(S("pe_begun"), 1)
                for k in range(CH):
                    ins = nc.tensor.transpose(turned(D, 0, k), L0["hc"][:, k, :], ident[:, :])
                ins.then_inc(S("l0_hT"), 1)
                pe.wait_ge(S("l0_hT_out"), c + 1)
                for k in range(CH):
                    ins = mm(turned(PART, 2, k), L0["hT"][:, k * PART:(k + 1) * PART], w_pq[:, :], start=True, stop=True)
                ins.then_inc(S("l0_pq"), 1)
            pe.wait_ge(S("l0_piece"), 4 * CHUNKS)
            pe.wait_ge(S("q_staged"), CHUNKS)

            def pre0(n, s, i):
                _, got = nc.values_load_multi_w_load_instructions(
                    block_row[:, bass.ds(i * UNROLL + s * SLOT, SLOT)], engines=[pe.engine], min_val=0, max_val=BLOCKS)
                pe.wait_ge(S(f"l0_rows{s}"), i * (16 * SLOT) + 16 * SLOT)
                pe.wait_ge(S("l0_ohT"), n + 1)
                if not isinstance(n, int) or n >= 1:
                    pe.wait_ge(S("l0_relu"), n)
                for k in range(SLOT):
                    target = ps[0:D, 0, k * PART:(k + 1) * PART]
                    ins = mm(target, rows[:, s, k, 0:D], ident[:, :], start=True, stop=False)
                    for piece in range(3):
                        ins = mm(target, p_split[:, bass.ds(got[k], 1), piece, :].rearrange("p o f -> p (o f)"),
                                 L0E["ohT"][:, s % 2, k * PART:(k + 1) * PART], start=False, stop=piece == 2)
                ins.then_inc(S("l0_pre"), 1)

            def msg0(m, s, i):
                pe.wait_ge(S("l0_relu"), m + 1)
                if not isinstance(m, int) or m >= 1:
                    pe.wait_ge(S("l0_scan"), m)
                mm(ps[0:D, 1, :], w_msg[:, :], L0E["pre"][:, s % 2, :], start=True, stop=True).then_inc(S("l0_msg"), 1)

            def turn0(m, s, i):
                pe.wait_ge(S("l0_scan"), m + 1)
                if not isinstance(m, int) or m >= 1:
                    pe.wait_ge(S("l0_turned"), m)
                pe.sem_inc(S("pe_begun"), 1)
                for k in range(SLOT):
                    ins = nc.tensor.transpose(ps[:, 2, k * D:(k + 1) * D],
                                              L0E["scan"][:, s % 2, k * PART:(k + 1) * PART], ident[0:D, 0:D])
                ins.then_inc(S("l0_turn"), 1)

            def ends0(m, s, i):
                pe.wait_ge(S("l0_turned"), m + 1)
                pe.wait_ge(S("l0_oh"), m + 1)
                if not isinstance(m, int) or m >= 1:
                    pe.wait_ge(S("l0_added"), m * SLOT)
                for k in range(SLOT):
                    ins = mm(ps[:, 3, k * D:(k + 1) * D], L0E["oh"][:, s % 2, k, :], L0E["scanT"][:, s % 2, k, :],
                             start=True, stop=True)
                ins.then_inc(S("l0_ends"), 1)

            def build0(i, s, pair):
                n = i * SLOTS + s
                pe.wait_ge(S("l0_hot"), n * 2 + pair + 1)
                if not isinstance(n, int) or n >= 1:
                    pe.wait_ge(S("l0_evac"), n * 2 - 1 + pair)
                for g in (2 * pair, 2 * pair + 1):
                    for h in range(2):
                        ins = mm(ps[:, 4 + g, 0:HOT], ADJ["oh_low"][:, g, h, :], ADJ["oh_hot"][:, g, h, :],
                                 start=h == 0, stop=h == 1)
                ins.then_inc(S("l0_built"), 1)

            def staged(work, i, s, lag):
                m = i * SLOTS + (s - lag)
                if not isinstance(m, int) or 0 <= m < ITERS * SLOTS:
                    work(m, (s - lag) % SLOTS, i + (s - lag) // SLOTS)

            def slot0(i, s):
                build0(i, s, 0)
                pre0(i * SLOTS + s, s, i)
                build0(i, s, 1)
                staged(msg0, i, s, 1)
                staged(turn0, i, s, 2)
                staged(ends0, i, s, 3)

            for s in range(SLOTS):
                slot0(0, s)
            with pe.Fori(1, ITERS) as i:
                for s in range(SLOTS):
                    slot0(i, s)
            for s in range(3):
                for lag, work in ((1, msg0), (2, turn0), (3, ends0)):
                    staged(work, ITERS, s, lag)

            def sums(layer, width):
                turn = DENSE[layer]
                with pe.Fori(0, ITERS) as i:
                    for s in range(SLOTS):
                        pe.wait_ge(S(f"sum_rows{s}"), i * (16 * SLOT) + 16 * SLOT * (turn * ITERS + 1))
                        pe.wait_ge(S("sum_oh"), i * SLOTS + (turn * (ITERS + 1) * SLOTS + s + 1))
                        for k in range(SLOT):
                            ins = mm(ps[:, s, k * width:(k + 1) * width], SUM["oh"][:, s, k, :], rows[:, s, k, 0:width],
                                     start=True, stop=True)
                        ins.then_inc(S("sum_sum"), 1)

            def block_sums(layer, width):
                t = split(width, BLOCKS)

                def half(i, k, first):
                    pe.wait_ge(S(f"adj_half{k}"), i * 16 + (DENSE[layer] * HALF_B * 16 + 16))
                    if k % 2 == 0 and not first:
                        pe.wait_ge(S("adj_summed"), i * 2 + (DENSE[layer] * BLOCKS + k // 2 - 1))
                    for h in range(HALF_B):
                        source = (k % 2) * HALF_B + h
                        ins = mm(ps[:, k // 2, 0:3 * width], RING["adj"][:, k, h, :],
                                 t[:, source, :, :].rearrange("p k f -> p (k f)"),
                                 start=source == 0, stop=source == BLOCKS - 1)
                    ins.then_inc(S("adj_used"), 1)
                for k in range(4):
                    half(0, k, True)
                with pe.Fori(1, HALF_B) as i:
                    for k in range(4):
                        half(i, k, False)

            bad = bad_groups(pe)
            pe.wait_ge(S("l1a_h"), 1)
            with pe.If(bad == 0):
                block_sums("l1a", D + 1)
            with pe.Else():
                sums("l1a", D + 1)
                pe.wait_ge(S("sum_added"), STEPS)
            with pe.Fori(0, CHUNKS) as c:
                pe.wait_ge(S("l1_nodes"), c + 1)
                for k in range(CH):
                    ins = nc.tensor.transpose(turned(PART, 0, k), L1["cat"][:, k, :], ident[:, :])
                ins.then_inc(S("l1_cat"), 1)
                pe.wait_ge(S("l1_catT"), c + 1)
                for b in range(2):
                    ins = mm(ps[:, 2 + b, 0:CH_N // 2], w1_cat[:, :], L1["catT"][:, b * CH_N // 2:(b + 1) * CH_N // 2],
                             start=True, stop=True)
                ins.then_inc(S("l1_hid"), 1)
                pe.wait_ge(S("l1_h1T"), c + 1)
                for k in range(CH):
                    ins = mm(turned(PART, 4, k), L1["h1T"][:, k * PART:(k + 1) * PART], w2_cat[:, :], start=True, stop=True)
                ins.then_inc(S("l1_zy"), 1)
            pe.wait_ge(S("z_staged"), CHUNKS)
            pe.wait_ge(S("l1b_nodes"), 1)
            with pe.If(bad == 0):
                block_sums("l1b", D)
            with pe.Else():
                sums("l1b", D)
                pe.wait_ge(S("sum_added"), 2 * STEPS)

            with pe.Fori(0, CHUNKS) as c:
                pe.wait_ge(S("l2_h"), c + 1)
                pe.sem_inc(S("pe_begun"), 1)
                for k in range(CH):
                    ins = nc.tensor.transpose(turned(D, 0, k), L2R["hc"][:, k, :], ident[:, :])
                ins.then_inc(S("l2_hT"), 1)
                pe.wait_ge(S("l2_hT_out"), c + 1)
                for k in range(CH):
                    ins = mm(turned(PART, 2, k), L2R["hT"][:, k * PART:(k + 1) * PART], w_r[:, :], start=True, stop=True)
                ins.then_inc(S("l2_r"), 1)
            pe.wait_ge(S("r_staged"), CHUNKS)

            def pre2(n, s, i):
                pe.wait_ge(S(f"l2_ea{s}"), i * (16 * SLOT) + 16 * SLOT)
                pe.wait_ge(S(f"l2_rows{s}"), i * (16 * SLOT) + 16 * SLOT)
                if not isinstance(n, int) or n >= 2:
                    pe.wait_ge(S("l2_relu"), n - 1)
                for k in range(SLOT):
                    ins = mm(ps[:, s % 2, k * HID:(k + 1) * HID], L2E["ea"][:, s, k, :], w_e[:, :], start=True, stop=False)
                    ins = mm(ps[:, s % 2, k * HID:(k + 1) * HID], ident[:, :], rows[:, s, k, :], start=False, stop=True)
                ins.then_inc(S("l2_pre"), 1)

            def sum2(m, s, i):
                pe.wait_ge(S("l2_relu"), m + 1)
                pe.wait_ge(S("l2_oh"), m + 1)
                if not isinstance(m, int) or m >= 2:
                    pe.wait_ge(S("l2_added"), (m - 1) * SLOT)
                for k in range(SLOT):
                    ins = mm(ps[:, 2 + s % 2, k * HID:(k + 1) * HID], L2E["oh"][:, s, k, :], L2E["act"][:, s % 2, k, :],
                             start=True, stop=True)
                ins.then_inc(S("l2_sum"), 1)

            def slot2(i, s):
                for lag, work in ((0, pre2), (1, sum2)):
                    sl, it = (s - lag) % SLOTS, i + (-1 if s < lag else 0)
                    m = i * SLOTS + (s - lag)
                    if isinstance(m, int) and not 0 <= m < ITERS * SLOTS:
                        continue
                    work(m, sl, it)
            for s in range(SLOTS):
                slot2(0, s)
            with pe.Fori(1, ITERS) as i:
                for s in range(SLOTS):
                    slot2(i, s)
            slot2(ITERS, 0)
            pe.wait_ge(S("l2_added"), STEPS)
            with pe.Fori(0, CHUNKS) as c:
                pe.wait_ge(S("l2_nodes"), c + 1)
                for k in range(CH):
                    nc.tensor.transpose(turned(PART, 0, k), L2P["m"][:, k, :], ident[:, :])
                for k in range(CH):
                    ins = nc.tensor.transpose(turned(D + 1, 2, k), L2P["hi"][:, k, :], ident[:, :])
                ins.then_inc(S("l2_mT"), 1)
                pe.wait_ge(S("l2_mT_out"), c + 1)
                for b in range(2):
                    half = slice(b * CH_N // 2, (b + 1) * CH_N // 2)
                    mm(ps[0:D, 4 + b, 0:CH_N // 2], w_agg[:, :], L2P["mT"][:, half], start=True, stop=False)
                    ins = mm(ps[0:D, 4 + b, 0:CH_N // 2], b_agg[:, :], L2P["hT"][:, half], start=False, stop=True)
                ins.then_inc(S("l2_agg"), 1)
                pe.wait_ge(S("l2_aT"), c + 1)
                for b in range(2):
                    half = slice(b * CH_N // 2, (b + 1) * CH_N // 2)
                    mm(ps[:, 6 + b, 0:CH_N // 2], w3_h[:, :], L2P["hT"][0:D, half], start=True, stop=False)
                    ins = mm(ps[:, 6 + b, 0:CH_N // 2], w3_a[:, :], L2P["aT"][:, half], start=False, stop=True)
                ins.then_inc(S("l2_g"), 1)
                pe.wait_ge(S("l2_gT"), c + 1)
                for k in range(CH):
                    ins = mm(ps[:, 0, k * D:(k + 1) * D], L2P["gT"][:, k * PART:(k + 1) * PART], w4[:, :], start=True, stop=True)
                ins.then_inc(S("l2_out"), 1)
            pe.wait_ge(S("l3_h"), 1)
            with pe.If(bad == 0):
                block_sums("l3", D)
            with pe.Else():
                sums("l3", D)


_INS = ["x", "src", "dst", "L0_gnn_W1", "L0_gnn_b1", "L0_gnn_W2", "L0_gnn_b2", "L1_gnn_W1_l", "L1_gnn_b1", "L1_gnn_W1_r",
        "L1_gnn_W2_l", "L1_gnn_b2", "L1_gnn_W2_r", "L2_gnn_W1", "L2_gnn_b1", "L2_gnn_W2", "L2_gnn_b2", "L2_gnn_W3", "L2_gnn_b3",
        "L2_gnn_W4", "L2_gnn_b4"]


def kernel(**inputs):
    import concourse.bacc as bacc
    from concourse.bass_utils import run_bass_kernel_spmd

    nc = bacc.Bacc("TRN2", target_bir_lowering=False, num_devices=1)
    arrays = {name: np.ascontiguousarray(inputs[name]) for name in _INS}
    arrays["edge_attr_T"] = np.ascontiguousarray(
        np.asarray(inputs["edge_attr_32"]).reshape(TILES, PART, DE).transpose(0, 2, 1))
    aps = {name: nc.dram_tensor(name, a.shape, mybir.dt.from_np(a.dtype), kind="ExternalInput").ap()
           for name, a in arrays.items()}
    out = nc.dram_tensor("out", (NODES, D), F32, kind="ExternalOutput").ap()
    gnn_kernel(nc, aps, out)
    result = run_bass_kernel_spmd(nc, [arrays], core_ids=[0])
    return result.results[0]["out"]
```

```python
import numpy as np
import concourse.bass as bass
from concourse import mybir
from contextlib import ExitStack

F32 = mybir.dt.float32
BF16 = mybir.dt.bfloat16
I32 = mybir.dt.int32
I16 = mybir.dt.int16
U8 = mybir.dt.uint8
F16 = mybir.dt.float16
ALU = mybir.AluOpType
ACT = mybir.ActivationFunctionType
AX = mybir.AxisListType.X

PART = 128
NODES, D = 12500, 64
EDGES, DE = 400000, 32
HID = 128
TILES = EDGES // PART
BLOCKS = -(-NODES // PART)
NODES_PAD = BLOCKS * PART
LAST_ROWS = NODES - (BLOCKS - 1) * PART
SLOT = 4
SLOTS = 4
UNROLL = SLOT * SLOTS
ITERS = -(-(TILES + BLOCKS - 1) // UNROLL)
STEPS = ITERS * UNROLL
SLOT_E = SLOT * PART
MAPPED = -(-STEPS // PART) * PART
MAP_CHUNKS = MAPPED // PART
STEP_COLS = MAPPED + UNROLL
NAT_P = 125
NAT_T = TILES // NAT_P
NAT_E = NAT_T * PART
CH = 7
CHUNKS = BLOCKS // CH
CH_N = CH * PART
BIG = 1.5e38
EPS = 1e-5
GROUP = 4
GROUPS = (ITERS * SLOTS + SLOTS) * 4
GROUP_CHUNKS = -(-GROUPS // PART)
HOT = GROUP * BLOCKS
WIN_STEP = 32
WINDOW = 2 * PART
WINDOWS = -(-(EDGES // WIN_STEP + 1) // 16) * 16
EDGES_PAD = (WINDOWS - 1) * WIN_STEP + WINDOW
NOWHERE = 1 << 14
ADJ_BLOCKS = ITERS * SLOTS * 4 * GROUP // PART
HALF_B = BLOCKS // 2
MAP_COLS = 416
MAP_MMS = MAPPED // MAP_COLS


def gnn_kernel(nc, A, out):
    ctx = ExitStack()
    with ctx:
        def sb(name, shape, dt=F32, stack=ctx):
            return stack.enter_context(nc.sbuf_tensor(name, shape, dt))

        def dram(name, shape, dt=F32):
            return nc.dram_tensor(name, shape, dt).ap()

        ctx.enter_context(nc.allow_non_contiguous_dma(reason="a few single words for each partition"))
        sems = {}

        def S(name):
            if name not in sems:
                sems[name] = ctx.enter_context(nc.semaphore(name))
            return sems[name]

        tile_table = dram("tile_table", (TILES, 3 * PART))
        tile_ends = dram("tile_ends", (2, TILES))
        pad_dst = dram("pad_dst", (EDGES_PAD,), I32)
        pad_src = dram("pad_src", (EDGES_PAD,), I32)
        windows = dram("windows", (WINDOWS, 2 * WINDOW), I32)
        edges_to = dram("edges_to", (1 + NODES_PAD,), I32)
        adjacency = [dram(f"adjacency{k}", (ADJ_BLOCKS, PART, HALF_B * PART), BF16) for k in range(2)]
        step_rows = dram("step_rows", (2, MAPPED), I16)
        step_rel = dram("step_rel", (MAPPED, PART), I16)
        step_mask = dram("step_mask", (MAPPED, PART), BF16)
        scan_table = dram("scan_table", (ITERS * SLOTS, PART, SLOT * D))
        q_table = dram("q_table", (NODES_PAD, D))
        h1_table = dram("h1_table", (NODES_PAD, D))
        z_table = dram("z_table", (NODES_PAD, D))
        r_table = dram("r_table", (NODES_PAD, HID))
        h3_table = dram("h3_table", (NODES_PAD, D))
        blocked = "(g p) f -> p g f"

        xh = sb("xh", [PART, 2, BLOCKS, D])
        x_sb = xh[:, 0, :, :]
        h_sb = xh[:, 1, :, :]
        adj_out = xh[:, :, :, :].rearrange("p k g f -> p (k g f)").bitcast(BF16).rearrange("p (k h j) -> p k h j", k=2, j=PART)
        ACC_WORDS = (BLOCKS + 1) * (D + 1)
        P_WORDS = max((BLOCKS + 1) * 3 * D, BLOCKS * 3 * (D + 1)) // 2
        big = sb("big", [PART, ACC_WORDS + P_WORDS])
        src_st = sb("src_st", [PART, STEP_COLS], I16)
        rel_st = sb("rel_st", [PART, STEP_COLS], I16)
        block_row = sb("block_row", [1, STEP_COLS], I16)
        tile_row = sb("tile_row", [1, STEP_COLS], I16)
        last_row = sb("last_row", [PART, BLOCKS], I32)
        iota_hot = sb("iota_hot", [PART, HOT], F16)
        bad_row = sb("bad_row", [1, 4], I32)
        ident = sb("ident", [PART, PART])
        iota_f = sb("iota_f", [PART, PART])
        iota_p = sb("iota_p", [PART, 1])
        small = sb("small", [PART, 4, BLOCKS])
        deg_inv = sb("deg_inv", [PART, BLOCKS])
        has_edge = sb("has_edge", [PART, BLOCKS])
        eps_t = sb("eps_t", [PART, 1])
        idx = sb("idx", [PART, SLOTS, SLOT], I32)
        rows = sb("rows", [PART, SLOTS, SLOT, HID])
        w_pq = sb("w_pq", [D + 1, 2 * D])
        w_msg = sb("w_msg", [D + 1, D])
        w1_cat = sb("w1_cat", [2 * D, HID])
        w2_cat = sb("w2_cat", [HID, 2 * D])
        b1_col = sb("b1_col", [HID, 1])
        b2_row = sb("b2_row", [PART, D])
        w_r = sb("w_r", [D + 1, HID])
        w_e = sb("w_e", [DE, HID])
        w_agg = sb("w_agg", [HID, D])
        b_agg = sb("b_agg", [D + 1, D])
        w3_h = sb("w3_h", [D, HID])
        w3_a = sb("w3_a", [D, HID])
        b3_col = sb("b3_col", [HID, 1])
        w4 = sb("w4", [HID, D])
        b4_row = sb("b4_row", [PART, D])

        def acc(width):
            return big[:, 0:(BLOCKS + 1) * width].rearrange("p (g f) -> p g f", f=width)

        def split(width, n):
            words = n * 3 * width // 2
            return big[:, ACC_WORDS:ACC_WORDS + words].bitcast(BF16).rearrange("p (g k f) -> p g k f", k=3, f=width)

        p_split = split(D, BLOCKS + 1)
        squares = big[:, 0:BLOCKS * D].rearrange("p (g f) -> p g f", f=D)

        ones_col = rows[:, 0, 0, D:D + 1]
        ps = ctx.enter_context(nc.psum_tensor("ps", [PART, 8, 512], F32))

        def stage(make):
            with ExitStack() as st:
                return make(lambda name, shape, dt=F32: sb(name, shape, dt, st))

        ends_all = big[:, NAT_T * 3 * PART:NAT_T * 3 * PART + 2 * TILES]
        iota_v, begun = big[:, 0:MAPPED], big[:, MAPPED:2 * MAPPED]

        def map_bufs(a):
            return dict(raw=h_sb[:, :, :].rearrange("p g f -> p (g f)").bitcast(I32)[0:NAT_P, 0:NAT_E], cat=a("cat", [NAT_P, NAT_E + 1]),
                        st_idx=a("st_idx", [PART, 2, MAP_CHUNKS], I16), near=a("near", [PART, 1], I32), ones=a("ones", [PART, PART]),
                        diag=a("diag", [PART, PART]), ends=a("ends", [NAT_P, 2, NAT_T]), cols=a("cols", [PART, 8]), tri=a("tri", [PART, 2, PART]),
                        cur=a("cur", [PART, 2, 1], I32),
                        got=a("got", [PART, 2, 3, PART]), rel=a("rel", [PART, 2, PART]),
                        rel16=a("rel16", [PART, 2, PART], I16), mask16=a("mask16", [PART, 2, PART], BF16),
                        blk=a("blk", [PART, MAP_CHUNKS]))

        def adj_bufs(a):
            return dict(hot=a("hot_st", [PART, GROUP_CHUNKS * WINDOW], I16),
                        low=a("low_st", [PART, GROUP_CHUNKS * WINDOW], U8),
                        oh_hot=a("oh_hot", [PART, 4, 2, HOT], BF16), oh_low=a("oh_low", [PART, 4, 2, PART], BF16))

        def group_bufs(a):
            return dict(node0=a("node0", [PART, GROUP_CHUNKS]), node4=a("node4", [PART, GROUP_CHUNKS]),
                        bad=a("bad", [PART, GROUP_CHUNKS]), start=a("gstart", [PART, GROUP_CHUNKS], I32),
                        win_i=a("win_i", [PART, GROUP_CHUNKS], I32), cur=a("gcur", [PART, 2, 1], I32),
                        win=a("gwin", [PART, 2, 2, WINDOW], I32), zero=a("gzero", [1, 1], I32),
                        node=a("gnode", [PART, WINDOW]), ok=a("gok", [PART, WINDOW]),
                        sblk=a("gsblk", [PART, WINDOW], I32), slow=a("gslow", [PART, WINDOW], I32),
                        hot=a("ghot", [PART, 2, WINDOW]), low=a("glow", [PART, 2, WINDOW]), sum=a("gsum", [PART, 1]),
                        begins=big[:, 0:TILES].bitcast(I16)[:, 0:TILES],
                        near=big[:, TILES:TILES + 2 * CH_N].bitcast(I32).rearrange("p (b k e) -> p b k e", b=2, e=PART),
                        id=a("node_id", [PART, BLOCKS]), last=a("node_tile", [PART, BLOCKS]), in_tile=a("node_in_tile", [PART, BLOCKS]),
                        own=a("node_own", [PART, BLOCKS]), last_i=a("node_tile_i", [PART, BLOCKS], I32),
                        slot=a("node_slot", [PART, BLOCKS], I32), edges=a("node_edges", [PART, BLOCKS], I32),
                         node_cur=a("node_cur", [PART, 2, CH], I32))

        def ring_bufs(a):
            return dict(adj=a("ring", [PART, 4, HALF_B, PART], BF16))

        def l0_bufs(a):
            return dict(hc=a("hc0", [PART, CH, D]), hT=a("hT0", [D + 1, CH_N]), qst=a("qst", [PART, CH, D]),
                        pres=a("pres", [PART, CH, D]))

        def l0_loop_bufs(a):
            return dict(rel=a("rel_row", [PART, SLOTS, SLOT_E], I16), mask=a("mask_row", [D, SLOTS, SLOT_E], BF16),
                        ohT=a("ohT", [PART, 2, SLOT_E], BF16), pre=a("pre", [D + 1, 2, SLOT_E]),
                        scan=a("scan", [D, 2, SLOT_E]), scanT=a("scanT", [PART, 2, SLOT, D]))

        def sum_bufs(a):
            return dict(oh=a("oh_sum", [PART, SLOTS, SLOT, PART]))

        def l1_bufs(a):
            return dict(cat=a("cat1", [PART, CH, 2 * D]), catT=a("catT", [PART, CH_N]), h1T=a("h1T", [PART, CH_N]),
                        zst=a("zst", [PART, CH, D]), spare=a("zspare", [PART, CH, D]))

        def l2_pre_bufs(a):
            return dict(hc=a("hc2", [PART, CH, D]), hT=a("hT2", [D + 1, CH_N]), rst=a("rst", [PART, CH, HID]))

        def l2_loop_bufs(a):
            return dict(oh=a("oh2", [PART, SLOTS, SLOT, PART]), ea=a("ea", [DE, SLOTS, SLOT, PART]),
                        act=a("act2", [PART, 2, SLOT, HID]))

        def l2_post_bufs(a):
            return dict(m=a("m2", [PART, CH, HID]), hi=a("hi", [PART, CH, D + 1]), mT=a("mT", [PART, CH_N]),
                        hT=a("hTi", [D + 1, CH_N]), aT=a("aT", [D, CH_N]), gT=a("gT", [PART, CH_N]))

        with ExitStack() as l0_stack:
            ADJ = adj_bufs(lambda name, shape, dt=F32: sb(name, shape, dt, l0_stack))
            MP, GRP, L0, L0E = (stage(m) for m in (map_bufs, group_bufs, l0_bufs, l0_loop_bufs))
        SUM, L1, L2R, L2E, L2P, RING = (stage(m) for m in (sum_bufs, l1_bufs, l2_pre_bufs, l2_loop_bufs, l2_post_bufs, ring_bufs))

        def bad_groups(eng):
            eng.wait_ge(S("bad_known"), 1)
            _, (bad,) = nc.values_load_multi_w_load_instructions(bad_row[0:1, 0:1], engines=[eng.engine], min_val=0,
                                                                 max_val=GROUPS)
            return bad

        block = ctx.enter_context(nc.Block())
        NORMS = ("l0", "l1a", "l2", "l3")
        DENSE = {"l1a": 0, "l1b": 1, "l3": 2}

        def finish(sp):
            sp.wait_ge(S("result"), 1)
            sp.dma_start(out[0:(BLOCKS - 1) * PART, :].rearrange(blocked, p=PART), x_sb[:, 0:BLOCKS - 1, :]
                         ).then_inc(S("out_stored"), 16)
            sp.dma_start(out[(BLOCKS - 1) * PART:, :], x_sb[0:LAST_ROWS, BLOCKS - 1, :]).then_inc(S("out_stored"), 16)
            sp.wait_ge(S("out_stored"), 32)

        @block.sync
        def _(sp):
            sp.dma_start(x_sb[:, 0:BLOCKS - 1, :],
                         A["x"][0:(BLOCKS - 1) * PART, :].rearrange(blocked, p=PART)).then_inc(S("x_loaded"), 16)
            sp.wait_ge(S("x_zeroed"), 1)
            sp.dma_start(x_sb[0:LAST_ROWS, BLOCKS - 1, :], A["x"][(BLOCKS - 1) * PART:, :]).then_inc(S("x_loaded"), 16)

            sp.wait_ge(S("cat_ends"), 1)
            col = lambda e0, n: A["dst"][e0:e0 + (n - 1) * NAT_E + 1:NAT_E].rearrange("(p o) -> p o", o=1)
            sp.dma_start(MP["near"][1:NAT_P, :], col(NAT_E - 1, NAT_P - 1)).then_inc(S("edge_ends"), 16)
            for name, padded, fill in (("dst", pad_dst, 0), ("src", pad_src, 1)):
                sp.dma_start(padded[0:EDGES].rearrange("(p e) -> p e", p=PART),
                             A[name].rearrange("(p e) -> p e", p=PART)).then_inc(S("padded"), 16)
                sp.dma_start(padded[EDGES:].rearrange("(p e) -> p e", p=WIN_STEP),
                             MP["got"][0:WIN_STEP, fill, 0, 0:(EDGES_PAD - EDGES) // WIN_STEP].bitcast(I32)
                             ).then_inc(S("padded"), 16)
            for n, name in enumerate(("dst", "src")):
                view = A[name].rearrange("(p e) -> p e", p=NAT_P)
                if n:
                    sp.wait_ge(S("raw_used"), 1)
                sp.dma_start(MP["raw"], view).then_inc(S("raw_loaded"), 16)
            for name, dst_ap in (("L0_gnn_W2", w_msg[0:D, :]), ("L1_gnn_W1_l", w1_cat[0:D, :]),
                                 ("L1_gnn_W1_r", w1_cat[D:2 * D, :]), ("L1_gnn_W2_l", w2_cat[:, 0:D]),
                                 ("L1_gnn_W2_r", w2_cat[:, D:2 * D]), ("L2_gnn_W2", w_agg[:, :]), ("L2_gnn_W4", w4[:, :])):
                sp.dma_start(dst_ap, A[name]).then_inc(S("weights"), 16)
            row = lambda name: A[name].rearrange("(o f) -> o f", o=1)
            column = lambda name: A[name].rearrange("(f o) -> f o", o=1)
            W1 = A["L0_gnn_W1"]
            sp.dma_start(w_pq[0:D, 0:D], W1[0:D, :]).then_inc(S("weights"), 16)
            sp.dma_start(w_pq[0:D, D:2 * D], W1[D:2 * D, :]).then_inc(S("weights"), 16)
            sp.dma_start(w_msg[D:D + 1, :], row("L0_gnn_b2")).then_inc(S("weights"), 16)
            sp.dma_start(b1_col[:, :], column("L1_gnn_b1")).then_inc(S("weights"), 16)
            sp.dma_start(b3_col[:, :], column("L2_gnn_b3")).then_inc(S("weights"), 16)
            sp.dma_start(w_r[0:D, :], A["L2_gnn_W1"][0:D, :]).then_inc(S("weights"), 16)
            sp.dma_start(w_r[D:D + 1, :], row("L2_gnn_b1")).then_inc(S("weights"), 16)
            sp.dma_start(w_e[:, :], A["L2_gnn_W1"][D:D + DE, :]).then_inc(S("weights"), 16)
            sp.dma_start(w3_h[:, :], A["L2_gnn_W3"][0:D, :]).then_inc(S("weights"), 16)
            sp.dma_start(w3_a[:, :], A["L2_gnn_W3"][D:2 * D, :]).then_inc(S("weights"), 16)
            sp.dma_start(b2_row[:, :], row("L1_gnn_b2").to_broadcast([PART, D])).then_inc(S("weights"), 16)
            sp.dma_start(b4_row[:, :], row("L2_gnn_b4").to_broadcast([PART, D])).then_inc(S("weights"), 16)
            sp.wait_ge(S("w_zeroed"), 1)
            sp.dma_start(w_pq[D:D + 1, 0:D], row("L0_gnn_b1")).then_inc(S("weights"), 16)
            sp.dma_start(b_agg[D:D + 1, :], row("L2_gnn_b2")).then_inc(S("weights"), 16)

            sp.wait_ge(S("padded"), 64)
            for n, padded in enumerate((pad_dst, pad_src)):
                overlapping = bass.AP(tensor=padded.tensor, offset=0, ap=[[WIN_STEP, WINDOWS], [1, WINDOW]])
                sp.dma_start(windows[:, n * WINDOW:(n + 1) * WINDOW], overlapping).then_inc(S("windowed"), 16)
            sp.wait_ge(S("tiles_built"), 1)
            sp.dma_start(tile_ends.rearrange("k (p t) -> p k t", p=NAT_P), MP["ends"][:, :, :]).then_inc(S("ends_stored"), 16)
            sp.dma_start(tile_table.rearrange("(p t) f -> p (t f)", p=NAT_P),
                         big[0:NAT_P, 0:NAT_T * 3 * PART]).then_inc(S("table_stored"), 16)
            sp.wait_ge(S("ends_stored"), 16)
            sp.dma_start(ends_all.rearrange("p (k t) -> p k t", k=2),
                         tile_ends.unsqueeze(0).to_broadcast([PART, 2, TILES])).then_inc(S("ends_spread"), 16)
            sp.wait_ge(S("steps_mapped"), 1)
            sp.dma_start(step_rows[0:1, :], tile_row[:, 0:MAPPED]).then_inc(S("steps_stored"), 16)
            sp.dma_start(step_rows[1:2, :], block_row[:, 0:MAPPED]).then_inc(S("steps_stored"), 16)
            sp.wait_ge(S("steps_stored"), 32)
            sp.dma_start(MP["st_idx"][:, :, :],
                         step_rows.rearrange("k (c p) -> p k c", p=PART)).then_inc(S("steps_turned"), 16)
            with sp.Fori(0, MAP_CHUNKS // 2) as i:
                for b in range(2):
                    sp.wait_ge(S("map_rows"), 2 * i + b + 1)
                    sp.dma_start(step_rel[bass.ds(i * (2 * PART) + b * PART, PART), :], MP["rel16"][:, b, :]
                                 ).then_inc(S(f"map_stored{b}"), 16)
                    sp.dma_start(step_mask[bass.ds(i * (2 * PART) + b * PART, PART), :], MP["mask16"][:, b, :]
                                 ).then_inc(S(f"map_stored{b}"), 16)

            sp.wait_ge(S("edges_counted"), 1)
            sp.dma_start(edges_to[0:1].rearrange("(p o) -> p o", o=1), GRP["zero"][:, :]).then_inc(S("edges_stored"), 16)
            sp.dma_start(edges_to[1:].rearrange("(g p) -> p g", p=PART), GRP["edges"][:, :]).then_inc(S("edges_stored"), 16)
            sp.wait_ge(S("edges_stored"), 32)
            firsts = edges_to[0:NODES_PAD].rearrange("(g j) -> g j", j=GROUP)[:, 0:1]
            whole = NODES_PAD // GROUP // PART
            rest = NODES_PAD // GROUP - whole * PART
            sp.dma_start(GRP["start"][:, 0:whole], firsts[0:whole * PART, :].rearrange("(c p) o -> p (c o)", p=PART)
                         ).then_inc(S("group_starts"), 16)
            sp.dma_start(GRP["start"][0:rest, whole:whole + 1], firsts[whole * PART:, :]).then_inc(S("group_starts"), 16)

            with sp.Fori(0, CHUNKS) as c:
                sp.wait_ge(S("q_staged"), c + 1)
                sp.dma_start(q_table[bass.ds(c * CH_N, CH_N), :].rearrange(blocked, p=PART), L0["qst"][:, :, :]
                             ).then_inc(S("q_stored"), 16)
            for b in range(2):
                sp.wait_ge(S(f"map_stored{b}"), 16 * MAP_CHUNKS)
            def edge_rows(i, s, first):
                n = i * SLOTS + s
                if not first:
                    sp.wait_ge(S("l0_ohT"), n - SLOTS + 1)
                v0 = i * UNROLL + s * SLOT
                sp.dma_start(L0E["rel"][:, s, :], step_rel[bass.ds(v0, SLOT), :].rearrange("v e -> (v e)").unsqueeze(0)
                             .to_broadcast([PART, SLOT_E])).then_inc(S(f"l0_rel{s}"), 16)
                if not first:
                    sp.wait_ge(S("l0_scan"), n - SLOTS + 1)
                sp.dma_start(L0E["mask"][:, s, :], step_mask[bass.ds(v0, SLOT), :].rearrange("v e -> (v e)").unsqueeze(0)
                             .to_broadcast([D, SLOT_E])).then_inc(S(f"l0_mask{s}"), 16)
            sp.wait_ge(S("q_stored"), 16 * CHUNKS)
            sp.wait_ge(S("l0_piece"), 4 * CHUNKS)
            for s in range(SLOTS):
                edge_rows(0, s, True)
            def store_block(b):
                sp.wait_ge(S("l0_evac"), b * 16 + 16)
                for half in range(2):
                    sp.dma_start(adjacency[half][bass.ds(b, 1), :, :].rearrange("o p f -> (o p) f"),
                                 adj_out[:, bass.ds(b % 2, 1), half * HALF_B:(half + 1) * HALF_B, :].rearrange("p o h j -> p (o h j)")
                                 ).then_inc(S("adj_stored"), 16)

            def store_scan(m, b):
                sp.wait_ge(S("l0_turned"), m + 1)
                sp.dma_start(scan_table[bass.ds(m, 1), :, :].rearrange("o p f -> (o p) f"),
                             L0E["scanT"][:, b, :, :].rearrange("p k f -> p (k f)")).then_inc(S(f"scan_stored{b}"), 16)

            SCAN_LAG = 6
            def slots_ahead(b, slots):
                for s in range(slots):
                    edge_rows(b * 2 + 1 + s // SLOTS, s % SLOTS, False)
                    m = b * (2 * SLOTS) + (SLOTS + s - SCAN_LAG)
                    if not isinstance(m, int) or m >= 0:
                        store_scan(m, s % 2)
            slots_ahead(0, 2 * SLOTS)
            store_block(0)
            with sp.Fori(1, ADJ_BLOCKS - 1) as b:
                slots_ahead(b, 2 * SLOTS)
                store_block(b)
            slots_ahead(ADJ_BLOCKS - 1, SLOTS + 1)
            for m in range(ITERS * SLOTS + 1 - SCAN_LAG, ITERS * SLOTS):
                store_scan(m, m % 2)
            store_block(ADJ_BLOCKS - 1)
            sp.wait_ge(S("adj_stored"), 2 * 16 * ADJ_BLOCKS)
            sp.dma_start(x_sb[:, 0:BLOCKS - 1, :],
                         A["x"][0:(BLOCKS - 1) * PART, :].rearrange(blocked, p=PART)).then_inc(S("x_loaded"), 16)
            sp.wait_ge(S("x_zeroed"), 2)
            sp.dma_start(x_sb[0:LAST_ROWS, BLOCKS - 1, :], A["x"][(BLOCKS - 1) * PART:, :]).then_inc(S("x_loaded"), 16)

            def adjacency_blocks(layer):
                used = DENSE[layer] * 2 * BLOCKS

                def half(b, k, first):
                    if not first:
                        sp.wait_ge(S("adj_used"), b * 2 + (used + k - 3))
                    sp.dma_start(RING["adj"][:, k, :, :].rearrange("p h j -> p (h j)"),
                                 adjacency[k % 2][bass.ds(b + k // 2, 1), :, :].rearrange("o p f -> (o p) f")
                                 ).then_inc(S(f"adj_half{k}"), 16)
                for k in range(4):
                    half(0, k, True)
                with sp.Fori(1, HALF_B) as i:
                    for k in range(4):
                        half(i * 2, k, False)

            bad = bad_groups(sp)
            sp.wait_ge(S("sum_nodes"), 1)
            with sp.If(bad == 0):
                adjacency_blocks("l1a")
            with sp.Else():
                sp.dma_start(h1_table.rearrange(blocked, p=PART), h_sb[:, :, :]).then_inc(S("sum_table"), 16)
            with sp.Fori(0, CHUNKS) as c:
                sp.wait_ge(S("z_staged"), c + 1)
                sp.dma_start(z_table[bass.ds(c * CH_N, CH_N), :].rearrange(blocked, p=PART), L1["zst"][:, :, :]
                             ).then_inc(S("z_stored"), 16)
            sp.wait_ge(S("z_stored"), 16 * CHUNKS)
            sp.wait_ge(S("sum_nodes"), 2)
            with sp.If(bad == 0):
                adjacency_blocks("l1b")
            with sp.Fori(0, CHUNKS) as c:
                sp.wait_ge(S("r_staged"), c + 1)
                sp.dma_start(r_table[bass.ds(c * CH_N, CH_N), :].rearrange(blocked, p=PART), L2R["rst"][:, :, :]
                             ).then_inc(S("r_stored"), 16)
            def attributes(i, s, first):
                _, tiles = nc.values_load_multi_w_load_instructions(
                    tile_row[:, bass.ds(i * UNROLL + s * SLOT, SLOT)], engines=[sp.engine], min_val=0, max_val=TILES - 1)
                if not first:
                    sp.wait_ge(S("l2_pre"), (i - 1) * SLOTS + s + 1)
                for k in range(SLOT):
                    sp.dma_start(L2E["ea"][:, s, k, :], A["edge_attr_T"][bass.ds(tiles[k], 1), :, :]
                                 .rearrange("o f e -> (o f) e")).then_inc(S(f"l2_ea{s}"), 16)
            sp.wait_ge(S("r_stored"), 16 * CHUNKS)
            for s in range(SLOTS):
                attributes(0, s, True)
            with sp.Fori(1, ITERS) as i:
                for s in range(SLOTS):
                    attributes(i, s, False)
            sp.wait_ge(S("sum_nodes"), 3)
            with sp.If(bad == 0):
                adjacency_blocks("l3")
            with sp.Else():
                sp.dma_start(h3_table.rearrange(blocked, p=PART), h_sb[:, :, :]).then_inc(S("sum_table"), 16)
            finish(sp)

        @block.gpsimd
        def _(pool):
            nc.gpsimd.memset(x_sb[:, BLOCKS - 1, :], 0.0).then_inc(S("x_zeroed"), 1)
            nc.gpsimd.iota(iota_f[:, :], [[1, PART]], base=0, channel_multiplier=0,
                           allow_small_or_imprecise_dtypes=True).then_inc(S("iotas"), 1)
            nc.gpsimd.iota(iota_p[:, :], [[0, 1]], base=0, channel_multiplier=1,
                           allow_small_or_imprecise_dtypes=True).then_inc(S("iotas"), 1)
            nc.gpsimd.iota(iota_hot[:, :], [[1, HOT]], base=1, channel_multiplier=0,
                           allow_small_or_imprecise_dtypes=True).then_inc(S("iotas"), 1)
            pool.wait_ge(S("table_stored"), 16)
            with pool.Fori(0, MAP_CHUNKS // 2) as i:
                for b in range(2):
                    pool.wait_ge(S("map_idx"), 2 * i + b + 1)
                    pool.sem_inc(S("pool_begun"), 1)
                    nc.gpsimd.indirect_dma_start(
                        out=MP["got"][:, b, :, :].rearrange("p k e -> p (k e)"), out_offset=None, in_=tile_table,
                        in_offset=bass.IndirectOffsetOnAxis(MP["cur"][:, b, :], 0)).then_inc(S(f"map_got{b}"), 16)

            def gathers(layer, table, width, turn=0):
                ready = turn * (ITERS + 1) * SLOTS
                with pool.Fori(0, ITERS) as i:
                    for s in range(SLOTS):
                        pool.wait_ge(S(f"{layer}_idx"), i * SLOTS + (ready + s + 1))
                        pool.sem_inc(S("pool_begun"), 1)
                        for k in range(SLOT):
                            nc.gpsimd.indirect_dma_start(
                                out=rows[:, s, k, 0:width], out_offset=None, in_=table,
                                in_offset=bass.IndirectOffsetOnAxis(idx[:, s, k:k + 1], 0)).then_inc(S(f"{layer}_rows{s}"), 16)

            with pool.Fori(0, CHUNKS // 2) as i:
                for b in range(2):
                    pool.wait_ge(S("node_idx"), i * 2 + b + 1)
                    pool.sem_inc(S("pool_begun"), 1)
                    for k in range(CH):
                        nc.gpsimd.indirect_dma_start(out=GRP["near"][:, b, k, :], out_offset=None,
                                                     in_=A["dst"].rearrange("(t e) -> t e", e=PART),
                                                     in_offset=bass.IndirectOffsetOnAxis(GRP["node_cur"][:, b, k:k + 1], 0)
                                                     ).then_inc(S(f"node_got{b}"), 16)
            pool.wait_ge(S("windowed"), 32)
            with pool.Fori(0, GROUP_CHUNKS // 2) as i:
                for b in range(2):
                    pool.wait_ge(S("gwin_idx"), i * 2 + b + 1)
                    pool.sem_inc(S("pool_begun"), 1)
                    nc.gpsimd.indirect_dma_start(out=GRP["win"][:, b, :, :].rearrange("p k e -> p (k e)"), out_offset=None, in_=windows,
                                                 in_offset=bass.IndirectOffsetOnAxis(GRP["cur"][:, b, :], 0)
                                                 ).then_inc(S(f"gwin_got{b}"), 16)

            pool.wait_ge(S("q_stored"), 16 * CHUNKS)
            gathers("l0", q_table, D)
            for b in range(2):
                pool.wait_ge(S(f"scan_stored{b}"), 16 * ITERS * SLOTS // 2)
            pool.sem_inc(S("pool_begun"), 1)
            for g in range(BLOCKS):
                nc.gpsimd.indirect_dma_start(out=acc(D)[:, g, :], out_offset=None,
                                             in_=scan_table.rearrange("n p (k f) -> (n p k) f", f=D),
                                             in_offset=bass.IndirectOffsetOnAxis(last_row[:, g:g + 1], 0)).then_inc(S("l0_max"), 16)
            bad = bad_groups(pool)
            with pool.If(bad > 0):
                pool.wait_ge(S("sum_table"), 16)
                gathers("sum", h1_table, D, DENSE["l1a"])
                pool.wait_ge(S("z_stored"), 16 * CHUNKS)
                gathers("sum", z_table, D, DENSE["l1b"])
            pool.wait_ge(S("r_stored"), 16 * CHUNKS)
            gathers("l2", r_table, HID)
            with pool.If(bad > 0):
                pool.wait_ge(S("sum_table"), 32)
                gathers("sum", h3_table, D, DENSE["l3"])

        @block.scalar
        def _(act):
            def indices(layer, i, s):
                nc.scalar.copy(idx[:, s, :], src_st[:, bass.ds(i * UNROLL + s * SLOT, SLOT)]).then_inc(S(f"{layer}_idx"), 1)

            def standard_deviation(layer):
                act.wait_ge(S("variance"), NORMS.index(layer) + 1)
                nc.scalar.activation(small[:, 2, :], small[:, 1, :], ACT.Sqrt, bias=eps_t[:, :],
                                     scale=1.0 / D).then_inc(S("deviation"), 1)

            act.wait_ge(S("w_zeroed"), 1)
            with act.Fori(0, MAP_CHUNKS // 2) as i:
                for b in range(2):
                    c = i * 2 + b
                    act.wait_ge(S("map_turned"), c + 1)
                    cols = bass.ds(i * (2 * PART) + b * PART, PART)
                    nc.scalar.copy(src_st[:, cols], ps[:, b, 0:PART])
                    nc.scalar.copy(rel_st[:, cols], ps[:, b, PART:2 * PART]).then_inc(S("map_done"), 1)

            with act.Fori(0, GROUP_CHUNKS // 2) as i:
                for b in range(2):
                    act.wait_ge(S("gturned"), i * 2 + b + 1)
                    cols = bass.ds(i * (2 * WINDOW) + b * WINDOW, WINDOW)
                    for n, store in enumerate((ADJ["hot"], ADJ["low"])):
                        ins = nc.scalar.copy(store[:, cols].rearrange("p (g h) -> p h g", h=2),
                                             ps[:, b, n * WINDOW:(n + 1) * WINDOW].rearrange("p (h g) -> p h g", h=2))
                    ins.then_inc(S("group_done"), 1)

            standard_deviation("l0")
            with act.Fori(0, CHUNKS) as c:
                act.wait_ge(S("l0_hT"), c + 1)
                nc.scalar.copy(L0["hT"][0:D, :], ps[0:D, 0:2, :].rearrange("p b f -> p (b f)")[:, 0:CH_N]).then_inc(S("l0_hT_out"), 1)
                act.wait_ge(S("l0_pq"), c + 1)
                nc.scalar.copy(L0["qst"][:, :, :], ps[:, 2:4, :].rearrange("p b (g f) -> p (b g) f", f=2 * D)[:, 0:CH, D:2 * D]
                               ).then_inc(S("q_staged"), 1)
                act.wait_ge(S("q_stored"), c * 16 + 16)

            def evac0(n, b, s, pair):
                act.wait_ge(S("l0_built"), n * 2 + pair + 1)
                at = s * (4 * GROUP) + pair * (2 * GROUP)
                nc.scalar.copy(adj_out[:, bass.ds(b % 2, 1), :, at:at + 2 * GROUP].rearrange("p o h (g j) -> p g (o h) j", g=2),
                               ps[:, 4 + 2 * pair:6 + 2 * pair, 0:HOT].rearrange("p g (h j) -> p g h j", j=GROUP)
                               ).then_inc(S("l0_evac"), 1)

            def relu0(n, s, i):
                act.wait_ge(S("l0_pre"), n + 1)
                if not isinstance(n, int) or n >= 2:
                    act.wait_ge(S("l0_msg"), n - 1)
                nc.scalar.activation(L0E["pre"][0:D, s % 2, :], ps[0:D, 3 * (s % 2), :], ACT.Relu).then_inc(S("l0_relu"), 1)
                indices("l0", i + 1, s)

            def turned0(b, s):
                m = b * (2 * SLOTS) + (s - 2)
                act.wait_ge(S("l0_turn"), m + 1)
                if not isinstance(m, int) or m >= 2:
                    act.wait_ge(S(f"scan_stored{s % 2}"), b * (16 * SLOTS) + 16 * (s // 2 - 1))
                nc.scalar.copy(L0E["scanT"][:, s % 2, :, :], ps[:, 2, 0:SLOT * D].rearrange("p (k f) -> p k f", f=D)
                               ).then_inc(S("l0_turned"), 1)

            def slot0(b, s):
                n = b * (2 * SLOTS) + s
                evac0(n, b, s, 0)
                relu0(n, s % SLOTS, b * 2 + s // SLOTS)
                evac0(n, b, s, 1)
                if not isinstance(n, int) or n >= 2:
                    turned0(b, s)

            for s in range(SLOTS):
                indices("l0", 0, s)
            for b in range(2):
                for s in range(2 * SLOTS):
                    slot0(b, s)
            with act.Fori(2, ADJ_BLOCKS) as b:
                act.wait_ge(S("adj_stored"), b * 32 - 32)
                for s in range(2 * SLOTS):
                    slot0(b, s)
            for s in range(2):
                turned0(ADJ_BLOCKS, s)

            def sums(layer):
                used = DENSE[layer] * ITERS * SLOTS
                for s in range(SLOTS):
                    indices("sum", 0, s)
                with act.Fori(0, ITERS) as i:
                    for s in range(SLOTS):
                        act.wait_ge(S("sum_sum"), i * SLOTS + (used + s + 1))
                        indices("sum", i + 1, s)

            bad = bad_groups(act)
            standard_deviation("l1a")
            with act.If(bad > 0):
                sums("l1a")
            with act.Fori(0, CHUNKS) as c:
                act.wait_ge(S("l1_cat"), c + 1)
                nc.scalar.copy(L1["catT"][:, :], ps[:, 0:2, :].rearrange("p b f -> p (b f)")[:, 0:CH_N]).then_inc(S("l1_catT"), 1)
                act.wait_ge(S("l1_hid"), c + 1)
                for b in range(2):
                    ins = nc.scalar.activation(L1["h1T"][:, b * CH_N // 2:(b + 1) * CH_N // 2], ps[:, 2 + b, 0:CH_N // 2],
                                               ACT.Relu, bias=b1_col[:, :])
                ins.then_inc(S("l1_h1T"), 1)
                act.wait_ge(S("l1_zy"), c + 1)
                nc.scalar.copy(L1["zst"][:, :, :], ps[:, 4:6, :].rearrange("p b (g f) -> p (b g) f", f=2 * D)[:, 0:CH, 0:D]
                               ).then_inc(S("z_staged"), 1)
                act.wait_ge(S("z_stored"), c * 16 + 16)
            with act.If(bad > 0):
                sums("l1b")

            standard_deviation("l2")
            with act.Fori(0, CHUNKS) as c:
                act.wait_ge(S("l2_hT"), c + 1)
                nc.scalar.copy(L2R["hT"][0:D, :], ps[0:D, 0:2, :].rearrange("p b f -> p (b f)")[:, 0:CH_N]).then_inc(S("l2_hT_out"), 1)
                act.wait_ge(S("l2_r"), c + 1)
                nc.scalar.copy(L2R["rst"][:, :, :], ps[:, 2:4, :].rearrange("p b (g f) -> p (b g) f", f=HID)[:, 0:CH, :]
                               ).then_inc(S("r_staged"), 1)
                act.wait_ge(S("r_stored"), c * 16 + 16)

            def relu2(n, s, i):
                act.wait_ge(S("l2_pre"), n + 1)
                if not isinstance(n, int) or n >= 2:
                    act.wait_ge(S("l2_sum"), n - 1)
                nc.scalar.activation(L2E["act"][:, s % 2, :, :].rearrange("p k f -> p (k f)"), ps[:, s % 2, :], ACT.Relu
                                     ).then_inc(S("l2_relu"), 1)
                indices("l2", i + 1, s)

            for s in range(SLOTS):
                indices("l2", 0, s)
            for s in range(SLOTS):
                relu2(s, s, 0)
            with act.Fori(1, ITERS) as i:
                for s in range(SLOTS):
                    relu2(i * SLOTS + s, s, i)
            with act.Fori(0, CHUNKS) as c:
                act.wait_ge(S("l2_mT"), c + 1)
                nc.scalar.copy(L2P["mT"][:, :], ps[:, 0:2, :].rearrange("p b f -> p (b f)")[:, 0:CH_N])
                nc.scalar.copy(L2P["hT"][:, :], ps[0:D + 1, 2:4, :].rearrange("p b f -> p (b f)")[:, 0:CH_N]).then_inc(S("l2_mT_out"), 1)
                act.wait_ge(S("l2_agg"), c + 1)
                nc.scalar.copy(L2P["aT"][:, :].rearrange("p (b f) -> p b f", b=2), ps[0:D, 4:6, 0:CH_N // 2]).then_inc(S("l2_aT"), 1)
                act.wait_ge(S("l2_g"), c + 1)
                nc.scalar.activation(L2P["gT"][:, :].rearrange("p (b f) -> p b f", b=2), ps[:, 6:8, 0:CH_N // 2], ACT.Relu,
                                     bias=b3_col[:, :]).then_inc(S("l2_gT"), 1)
            standard_deviation("l3")
            with act.If(bad > 0):
                sums("l3")

        @block.vector
        def _(dve):
            chain = [0]

            def link(ins):
                chain[0] += 1
                ins.then_inc(S("dve_chain"), 1)
                dve.wait_ge(S("dve_chain"), chain[0])

            def broadcast(ap, shape):
                return ap.unsqueeze(len(shape) - 1).to_broadcast(shape)

            vec = nc.vector
            vec.memset(src_st[:, MAPPED:], 0)
            vec.memset(rel_st[:, MAPPED:], -1.0)
            vec.memset(eps_t[:, :], EPS)
            vec.memset(w_pq[D:D + 1, D:2 * D], 0.0)
            vec.memset(rows[:, :, :, D:D + 1], 1.0)
            vec.memset(b_agg[:, :], 0.0)
            vec.memset(block_row[:, MAPPED:], 0).then_inc(S("w_zeroed"), 1)
            dve.wait_ge(S("iotas"), 3)
            vec.tensor_scalar(ident[:, :], iota_f[:, :], iota_p[:, :], None, ALU.is_equal)
            vec.tensor_scalar(MP["tri"][:, 0, :], iota_f[:, :], iota_p[:, :], None, ALU.is_gt)
            link(vec.tensor_scalar(MP["tri"][:, 1, :], iota_f[:, :], 1.0, iota_p[:, :], ALU.subtract, ALU.is_equal))
            vec.tensor_tensor(MP["tri"][:, 1, :], ident[:, :], MP["tri"][:, 1, :], ALU.subtract).then_inc(S("consts"), 1)
            vec.tensor_scalar(MP["cols"][:, 0:1], iota_p[:, :], float(PART), None, ALU.mult)
            vec.tensor_scalar(MP["cols"][:, 1:2], iota_p[:, :], 1.0, float(PART), ALU.add, ALU.mult)
            vec.memset(MP["got"][:, 0, 0, :].bitcast(I32), NOWHERE)
            vec.memset(MP["got"][:, 1, 0, :].bitcast(I32), 0)
            vec.memset(MP["near"][:, :], -1).then_inc(S("cat_ends"), 1)
            table = big[0:NAT_P, 0:NAT_T * 3 * PART].rearrange("p (t k e) -> p t k e", k=3, e=PART)
            tiled = lambda ap: ap.rearrange("p (t e) -> p t e", e=PART)
            cat = MP["cat"]
            dve.wait_ge(S("edge_ends"), 16)
            vec.tensor_copy(cat[:, 0:1], MP["near"][0:NAT_P, :])
            dve.wait_ge(S("raw_loaded"), 16)
            link(vec.tensor_copy(cat[:, 1:NAT_E + 1], MP["raw"]))
            dve.sem_inc(S("raw_used"), 1)
            here = cat[:, 1:NAT_E + 1]
            vec.tensor_copy(table[:, :, 1, :], tiled(here))
            vec.tensor_copy(MP["ends"][:, 0, :], tiled(here)[:, :, 0])
            vec.tensor_copy(MP["ends"][:, 1, :], tiled(here)[:, :, PART - 1])
            link(vec.tensor_tensor(table[:, :, 2, :], tiled(cat[:, 0:NAT_E]), tiled(here), ALU.not_equal))
            vec.tensor_scalar(table[:, :, 2, :], table[:, :, 2, :], -2.0 * BIG, BIG, ALU.mult, ALU.add)
            dve.wait_ge(S("raw_loaded"), 32)
            vec.tensor_copy(table[:, :, 0, :], tiled(MP["raw"])).then_inc(S("tiles_built"), 1)
            dve.wait_ge(S("ends_spread"), 16)
            junk = h_sb[:, :, :].rearrange("p g f -> p (g f)")
            link(vec.tensor_scalar(junk[:, 0:TILES], ends_all[:, 0:TILES], MP["cols"][:, 1:2], 0.0, ALU.is_lt, ALU.add,
                                   accum_out=MP["cols"][:, 2:3]))
            link(vec.tensor_scalar(junk[:, TILES:2 * TILES], ends_all[:, TILES:], MP["cols"][:, 0:1], 0.0, ALU.is_lt, ALU.add,
                                   accum_out=MP["cols"][:, 3:4]))
            link(vec.tensor_tensor(MP["cols"][:, 4:5], MP["cols"][:, 2:3], MP["cols"][:, 3:4], ALU.subtract))
            vec.tensor_scalar(MP["cols"][:, 4:5], MP["cols"][:, 4:5], 0.0, None, ALU.max).then_inc(S("block_steps"), 1)
            dve.wait_ge(S("block_begin"), 1)
            link(vec.tensor_copy(MP["cols"][:, 5:6], ps[:, 0, 0:1]))
            vec.tensor_tensor(MP["cols"][:, 6:7], MP["cols"][:, 3:4], MP["cols"][:, 5:6], ALU.subtract).then_inc(S("block_shift"), 1)
            dve.wait_ge(S("block_delta"), 1)
            link(vec.tensor_copy(MP["cols"][:, 7:8], ps[:, 0, 1:2]))
            vec.memset(MP["ones"][:, :], 1.0)
            vec.tensor_scalar(MP["diag"][:, :], ident[:, :], MP["cols"][:, 6:7], None, ALU.mult).then_inc(S("shift_diag"), 1)
            dve.wait_ge(S("shift_row"), 1)
            vec.tensor_copy(small[:, 0, :], ps[:, 4, 0:BLOCKS])
            dve.wait_ge(S("table_stored"), 16)
            link(vec.tensor_scalar(iota_v[:, 0:PART], iota_f[:, :], 0.0, None, ALU.add))
            for c in range(1, MAP_CHUNKS):
                ins = vec.tensor_scalar(iota_v[:, c * PART:(c + 1) * PART], iota_f[:, :], float(c * PART), None, ALU.add)
            link(ins)
            vec.tensor_scalar(begun, iota_v, MP["cols"][:, 5:6], None, ALU.is_ge).then_inc(S("block_begun"), 1)
            for m in range(MAP_MMS):
                cols = slice(m * MAP_COLS, (m + 1) * MAP_COLS)
                dve.wait_ge(S("steps_summed"), m + 1)
                link(vec.tensor_tensor(junk[0:1, 0:MAP_COLS], ps[0:1, 2 * (m % 2), 0:MAP_COLS], iota_v[0:1, cols], ALU.add))
                vec.tensor_scalar(tile_row[:, cols], junk[0:1, 0:MAP_COLS], float(TILES - 1), None, ALU.min)
                link(vec.tensor_scalar(block_row[:, cols], ps[0:1, 2 * (m % 2) + 1, 0:MAP_COLS], 1.0, float(BLOCKS),
                                       ALU.subtract, ALU.min))
                dve.sem_inc(S("steps_read"), 1)
            dve.sem_inc(S("steps_mapped"), 1)
            dve.wait_ge(S("steps_turned"), 16)
            link(vec.tensor_scalar(MP["blk"][:, :], MP["st_idx"][:, 1, :], float(PART), None, ALU.mult))
            for b in range(2):
                vec.tensor_copy(MP["cur"][:, b, :], MP["st_idx"][:, 0, b:b + 1]).then_inc(S("map_idx"), 1)

            def map_chunk(i, b, first, last):
                got, rel = MP["got"][:, b, :, :], MP["rel"][:, b, :]
                dve.wait_ge(S(f"map_got{b}"), i * 16 + 16)
                if not first:
                    dve.wait_ge(S(f"map_stored{b}"), i * 32)
                vec.tensor_scalar(rel, got[:, 1, :], MP["blk"][:, bass.ds(i * 2 + b, 1)], None, ALU.subtract).then_inc(S("map_rel"), 1)
                vec.tensor_copy(MP["mask16"][:, b, :], got[:, 2, :])
                dve.wait_ge(S("map_rel"), i * 2 + b + 1)
                vec.tensor_copy(MP["rel16"][:, b, :], rel).then_inc(S("map_rows"), 1)
                dve.wait_ge(S("map_turned"), i * 2 + b + 1)
                if not last:
                    vec.tensor_copy(MP["cur"][:, b, :], MP["st_idx"][:, 0, bass.ds(i * 2 + b + 2, 1)]).then_inc(S("map_idx"), 1)
            for b in range(2):
                map_chunk(0, b, True, False)
            with dve.Fori(1, MAP_CHUNKS // 2 - 1) as i:
                for b in range(2):
                    map_chunk(i, b, False, False)
            for b in range(2):
                map_chunk(MAP_CHUNKS // 2 - 1, b, False, True)

            for b in range(2):
                dve.wait_ge(S(f"map_stored{b}"), 16 * MAP_CHUNKS)
            for c in range(GROUP_CHUNKS):
                ins = vec.tensor_scalar(GRP["node0"][:, c:c + 1], iota_p[:, :], float(GROUP), float(c * PART * GROUP), ALU.mult, ALU.add)
            link(ins)
            vec.memset(GRP["start"][:, :], EDGES)
            vec.memset(GRP["zero"][:, :], 0)
            link(vec.tensor_scalar(GRP["node4"][:, :], GRP["node0"][:, :], float(GROUP), None, ALU.add))
            for g in range(BLOCKS):
                ins = vec.tensor_scalar(GRP["id"][:, g:g + 1], iota_p[:, :], float(g * PART), None, ALU.add)
            link(ins)
            link(vec.tensor_copy(GRP["begins"], ends_all[:, 0:TILES]))
            counted = junk.bitcast(I16)[:, 0:TILES]
            with dve.Fori(0, BLOCKS) as g:
                vec.tensor_scalar(counted, GRP["begins"], GRP["id"][:, bass.ds(g, 1)], 0.0, ALU.is_le, ALU.add,
                                  accum_out=GRP["last"][:, bass.ds(g, 1)]).then_inc(S("node_tile"), 1)
                dve.wait_ge(S("node_tile"), g + 1)
            link(vec.tensor_scalar(GRP["last"][:, :], GRP["last"][:, :], 1.0, 0.0, ALU.subtract, ALU.max))
            link(vec.tensor_copy(GRP["last_i"][:, :], GRP["last"][:, :]))
            def node_index(col, b):
                vec.tensor_copy(GRP["node_cur"][:, b, :], GRP["last_i"][:, col]).then_inc(S("node_idx"), 1)

            def node_chunk(i, b, last):
                c = i * 2 + b
                dve.wait_ge(S(f"node_got{b}"), i * (16 * CH) + 16 * CH)
                for k in range(CH):
                    for n, (test, count) in enumerate(((ALU.is_le, GRP["in_tile"]), (ALU.is_equal, GRP["own"]))):
                        col = bass.ds(c * CH + k, 1)
                        ins = vec.tensor_scalar(junk[:, (2 * k + n) * PART:(2 * k + n + 1) * PART], GRP["near"][:, b, k, :],
                                                GRP["id"][:, col], 0.0, test, ALU.add, accum_out=count[:, col])
                ins.then_inc(S("node_counted"), 1)
                dve.wait_ge(S("node_counted"), c + 1)
                if not last:
                    node_index(bass.ds((c + 2) * CH, CH), b)
            for b in range(2):
                node_index(slice(b * CH, (b + 1) * CH), b)
            with dve.Fori(0, CHUNKS // 2 - 1) as i:
                for b in range(2):
                    node_chunk(i, b, False)
            for b in range(2):
                node_chunk(CHUNKS // 2 - 1, b, True)
            link(vec.scalar_tensor_tensor(GRP["edges"][:, :], GRP["last"][:, :], float(PART), GRP["in_tile"][:, :], ALU.mult, ALU.add))
            dve.sem_inc(S("edges_counted"), 1)
            last = GRP["last"][:, :]
            link(vec.tensor_tensor(last, last, small[:, 0, :], ALU.subtract))
            link(vec.tensor_scalar(last, last, 0.0, float(STEPS - 1), ALU.max, ALU.min))
            link(vec.tensor_copy(GRP["last_i"][:, :], last))
            link(vec.tensor_scalar(GRP["slot"][:, :], GRP["last_i"][:, :], SLOT.bit_length() - 1, None, ALU.logical_shift_right))
            link(vec.scalar_tensor_tensor(last, GRP["slot"][:, :], float(SLOT * PART - SLOT), last, ALU.mult, ALU.add))
            link(vec.tensor_scalar(GRP["in_tile"][:, :], GRP["in_tile"][:, :], 1.0, 0.0, ALU.subtract, ALU.max))
            link(vec.scalar_tensor_tensor(last, GRP["in_tile"][:, :], float(SLOT), last, ALU.mult, ALU.add))
            vec.tensor_copy(last_row[:, :], last)
            link(vec.tensor_scalar(has_edge[:, :], GRP["own"][:, :], 1.0, None, ALU.min))

            def next_window(col, b):
                vec.tensor_copy(GRP["cur"][:, b, :], GRP["win_i"][:, col]).then_inc(S("gwin_idx"), 1)

            dve.wait_ge(S("group_starts"), 32)
            link(vec.tensor_scalar(GRP["win_i"][:, :], GRP["start"][:, :], WIN_STEP.bit_length() - 1, None, ALU.logical_shift_right))

            def window_chunk(i, b, last):
                c = i * 2 + b
                dve.wait_ge(S(f"gwin_got{b}"), i * 16 + 16)
                dst, src = GRP["win"][:, b, 0, :], GRP["win"][:, b, 1, :]
                col = bass.ds(c, 1)
                steps = [
                    lambda: vec.tensor_scalar(GRP["node"][:, :], dst, GRP["node0"][:, col], None, ALU.subtract),
                    lambda: vec.tensor_scalar(GRP["ok"][:, :], GRP["node"][:, :], 0.0, None, ALU.is_ge),
                    lambda: vec.scalar_tensor_tensor(GRP["ok"][:, :], GRP["node"][:, :], float(GROUP), GRP["ok"][:, :], ALU.is_lt, ALU.mult),
                    lambda: vec.tensor_scalar(GRP["sblk"][:, :], src, PART.bit_length() - 1, None, ALU.logical_shift_right),
                    lambda: vec.tensor_scalar(GRP["slow"][:, :], src, PART - 1, None, ALU.bitwise_and),
                    lambda: vec.scalar_tensor_tensor(GRP["node"][:, :], GRP["sblk"][:, :], float(GROUP), GRP["node"][:, :], ALU.mult, ALU.add),
                    lambda: vec.scalar_tensor_tensor(GRP["hot"][:, b, :], GRP["node"][:, :], 1.0, GRP["ok"][:, :], ALU.add, ALU.mult),
                    lambda: vec.tensor_scalar(GRP["bad"][:, col], dst[:, WINDOW - 1:WINDOW], GRP["node4"][:, col], None, ALU.is_lt),
                    lambda: vec.tensor_scalar(GRP["low"][:, b, :], GRP["slow"][:, :], 1.0, None, ALU.add)]
                for k, step in enumerate(steps):
                    step().then_inc(S("group_step"), 1)
                    dve.wait_ge(S("group_step"), c * len(steps) + k + 1)
                dve.sem_inc(S("group_rows"), 1)
                dve.wait_ge(S("gturned"), c + 1)
                if not last:
                    next_window(bass.ds(c + 2, 1), b)

            for b in range(2):
                next_window(slice(b, b + 1), b)
            with dve.Fori(0, GROUP_CHUNKS // 2 - 1) as i:
                for b in range(2):
                    window_chunk(i, b, False)
            for b in range(2):
                window_chunk(GROUP_CHUNKS // 2 - 1, b, True)
            vec.tensor_reduce(GRP["sum"][:, :], GRP["bad"][:, :], AX, ALU.add).then_inc(S("bad_sum"), 1)
            dve.wait_ge(S("bad_total"), 1)
            link(vec.tensor_copy(bad_row[0:1, 0:1], ps[0:1, 0, 0:1]))
            dve.sem_inc(S("bad_known"), 1)

            def centred(layer):
                link(vec.tensor_reduce(small[:, 0, :], x_sb[:, :, :], AX, ALU.add))
                link(vec.tensor_scalar(small[:, 0, :], small[:, 0, :], 1.0 / D, None, ALU.mult))
                link(vec.tensor_tensor(h_sb[:, :, :], x_sb[:, :, :], broadcast(small[:, 0, :], [PART, BLOCKS, D]), ALU.subtract))
                link(vec.tensor_tensor(squares, h_sb[:, :, :], h_sb[:, :, :], ALU.mult))
                vec.tensor_reduce(small[:, 1, :], squares, AX, ALU.add).then_inc(S("variance"), 1)
                dve.wait_ge(S("deviation"), NORMS.index(layer) + 1)
                link(vec.reciprocal(small[:, 3, :], small[:, 2, :]))

            def normed(out_ap, g0, n):
                return vec.scalar_tensor_tensor(out_ap, h_sb[:, bass.ds(g0, n), :], 0.0,
                                                broadcast(small[:, 3, bass.ds(g0, n)], [PART, n, D]), ALU.max, ALU.mult)

            def clear(layer, width, turn=0):
                vec.memset(big[:, 0:(BLOCKS + 1) * width], 0.0).then_inc(S(f"{layer}_cleared"), 1)
                dve.wait_ge(S(f"{layer}_cleared"), turn + 1)

            def blocks_of(i, s):
                _, got = nc.values_load_multi_w_load_instructions(
                    block_row[:, bass.ds(i * UNROLL + s * SLOT, SLOT)], engines=[dve.engine], min_val=0, max_val=BLOCKS)
                return got

            def one_hot(out_ap, source, i, s):
                for k in range(SLOT):
                    ins = vec.tensor_scalar(out_ap[:, k, :], iota_f[:, :], source[:, bass.ds(i * UNROLL + s * SLOT + k, 1)],
                                            None, ALU.is_equal)
                return ins

            def add_up(layer, width, i, s, bank, m):
                got = blocks_of(i, s)
                for k in range(SLOT):
                    target = acc(width)[:, bass.ds(got[k], 1), :].rearrange("p o f -> p (o f)")
                    vec.tensor_tensor(target, target, bank[:, k * width:(k + 1) * width], ALU.add).then_inc(S(f"{layer}_added"), 1)
                    dve.wait_ge(S(f"{layer}_added"), m * SLOT + k + 1)

            dve.wait_ge(S("x_loaded"), 32)
            dve.wait_ge(S("weights"), 16 * 21)
            link(vec.tensor_tensor(w_pq[0:D, 0:D], w_pq[0:D, 0:D], w_pq[0:D, D:2 * D], ALU.subtract))
            dve.wait_ge(S("group_done"), GROUP_CHUNKS)
            vec.memset(L0["hT"][D:D + 1, :], 1.0)
            centred("l0")
            vec.memset(p_split[:, BLOCKS, :, :], 0.0)
            with dve.Fori(0, CHUNKS) as c:
                normed(L0["hc"][:, :, :], c * CH, CH).then_inc(S("l0_h"), 1)
                dve.wait_ge(S("q_staged"), c + 1)
                p = ps[:, 2:4, :].rearrange("p b (g f) -> p (b g) f", f=2 * D)[:, 0:CH, 0:D]
                pieces = [p_split[:, bass.ds(c * CH, CH), k, :] for k in range(3)]
                steps = [lambda: vec.tensor_copy(pieces[0], p),
                         lambda: vec.tensor_tensor(L0["pres"][:, :, :], p, pieces[0], ALU.subtract),
                         lambda: vec.tensor_copy(pieces[1], L0["pres"][:, :, :]),
                         lambda: vec.tensor_tensor(pieces[2], L0["pres"][:, :, :], pieces[1], ALU.subtract)]
                for k, step in enumerate(steps):
                    step().then_inc(S("l0_piece"), 1)
                    dve.wait_ge(S("l0_piece"), c * len(steps) + k + 1)
            dve.wait_ge(S("q_stored"), 16 * CHUNKS)
            vec.memset(L0E["pre"][D:D + 1, :, :], 1.0)
            link(vec.memset(L0E["scan"][:, :, :], -BIG))

            def ohT0(n, s, i):
                dve.wait_ge(S(f"l0_rel{s}"), i * 16 + 16)
                if not isinstance(n, int) or n >= 2:
                    dve.wait_ge(S("l0_pre"), n - 1)
                vec.tensor_scalar(L0E["ohT"][:, s % 2, :], L0E["rel"][:, s, :], iota_p[:, :], None, ALU.is_equal).then_inc(S("l0_ohT"), 1)

            def scan0(m, s, i):
                dve.wait_ge(S("l0_msg"), m + 1)
                dve.wait_ge(S(f"l0_mask{s}"), i * 16 + 16)
                if not isinstance(m, int) or m >= 2:
                    dve.wait_ge(S("l0_turn"), m - 1)
                if not isinstance(m, int) or m >= 1:
                    dve.wait_ge(S("l0_scan"), m)
                vec.tensor_tensor_scan(L0E["scan"][:, s % 2, :], L0E["mask"][:, s, :], ps[0:D, 1, :],
                                       L0E["scan"][:, (s + 1) % 2, SLOT_E - 1:SLOT_E], ALU.min, ALU.max).then_inc(S("l0_scan"), 1)

            def hot0(i, s, pair):
                n1 = i * SLOTS + s + 1
                if not isinstance(n1, int) or n1 >= 1:
                    dve.wait_ge(S("l0_built"), n1 * 2 - 1 + pair)
                for g in (2 * pair, 2 * pair + 1):
                    for h in range(2):
                        col = bass.ds((i * SLOTS + s + 1) * 8 + 2 * g + h, 1)
                        vec.tensor_scalar(ADJ["oh_low"][:, g, h, :], iota_hot[:, 0:PART], ADJ["low"][:, col], None, ALU.is_equal)
                        ins = vec.tensor_scalar(ADJ["oh_hot"][:, g, h, :], iota_hot[:, :], ADJ["hot"][:, col], None, ALU.is_equal)
                ins.then_inc(S("l0_hot"), 1)

            def staged(work, i, s, lag):
                m = i * SLOTS + (s - lag)
                if not isinstance(m, int) or 0 <= m < ITERS * SLOTS:
                    work(m, (s - lag) % SLOTS, i + (s - lag) // SLOTS)

            def slot0(i, s):
                staged(scan0, i, s, 1)
                hot0(i, s, 0)
                staged(ohT0, i, s, -1)
                hot0(i, s, 1)

            ohT0(0, 0, 0)
            hot0(0, -1, 0)
            hot0(0, -1, 1)
            for s in range(SLOTS):
                slot0(0, s)
            with dve.Fori(1, ITERS) as i:
                for s in range(SLOTS):
                    slot0(i, s)
            staged(scan0, ITERS, 0, 1)
            dve.wait_ge(S("adj_stored"), 2 * 16 * ADJ_BLOCKS)
            vec.memset(x_sb[:, BLOCKS - 1, :], 0.0).then_inc(S("x_zeroed"), 1)
            dve.wait_ge(S("x_loaded"), 64)
            dve.wait_ge(S("l0_mask0"), 16 * (ITERS + 1))
            dve.wait_ge(S("l0_max"), 16 * BLOCKS)
            maxima = acc(D)[:, 0:BLOCKS, :]
            link(vec.tensor_tensor(maxima, maxima, broadcast(has_edge[:, :], [PART, BLOCKS, D]), ALU.mult))
            link(vec.tensor_tensor(x_sb[:, :, :], x_sb[:, :, :], maxima, ALU.add))

            def sums(layer, width):
                done = DENSE[layer] * ITERS * SLOTS
                clear("sum", width, DENSE[layer])
                for s in range(SLOTS):
                    one_hot(SUM["oh"][:, s, :, :], rel_st, 0, s).then_inc(S("sum_oh"), 1)
                with dve.Fori(0, ITERS) as i:
                    for s in range(SLOTS):
                        dve.wait_ge(S("sum_sum"), i * SLOTS + (done + s + 1))
                        add_up("sum", width, i, s, ps[:, s, :], i * SLOTS + (done + s))
                        one_hot(SUM["oh"][:, s, :, :], rel_st, i + 1, s).then_inc(S("sum_oh"), 1)

            def pieces_of(width, g, value, spare, count):
                t = split(width, BLOCKS)
                piece = [t[:, g, k, 0:D] for k in range(3)]
                for k, step in enumerate((
                        lambda: vec.tensor_copy(piece[0], value),
                        lambda: vec.tensor_tensor(spare, value, piece[0], ALU.subtract),
                        lambda: vec.tensor_copy(piece[1], spare),
                        lambda: vec.tensor_tensor(piece[2], spare, piece[1], ALU.subtract))):
                    step().then_inc(S("piece"), 1)
                    dve.wait_ge(S("piece"), count * 4 + k + 1)

            def block_sums(layer, width):
                with dve.Fori(0, HALF_B) as i:
                    for b in range(2):
                        dve.wait_ge(S("adj_used"), i * 4 + (DENSE[layer] * 2 * BLOCKS + 2 * b + 2))
                        vec.tensor_reduce(acc(width)[:, bass.ds(i * 2 + b, 1), :].rearrange("p o f -> p (o f)"),
                                          ps[:, b, 0:3 * width].rearrange("p (k f) -> p f k", k=3), AX, ALU.add
                                          ).then_inc(S("adj_summed"), 1)
                dve.wait_ge(S("adj_summed"), (DENSE[layer] + 1) * BLOCKS)

            bad = bad_groups(dve)
            centred("l1a")
            link(normed(h_sb[:, :, :], 0, BLOCKS))
            ones = split(D + 1, BLOCKS)
            vec.memset(ones[:, :, 0, D:D + 1], 1.0)
            vec.memset(ones[:, :, 1:3, D:D + 1], 0.0)
            pieces_of(D + 1, slice(0, BLOCKS), h_sb[:, :, :], squares, 0)
            dve.sem_inc(S("sum_nodes"), 1)
            with dve.If(bad == 0):
                block_sums("l1a", D + 1)
            with dve.Else():
                sums("l1a", D + 1)
            sums1 = acc(D + 1)
            degrees = sums1[:, 0:BLOCKS, D:D + 1].rearrange("p g o -> p (g o)")
            link(vec.tensor_scalar(deg_inv[:, :], degrees, 1.0, None, ALU.max))
            link(vec.reciprocal(deg_inv[:, :], deg_inv[:, :]))
            with dve.Fori(0, CHUNKS) as c:
                vec.tensor_tensor(L1["cat"][:, :, 0:D], sums1[:, bass.ds(c * CH, CH), 0:D],
                                  broadcast(deg_inv[:, bass.ds(c * CH, CH)], [PART, CH, D]), ALU.mult)
                vec.tensor_copy(L1["cat"][:, :, D:2 * D], h_sb[:, bass.ds(c * CH, CH), :]).then_inc(S("l1_nodes"), 1)
                dve.wait_ge(S("z_staged"), c + 1)
                zy = ps[:, 4:6, :].rearrange("p b (g f) -> p (b g) f", f=2 * D)
                pieces_of(D, bass.ds(c * CH, CH), zy[:, 0:CH, 0:D], L1["spare"][:, :, :], c + 1)
                vec.tensor_tensor(h_sb[:, bass.ds(c * CH, CH), :],
                                  ps[:, 4:6, :].rearrange("p b (g f) -> p (b g) f", f=2 * D)[:, 0:CH, D:2 * D],
                                  b2_row[:, :].unsqueeze(1).to_broadcast([PART, CH, D]), ALU.add).then_inc(S("l1_y"), 1)
                dve.wait_ge(S("l1_y"), c + 1)
            dve.wait_ge(S("z_stored"), 16 * CHUNKS)
            dve.sem_inc(S("sum_nodes"), 1)
            with dve.If(bad == 0):
                block_sums("l1b", D)
            with dve.Else():
                sums("l1b", D)
            link(vec.tensor_tensor(h_sb[:, :, :], h_sb[:, :, :], x_sb[:, :, :], ALU.add))
            link(vec.tensor_tensor(x_sb[:, :, :], acc(D)[:, 0:BLOCKS, :], broadcast(deg_inv[:, :], [PART, BLOCKS, D]), ALU.mult))
            link(vec.tensor_tensor(x_sb[:, :, :], x_sb[:, :, :], h_sb[:, :, :], ALU.add))

            centred("l2")
            link(normed(h_sb[:, :, :], 0, BLOCKS))
            vec.memset(L2R["hT"][D:D + 1, :], 1.0)
            with dve.Fori(0, CHUNKS) as c:
                vec.tensor_copy(L2R["hc"][:, :, :], h_sb[:, bass.ds(c * CH, CH), :]).then_inc(S("l2_h"), 1)
                dve.wait_ge(S("l2_hT"), c + 1)
            clear("l2", HID)
            dve.wait_ge(S("r_staged"), CHUNKS)
            dve.wait_ge(S("r_stored"), 16 * CHUNKS)
            for s in range(SLOTS):
                one_hot(L2E["oh"][:, s, :, :], rel_st, 0, s).then_inc(S("l2_oh"), 1)
            with dve.Fori(0, ITERS) as i:
                for s in range(SLOTS):
                    dve.wait_ge(S("l2_sum"), i * SLOTS + s + 1)
                    add_up("l2", HID, i, s, ps[:, 2 + s % 2, :], i * SLOTS + s)
                    one_hot(L2E["oh"][:, s, :, :], rel_st, i + 1, s).then_inc(S("l2_oh"), 1)
            with dve.Fori(0, CHUNKS) as c:
                g = bass.ds(c * CH, CH)
                vec.tensor_tensor(L2P["m"][:, :, :], acc(HID)[:, g, :], broadcast(deg_inv[:, g], [PART, CH, HID]), ALU.mult)
                vec.tensor_copy(L2P["hi"][:, :, 0:D], h_sb[:, g, :])
                vec.tensor_copy(L2P["hi"][:, :, D:D + 1], has_edge[:, g].unsqueeze(2)).then_inc(S("l2_nodes"), 1)
                dve.wait_ge(S("l2_out"), c + 1)
                y = ps[:, 0, 0:CH * D].rearrange("p (g f) -> p g f", f=D)
                vec.tensor_tensor(x_sb[:, g, :], x_sb[:, g, :], y, ALU.add).then_inc(S("l2_x"), 1)
                dve.wait_ge(S("l2_x"), c + 1)
            link(vec.tensor_tensor(x_sb[:, :, :], x_sb[:, :, :], b4_row[:, :].unsqueeze(1).to_broadcast([PART, BLOCKS, D]), ALU.add))

            centred("l3")
            link(normed(h_sb[:, :, :], 0, BLOCKS))
            pieces_of(D, slice(0, BLOCKS), h_sb[:, :, :], squares, 1 + CHUNKS)
            dve.sem_inc(S("sum_nodes"), 1)
            with dve.If(bad == 0):
                block_sums("l3", D)
            with dve.Else():
                sums("l3", D)
            link(vec.tensor_tensor(x_sb[:, :, :], x_sb[:, :, :], acc(D)[:, 0:BLOCKS, :], ALU.add))
            dve.sem_inc(S("result"), 1)

        @block.tensor
        def _(pe):
            mm = nc.tensor.matmul
            pe.wait_ge(S("w_zeroed"), 1)
            pe.wait_ge(S("consts"), 1)
            pe.wait_ge(S("block_steps"), 1)
            mm(ps[:, 0, 0:1], MP["tri"][:, 0, :], MP["cols"][:, 4:5], start=True, stop=True).then_inc(S("block_begin"), 1)
            pe.wait_ge(S("block_shift"), 1)
            mm(ps[:, 0, 1:2], MP["tri"][:, 1, :], MP["cols"][:, 6:7], start=True, stop=True).then_inc(S("block_delta"), 1)
            pe.wait_ge(S("shift_diag"), 1)
            mm(ps[:, 4, 0:BLOCKS], MP["ones"][:, :], MP["diag"][:, 0:BLOCKS], start=True, stop=True).then_inc(S("shift_row"), 1)
            pe.wait_ge(S("block_begun"), 1)
            for m in range(MAP_MMS):
                cols = slice(m * MAP_COLS, (m + 1) * MAP_COLS)
                if m >= 2:
                    pe.wait_ge(S("steps_read"), m - 1)
                mm(ps[0:1, 2 * (m % 2), 0:MAP_COLS], MP["cols"][:, 7:8], begun[:, cols], start=True, stop=True)
                mm(ps[0:1, 2 * (m % 2) + 1, 0:MAP_COLS], ones_col, begun[:, cols], start=True, stop=True).then_inc(S("steps_summed"), 1)
            pe.wait_ge(S("steps_read"), MAP_MMS)

            def map_chunk(i, b, first):
                pe.wait_ge(S("map_rows"), i * 2 + b + 1)
                if not first:
                    pe.wait_ge(S("map_done"), i * 2 + b - 1)
                for k, edges in enumerate((MP["got"][:, b, 0, :], MP["rel"][:, b, :])):
                    ins = nc.tensor.transpose(ps[:, b, k * PART:(k + 1) * PART], edges, ident[:, :])
                ins.then_inc(S("map_turned"), 1)
            for b in range(2):
                map_chunk(0, b, True)
            with pe.Fori(1, MAP_CHUNKS // 2) as i:
                for b in range(2):
                    map_chunk(i, b, False)
            pe.wait_ge(S("map_done"), MAP_CHUNKS)

            def group_chunk(i, b, first):
                pe.wait_ge(S("group_rows"), i * 2 + b + 1)
                if not first:
                    pe.wait_ge(S("group_done"), i * 2 + b - 1)
                for k, edges in enumerate((GRP["hot"][:, b, :], GRP["low"][:, b, :])):
                    for h in range(2):
                        ins = nc.tensor.transpose(ps[:, b, (2 * k + h) * PART:(2 * k + h + 1) * PART],
                                                  edges[:, h * PART:(h + 1) * PART], ident[:, :])
                ins.then_inc(S("gturned"), 1)
            for b in range(2):
                group_chunk(0, b, True)
            with pe.Fori(1, GROUP_CHUNKS // 2) as i:
                for b in range(2):
                    group_chunk(i, b, False)
            pe.wait_ge(S("group_done"), GROUP_CHUNKS)
            pe.wait_ge(S("bad_sum"), 1)
            mm(ps[0:1, 0, 0:1], GRP["sum"][:, :], ones_col, start=True, stop=True).then_inc(S("bad_total"), 1)
            pe.wait_ge(S("bad_known"), 1)

            turned = lambda rows_, b0, k: ps[0:rows_, b0 + k // 4, (k % 4) * PART:(k % 4 + 1) * PART]

            with pe.Fori(0, CHUNKS) as c:
                pe.wait_ge(S("l0_h"), c + 1)
                pe.sem_inc(S("pe_begun"), 1)
                for k in range(CH):
                    ins = nc.tensor.transpose(turned(D, 0, k), L0["hc"][:, k, :], ident[:, :])
                ins.then_inc(S("l0_hT"), 1)
                pe.wait_ge(S("l0_hT_out"), c + 1)
                for k in range(CH):
                    ins = mm(turned(PART, 2, k), L0["hT"][:, k * PART:(k + 1) * PART], w_pq[:, :], start=True, stop=True)
                ins.then_inc(S("l0_pq"), 1)
            pe.wait_ge(S("l0_piece"), 4 * CHUNKS)
            pe.wait_ge(S("q_staged"), CHUNKS)

            def pre0(n, s, i):
                _, got = nc.values_load_multi_w_load_instructions(
                    block_row[:, bass.ds(i * UNROLL + s * SLOT, SLOT)], engines=[pe.engine], min_val=0, max_val=BLOCKS)
                pe.wait_ge(S(f"l0_rows{s}"), i * (16 * SLOT) + 16 * SLOT)
                pe.wait_ge(S("l0_ohT"), n + 1)
                if not isinstance(n, int) or n >= 2:
                    pe.wait_ge(S("l0_relu"), n - 1)
                pe.sem_inc(S("pe_begun"), 1)
                for k in range(SLOT):
                    target = ps[0:D, 3 * (s % 2), k * PART:(k + 1) * PART]
                    mm(target, rows[:, s, k, 0:D], ident[:, :], start=True, stop=False, is_transpose=True)
                    for piece in range(3):
                        ins = mm(target, p_split[:, bass.ds(got[k], 1), piece, :].rearrange("p o f -> p (o f)"),
                                 L0E["ohT"][:, s % 2, k * PART:(k + 1) * PART], start=False, stop=piece == 2)
                ins.then_inc(S("l0_pre"), 1)

            def msg0(m, s, i):
                pe.wait_ge(S("l0_relu"), m + 1)
                if not isinstance(m, int) or m >= 1:
                    pe.wait_ge(S("l0_scan"), m)
                mm(ps[0:D, 1, :], w_msg[:, :], L0E["pre"][:, s % 2, :], start=True, stop=True).then_inc(S("l0_msg"), 1)

            def turn0(m, s, i):
                pe.wait_ge(S("l0_scan"), m + 1)
                if not isinstance(m, int) or m >= 1:
                    pe.wait_ge(S("l0_turned"), m)
                pe.sem_inc(S("pe_begun"), 1)
                for k in range(SLOT):
                    ins = nc.tensor.transpose(ps[:, 2, k * D:(k + 1) * D],
                                              L0E["scan"][:, s % 2, k * PART:(k + 1) * PART], ident[0:D, 0:D])
                ins.then_inc(S("l0_turn"), 1)

            def build0(i, s, pair):
                n = i * SLOTS + s
                pe.wait_ge(S("l0_hot"), n * 2 + pair + 1)
                if not isinstance(n, int) or n >= 1:
                    pe.wait_ge(S("l0_evac"), n * 2 - 1 + pair)
                for g in (2 * pair, 2 * pair + 1):
                    for h in range(2):
                        ins = mm(ps[:, 4 + g, 0:HOT], ADJ["oh_low"][:, g, h, :], ADJ["oh_hot"][:, g, h, :],
                                 start=h == 0, stop=h == 1)
                ins.then_inc(S("l0_built"), 1)

            def staged(work, i, s, lag):
                m = i * SLOTS + (s - lag)
                if not isinstance(m, int) or 0 <= m < ITERS * SLOTS:
                    work(m, (s - lag) % SLOTS, i + (s - lag) // SLOTS)

            def slot0(i, s):
                build0(i, s, 0)
                staged(msg0, i, s, 1)
                pre0(i * SLOTS + s, s, i)
                build0(i, s, 1)
                staged(turn0, i, s, 2)

            for s in range(SLOTS):
                slot0(0, s)
            with pe.Fori(1, ITERS) as i:
                for s in range(SLOTS):
                    slot0(i, s)
            staged(msg0, ITERS, 0, 1)
            for s in range(2):
                staged(turn0, ITERS, s, 2)

            def sums(layer, width):
                turn = DENSE[layer]
                with pe.Fori(0, ITERS) as i:
                    for s in range(SLOTS):
                        pe.wait_ge(S(f"sum_rows{s}"), i * (16 * SLOT) + 16 * SLOT * (turn * ITERS + 1))
                        pe.wait_ge(S("sum_oh"), i * SLOTS + (turn * (ITERS + 1) * SLOTS + s + 1))
                        for k in range(SLOT):
                            ins = mm(ps[:, s, k * width:(k + 1) * width], SUM["oh"][:, s, k, :], rows[:, s, k, 0:width],
                                     start=True, stop=True)
                        ins.then_inc(S("sum_sum"), 1)

            def block_sums(layer, width):
                t = split(width, BLOCKS)

                def half(i, k, first):
                    pe.wait_ge(S(f"adj_half{k}"), i * 16 + (DENSE[layer] * HALF_B * 16 + 16))
                    if k % 2 == 0 and not first:
                        pe.wait_ge(S("adj_summed"), i * 2 + (DENSE[layer] * BLOCKS + k // 2 - 1))
                    for h in range(HALF_B):
                        source = (k % 2) * HALF_B + h
                        ins = mm(ps[:, k // 2, 0:3 * width], RING["adj"][:, k, h, :],
                                 t[:, source, :, :].rearrange("p k f -> p (k f)"),
                                 start=source == 0, stop=source == BLOCKS - 1)
                    ins.then_inc(S("adj_used"), 1)
                for k in range(4):
                    half(0, k, True)
                with pe.Fori(1, HALF_B) as i:
                    for k in range(4):
                        half(i, k, False)

            bad = bad_groups(pe)
            pe.wait_ge(S("sum_nodes"), 1)
            with pe.If(bad == 0):
                block_sums("l1a", D + 1)
            with pe.Else():
                sums("l1a", D + 1)
                pe.wait_ge(S("sum_added"), STEPS)
            with pe.Fori(0, CHUNKS) as c:
                pe.wait_ge(S("l1_nodes"), c + 1)
                for k in range(CH):
                    ins = nc.tensor.transpose(turned(PART, 0, k), L1["cat"][:, k, :], ident[:, :])
                ins.then_inc(S("l1_cat"), 1)
                pe.wait_ge(S("l1_catT"), c + 1)
                for b in range(2):
                    ins = mm(ps[:, 2 + b, 0:CH_N // 2], w1_cat[:, :], L1["catT"][:, b * CH_N // 2:(b + 1) * CH_N // 2],
                             start=True, stop=True)
                ins.then_inc(S("l1_hid"), 1)
                pe.wait_ge(S("l1_h1T"), c + 1)
                for k in range(CH):
                    ins = mm(turned(PART, 4, k), L1["h1T"][:, k * PART:(k + 1) * PART], w2_cat[:, :], start=True, stop=True)
                ins.then_inc(S("l1_zy"), 1)
            pe.wait_ge(S("z_staged"), CHUNKS)
            pe.wait_ge(S("sum_nodes"), 2)
            with pe.If(bad == 0):
                block_sums("l1b", D)
            with pe.Else():
                sums("l1b", D)
                pe.wait_ge(S("sum_added"), 2 * STEPS)

            with pe.Fori(0, CHUNKS) as c:
                pe.wait_ge(S("l2_h"), c + 1)
                pe.sem_inc(S("pe_begun"), 1)
                for k in range(CH):
                    ins = nc.tensor.transpose(turned(D, 0, k), L2R["hc"][:, k, :], ident[:, :])
                ins.then_inc(S("l2_hT"), 1)
                pe.wait_ge(S("l2_hT_out"), c + 1)
                for k in range(CH):
                    ins = mm(turned(PART, 2, k), L2R["hT"][:, k * PART:(k + 1) * PART], w_r[:, :], start=True, stop=True)
                ins.then_inc(S("l2_r"), 1)
            pe.wait_ge(S("r_staged"), CHUNKS)

            def pre2(n, s, i):
                pe.wait_ge(S(f"l2_ea{s}"), i * (16 * SLOT) + 16 * SLOT)
                pe.wait_ge(S(f"l2_rows{s}"), i * (16 * SLOT) + 16 * SLOT)
                if not isinstance(n, int) or n >= 2:
                    pe.wait_ge(S("l2_relu"), n - 1)
                for k in range(SLOT):
                    ins = mm(ps[:, s % 2, k * HID:(k + 1) * HID], L2E["ea"][:, s, k, :], w_e[:, :], start=True, stop=False)
                    ins = mm(ps[:, s % 2, k * HID:(k + 1) * HID], ident[:, :], rows[:, s, k, :], start=False, stop=True)
                ins.then_inc(S("l2_pre"), 1)

            def sum2(m, s, i):
                pe.wait_ge(S("l2_relu"), m + 1)
                pe.wait_ge(S("l2_oh"), m + 1)
                if not isinstance(m, int) or m >= 2:
                    pe.wait_ge(S("l2_added"), (m - 1) * SLOT)
                for k in range(SLOT):
                    ins = mm(ps[:, 2 + s % 2, k * HID:(k + 1) * HID], L2E["oh"][:, s, k, :], L2E["act"][:, s % 2, k, :],
                             start=True, stop=True)
                ins.then_inc(S("l2_sum"), 1)

            def slot2(i, s):
                for lag, work in ((0, pre2), (1, sum2)):
                    sl, it = (s - lag) % SLOTS, i + (-1 if s < lag else 0)
                    m = i * SLOTS + (s - lag)
                    if isinstance(m, int) and not 0 <= m < ITERS * SLOTS:
                        continue
                    work(m, sl, it)
            for s in range(SLOTS):
                slot2(0, s)
            with pe.Fori(1, ITERS) as i:
                for s in range(SLOTS):
                    slot2(i, s)
            slot2(ITERS, 0)
            pe.wait_ge(S("l2_added"), STEPS)
            with pe.Fori(0, CHUNKS) as c:
                pe.wait_ge(S("l2_nodes"), c + 1)
                for k in range(CH):
                    nc.tensor.transpose(turned(PART, 0, k), L2P["m"][:, k, :], ident[:, :])
                for k in range(CH):
                    ins = nc.tensor.transpose(turned(D + 1, 2, k), L2P["hi"][:, k, :], ident[:, :])
                ins.then_inc(S("l2_mT"), 1)
                pe.wait_ge(S("l2_mT_out"), c + 1)
                for b in range(2):
                    half = slice(b * CH_N // 2, (b + 1) * CH_N // 2)
                    mm(ps[0:D, 4 + b, 0:CH_N // 2], w_agg[:, :], L2P["mT"][:, half], start=True, stop=False)
                    ins = mm(ps[0:D, 4 + b, 0:CH_N // 2], b_agg[:, :], L2P["hT"][:, half], start=False, stop=True)
                ins.then_inc(S("l2_agg"), 1)
                pe.wait_ge(S("l2_aT"), c + 1)
                for b in range(2):
                    half = slice(b * CH_N // 2, (b + 1) * CH_N // 2)
                    mm(ps[:, 6 + b, 0:CH_N // 2], w3_h[:, :], L2P["hT"][0:D, half], start=True, stop=False)
                    ins = mm(ps[:, 6 + b, 0:CH_N // 2], w3_a[:, :], L2P["aT"][:, half], start=False, stop=True)
                ins.then_inc(S("l2_g"), 1)
                pe.wait_ge(S("l2_gT"), c + 1)
                for k in range(CH):
                    ins = mm(ps[:, 0, k * D:(k + 1) * D], L2P["gT"][:, k * PART:(k + 1) * PART], w4[:, :], start=True, stop=True)
                ins.then_inc(S("l2_out"), 1)
            pe.wait_ge(S("sum_nodes"), 3)
            with pe.If(bad == 0):
                block_sums("l3", D)
            with pe.Else():
                sums("l3", D)


_INS = ["x", "src", "dst", "L0_gnn_W1", "L0_gnn_b1", "L0_gnn_W2", "L0_gnn_b2", "L1_gnn_W1_l", "L1_gnn_b1", "L1_gnn_W1_r",
        "L1_gnn_W2_l", "L1_gnn_b2", "L1_gnn_W2_r", "L2_gnn_W1", "L2_gnn_b1", "L2_gnn_W2", "L2_gnn_b2", "L2_gnn_W3", "L2_gnn_b3",
        "L2_gnn_W4", "L2_gnn_b4"]


def kernel(**inputs):
    import concourse.bacc as bacc
    from concourse.bass_utils import run_bass_kernel_spmd

    nc = bacc.Bacc("TRN2", target_bir_lowering=False, num_devices=1)
    arrays = {name: np.ascontiguousarray(inputs[name]) for name in _INS}
    arrays["edge_attr_T"] = np.ascontiguousarray(
        np.asarray(inputs["edge_attr_32"]).reshape(TILES, PART, DE).transpose(0, 2, 1))
    aps = {name: nc.dram_tensor(name, a.shape, mybir.dt.from_np(a.dtype), kind="ExternalInput").ap()
           for name, a in arrays.items()}
    out = nc.dram_tensor("out", (NODES, D), F32, kind="ExternalOutput").ap()
    gnn_kernel(nc, aps, out)
    result = run_bass_kernel_spmd(nc, [arrays], core_ids=[0])
    return result.results[0]["out"]
```
